# Optimizing a Trainium2 kernel written in Bass

```python
import numpy as np
import jax
import jax.numpy as jnp

def _softmax(x, axis=-1):
    return jax.nn.softmax(x, axis=axis)

def _gelu(x):
    return jax.nn.gelu(x, approximate=True)

def _silu(x):
    return jax.nn.silu(x)

def _sigmoid(x):
    return jax.nn.sigmoid(x)

def _layernorm(x, axis=-1, eps=1e-05):
    m = jnp.mean(x, axis=axis, keepdims=True)
    v = jnp.var(x, axis=axis, keepdims=True)
    return (x - m) / jnp.sqrt(v + eps)

def _scatter_add(tgt, idx, src, axis=0):
    return tgt.at[idx].add(src)

def _segment_sum(src, seg, n):
    return jax.ops.segment_sum(src, seg, n)
kernel_name = 'mk_decoder_preln_d4_seqx_r8_ff2524'

def setup_inputs(seed: int=0):
    np.random.seed(seed)
    _w = jnp.asarray

    def _rec_inputs():
        import jax
        import jax.numpy as jnp
        _rk = jax.random.key(seed)
        x = -0.0002928 + 1 * jax.random.normal(jax.random.fold_in(_rk, 1), (32, 128, 128), jnp.float32)
        _lenS = 128 - jax.random.randint(jax.random.fold_in(_rk, 7), (32,), 0, max(1, 128 // 4) + 1, jnp.int32)
        _lenS2 = 128 - jax.random.randint(jax.random.fold_in(_rk, 8), (32,), 0, max(1, 128 // 4) + 1, jnp.int32)
        _ctx_1024P = jax.random.normal(jax.random.fold_in(_rk, 11), (32, 16, 128), jnp.float32)
        _ctx_1024c = jax.random.dirichlet(jax.random.fold_in(_rk, 511), 0.3 * jnp.ones((16,), jnp.float32), (32, 128))
        _ctx_1024t = jnp.einsum('bsk,bkd->bsd', _ctx_1024c, _ctx_1024P)
        _ctx_1024t = _ctx_1024t * jax.lax.rsqrt(jnp.mean(jnp.square(_ctx_1024t)) + 1e-12) * 0.953939
        ctx_1024 = -1.39393e-06 + 0.999914 * (_ctx_1024t + 0.3 * jax.random.normal(jax.random.fold_in(_rk, 611), (32, 128, 128), jnp.float32))
        _validS = jnp.arange(128)[None, :] < _lenS[:, None]
        _validS2 = jnp.arange(128)[None, :] < _lenS2[:, None]
        _causal = jnp.tril(jnp.ones((128, 128), dtype=bool))
        mask_BxSxS2_if1 = jnp.where(jnp.ones((32, 128, 128), dtype=bool), 1, 0).astype(jnp.int32)
        mask_BxS2_bk0 = jnp.logical_not(jnp.broadcast_to(_validS2[:, :], (32, 128)))
        return (x, ctx_1024, mask_BxSxS2_if1, mask_BxS2_bk0)
    x, ctx_1024, mask_BxSxS2_if1, mask_BxS2_bk0 = _rec_inputs()

    def _L0_attn_setup():
        import jax, jax.numpy as jnp
        import numpy as np
        CHUNK = 32
        FLOOR = 0.01
        EPS_MIX = 1e-05
        EPS_NORM = 1e-05

        def l2norm(x):
            return x / jnp.sqrt(jnp.sum(x * x, -1, keepdims=True) + 1e-12)

        def dw_causal_conv(x, w):
            K = w.shape[-1]
            L = x.shape[1]
            xp = jnp.pad(x, ((0, 0), (K - 1, 0), (0, 0)))
            y = jnp.zeros_like(x)
            for t in range(K):
                y = y + xp[:, t:t + L, :] * w[:, t]
            return y

        def delta_rule_chunkwise(q, k, v, beta):
            b, h, L, dk = q.shape
            dv = v.shape[-1]
            c = CHUNK
            n = L // c
            q = l2norm(q)
            k = l2norm(k)
            v = v * beta[..., None]
            kb = k * beta[..., None]
            rs = lambda x: x.reshape(b, h, n, c, -1)
            qc, kc, vc, kbc = (rs(q), rs(k), rs(v), rs(kb))
            T = -jnp.einsum('bhnid,bhnjd->bhnij', kbc, kc)
            tri_strict = jnp.tril(jnp.ones((c, c), bool), -1)
            T = jnp.where(tri_strict, T, 0.0)
            for i in range(1, c):
                T = T.at[..., i, :i].add(jnp.einsum('bhnj,bhnji->bhni', T[..., i, :], T[..., :, :i]))
            T = T + jnp.eye(c, dtype=T.dtype)
            u = jnp.einsum('bhnij,bhnjd->bhnid', T, vc)
            w = jnp.einsum('bhnij,bhnjd->bhnid', T, kbc)
            mask_incl = jnp.tril(jnp.ones((c, c), bool), 0)

            def step(S, inp):
                qi, ki, ui, wi = inp
                attn = jnp.einsum('bhid,bhjd->bhij', qi, ki)
                attn = jnp.where(mask_incl, attn, 0.0)
                u_i = ui - jnp.einsum('bhik,bhkd->bhid', wi, S)
                o_i = jnp.einsum('bhik,bhkd->bhid', qi, S) + jnp.einsum('bhij,bhjd->bhid', attn, u_i)
                S = S + jnp.einsum('bhci,bhcd->bhid', ki, u_i)
                return (S, o_i)
            S0 = jnp.zeros((b, h, dk, dv), q.dtype)
            xs = tuple((jnp.moveaxis(a, 2, 0) for a in (qc, kc, u, w)))
            S, o = jax.lax.scan(step, S0, xs)
            o = jnp.moveaxis(o, 0, 2).reshape(b, h, L, dv)
            return (o, S)
        key = jax.random.key(seed)
        B, L, D, H = (4, 512, 128, 4)
        dh = D // H
        ks = jax.random.split(key, 20)
        s = 1.0 / np.sqrt(D)
        inp = {'hidden_states': jax.random.normal(ks[0], (B, L, D), jnp.float32), 'Wq': jax.random.normal(ks[1], (D, D), jnp.float32) * s, 'Wk': jax.random.normal(ks[2], (D, D), jnp.float32) * s, 'Wv': jax.random.normal(ks[3], (D, D), jnp.float32) * s, 'Wb': jax.random.normal(ks[4], (D, H), jnp.float32) * s, 'conv_q_w': jax.random.normal(ks[5], (D, 4), jnp.float32) * 0.5, 'conv_k_w': jax.random.normal(ks[6], (D, 4), jnp.float32) * 0.5, 'conv_v_w': jax.random.normal(ks[7], (D, 4), jnp.float32) * 0.5, 'local_w': (jax.random.normal(ks[8], (H * dh, 7), jnp.float32) / np.sqrt(7.0)).at[:, -1].add(1.0), 'mid_w': (jax.random.normal(ks[9], (H * dh, 25), jnp.float32) / np.sqrt(25.0)).at[:, -1].add(1.0), 'r_w1': jax.random.normal(ks[10], (D + 14 * H, 2 * (D + 14 * H)), jnp.float32) / np.sqrt(D + 14 * H), 'r_b1': jnp.zeros((2 * (D + 14 * H),), jnp.float32), 'r_w2': jax.random.normal(ks[11], (2 * (D + 14 * H), H * 4), jnp.float32) / np.sqrt(2.0 * (D + 14 * H)), 'r_b2': jnp.zeros((H, 4), jnp.float32).at[:, 2:].set(0.7).reshape(-1), 'mix_w': jnp.ones((H, dh), jnp.float32), 'onorm_w': jnp.ones((dh,), jnp.float32), 'Wo': jax.random.normal(ks[12], (D, D), jnp.float32) * s}
        return inp
    _L0_attn_all = _L0_attn_setup()
    _L0_attn_in = {k: v for k, v in _L0_attn_all.items() if k in ('Wq', 'Wk', 'Wv', 'Wb', 'conv_q_w', 'conv_k_w', 'conv_v_w', 'local_w', 'mid_w', 'r_w1', 'r_b1', 'r_w2', 'r_b2', 'mix_w', 'onorm_w', 'Wo')}
    del _L0_attn_all

    def _L0_xattn_setup():
        import jax, jax.numpy as jnp
        import numpy as np
        N_HEADS = 16
        D_MODEL = 128
        D_K = D_MODEL // N_HEADS
        key = jax.random.key(seed)
        ks = jax.random.split(key, 7)
        B, S = (2, 256)
        scale = 1.0 / np.sqrt(D_MODEL)
        return {'q': jax.random.normal(ks[0], (B, S, D_MODEL), dtype=jnp.float32), 'k': jax.random.normal(ks[1], (B, S, D_MODEL), dtype=jnp.float32), 'v': jax.random.normal(ks[2], (B, S, D_MODEL), dtype=jnp.float32), 'Wq': jax.random.normal(ks[3], (D_MODEL, D_MODEL), dtype=jnp.float32) * scale, 'Wk': jax.random.normal(ks[4], (D_MODEL, D_MODEL), dtype=jnp.float32) * scale, 'Wv': jax.random.normal(ks[5], (D_MODEL, D_MODEL), dtype=jnp.float32) * scale, 'Wo': jax.random.normal(ks[6], (D_MODEL, D_MODEL), dtype=jnp.float32) * scale}
    _L0_xattn_all = _L0_xattn_setup()
    _L0_xattn_in = {k: v for k, v in _L0_xattn_all.items() if k in ('Wq', 'Wk', 'Wv', 'Wo')}
    del _L0_xattn_all

    def _L0_ffn_setup():
        import jax, jax.numpy as jnp
        import numpy as np
        DIM = 128
        HIDDEN = 384
        SCALE = 1.0 / 127.0

        def _dequant(w_int, dtype):
            return w_int.astype(dtype) * jnp.asarray(SCALE, dtype)
        key = jax.random.key(seed)
        k_x, k_g, k_u, k_d = jax.random.split(key, 4)
        x = jax.random.normal(k_x, (4, 256, DIM), dtype=jnp.float32)
        w_gate = jax.random.randint(k_g, (HIDDEN, DIM), -127, 128, dtype=jnp.int32)
        w_up = jax.random.randint(k_u, (HIDDEN, DIM), -127, 128, dtype=jnp.int32)
        w_down = jax.random.randint(k_d, (DIM, HIDDEN), -127, 128, dtype=jnp.int32)
        return {'x': x, 'w_gate': w_gate, 'w_up': w_up, 'w_down': w_down}
    _L0_ffn_all = _L0_ffn_setup()
    _L0_ffn_in = {k: v for k, v in _L0_ffn_all.items() if k in ('w_gate', 'w_up', 'w_down')}
    del _L0_ffn_all

    def _L1_attn_setup():
        import jax, jax.numpy as jnp
        import numpy as np
        N_EMBD = 128
        N_HEAD = 16
        SEQ = 256
        BATCH = 2
        NEG = -1000000000.0
        key = jax.random.key(seed)
        k0, k1, k2 = jax.random.split(key, 3)
        return {'hidden_states': jax.random.normal(k0, (BATCH, SEQ, N_EMBD), dtype=jnp.float32), 'w_attn': jax.random.normal(k1, (3 * N_EMBD, N_EMBD), dtype=jnp.float32) * 0.02, 'b_attn': jnp.zeros((3 * N_EMBD,), dtype=jnp.float32), 'w_proj': jax.random.normal(k2, (N_EMBD, N_EMBD), dtype=jnp.float32) * 0.02, 'b_proj': jnp.zeros((N_EMBD,), dtype=jnp.float32)}
    _L1_attn_all = _L1_attn_setup()
    _L1_attn_in = {k: v for k, v in _L1_attn_all.items() if k in ('w_attn', 'b_attn', 'w_proj', 'b_proj')}
    del _L1_attn_all

    def _L1_xattn_setup():
        import jax, jax.numpy as jnp
        import numpy as np
        D1, D2, D3 = (128, 128, 128)
        key = jax.random.key(seed)
        k1, k2, kw, kb = jax.random.split(key, 4)
        x1 = jax.random.normal(k1, (8, 256, D1), dtype=jnp.float32)
        x2 = jax.random.normal(k2, (8, 256, D2), dtype=jnp.float32)
        bound = 1.0 / np.sqrt(D1 + D2)
        W = jax.random.uniform(kw, (D3, D1 + D2), minval=-bound, maxval=bound, dtype=jnp.float32)
        b = jax.random.uniform(kb, (D3,), minval=-bound, maxval=bound, dtype=jnp.float32)
        return {'x1': x1, 'x2': x2, 'W': W, 'b': b}
    _L1_xattn_all = _L1_xattn_setup()
    _L1_xattn_in = {k: v for k, v in _L1_xattn_all.items() if k in ('W', 'b')}
    del _L1_xattn_all

    def _L1_ffn_setup():
        import jax, jax.numpy as jnp
        import numpy as np
        B, T, C = (4, 256, 128)
        E = 8
        K = 2
        H = 176
        HS = 176 * 2
        key = jax.random.key(seed)
        k = jax.random.split(key, 8)
        s = 0.02
        return {'x': jax.random.normal(k[0], (B, T, C), jnp.float32), 'Wg': jax.random.normal(k[1], (C, E), jnp.float32) * s, 'W1': jax.random.normal(k[2], (E, C, H), jnp.float32) * s, 'W2': jax.random.normal(k[3], (E, C, H), jnp.float32) * s, 'W3': jax.random.normal(k[4], (E, H, C), jnp.float32) * s, 'Ws1': jax.random.normal(k[5], (C, HS), jnp.float32) * s, 'Ws2': jax.random.normal(k[6], (C, HS), jnp.float32) * s, 'Ws3': jax.random.normal(k[7], (HS, C), jnp.float32) * s}
    _L1_ffn_all = _L1_ffn_setup()
    _L1_ffn_in = {k: v for k, v in _L1_ffn_all.items() if k in ('Wg', 'W1', 'W2', 'W3', 'Ws1', 'Ws2', 'Ws3')}
    del _L1_ffn_all

    def _L2_attn_setup():
        import jax, jax.numpy as jnp
        import numpy as np
        D_MODEL = 128
        NUM_HEADS = 16
        HEAD_DIM = D_MODEL // NUM_HEADS
        THETA = 10000.0
        B, T = (4, 256)

        def _cos_sin(seq_len, head_dim, theta):
            freqs = 1.0 / theta ** (jnp.arange(0, head_dim, 2, dtype=jnp.float32) / head_dim)
            t = jnp.arange(seq_len, dtype=jnp.float32)
            angles = jnp.outer(t, freqs)
            return jnp.concatenate([jnp.cos(angles), jnp.sin(angles)], axis=-1)

        def _apply_rope(x, cos_sin):
            x1 = x[..., 0::2]
            x2 = x[..., 1::2]
            half = x.shape[-1] // 2
            cos = cos_sin[:, :half]
            sin = cos_sin[:, half:]
            out = jnp.stack([x1 * cos - x2 * sin, x1 * sin + x2 * cos], axis=-1)
            return out.reshape(x.shape)
        key = jax.random.key(seed)
        k1, k2, k3 = jax.random.split(key, 3)
        x = jax.random.normal(k1, (B, T, D_MODEL), dtype=jnp.float32)
        W_qkv = jax.random.normal(k2, (3 * D_MODEL, D_MODEL), dtype=jnp.float32) * D_MODEL ** (-0.5)
        W_out = jax.random.normal(k3, (D_MODEL, D_MODEL), dtype=jnp.float32) * D_MODEL ** (-0.5)
        return {'x': x, 'W_qkv': W_qkv, 'W_out': W_out}
    _L2_attn_all = _L2_attn_setup()
    _L2_attn_in = {k: v for k, v in _L2_attn_all.items() if k in ('W_qkv', 'W_out')}
    del _L2_attn_all

    def _L2_xattn_setup():
        import jax, jax.numpy as jnp
        import numpy as np
        NUM_HEADS = 16
        KEY_DIM = 128
        D_MODEL = 128

        def _split_heads(x, H):
            B, S, D = x.shape
            return x.reshape(B, S, H, D // H).transpose(0, 2, 1, 3)
        key = jax.random.key(seed)
        ks = jax.random.split(key, 12)
        B, S = (2, 256)
        init = lambda k, shape: jax.random.normal(k, shape, dtype=jnp.float32) * 0.02
        return {'query': jax.random.normal(ks[0], (B, S, D_MODEL), dtype=jnp.float32), 'key': jax.random.normal(ks[1], (B, S, D_MODEL), dtype=jnp.float32), 'value': jax.random.normal(ks[2], (B, S, D_MODEL), dtype=jnp.float32), 'attention_mask': jnp.ones((B, S, S), dtype=jnp.int32), 'Wq': init(ks[3], (D_MODEL, KEY_DIM)), 'bq': jnp.zeros((KEY_DIM,), jnp.float32), 'Wk': init(ks[4], (D_MODEL, KEY_DIM)), 'bk': jnp.zeros((KEY_DIM,), jnp.float32), 'Wv': init(ks[5], (D_MODEL, KEY_DIM)), 'bv': jnp.zeros((KEY_DIM,), jnp.float32), 'Wo': init(ks[6], (KEY_DIM, D_MODEL)), 'bo': jnp.zeros((D_MODEL,), jnp.float32)}
    _L2_xattn_all = _L2_xattn_setup()
    _L2_xattn_in = {k: v for k, v in _L2_xattn_all.items() if k in ('Wq', 'bq', 'Wk', 'bk', 'Wv', 'bv', 'Wo', 'bo')}
    del _L2_xattn_all

    def _L2_ffn_setup():
        import jax, jax.numpy as jnp
        import numpy as np
        B, S, D, E, F = (2, 256, 128, 14, 256)
        key = jax.random.key(seed)
        k = jax.random.split(key, 4)
        h = jax.random.normal(k[0], (B, S, D), dtype=jnp.float32)
        router_w = jax.random.normal(k[1], (D, E), dtype=jnp.float32) * 0.02
        w1 = jax.random.uniform(k[2], (E, D, F), dtype=jnp.float32, minval=-1.0, maxval=1.0) * float(np.sqrt(6.0 / D))
        w2 = jax.random.uniform(k[3], (E, F, D), dtype=jnp.float32, minval=-1.0, maxval=1.0) * float(np.sqrt(6.0 / F))
        b1 = jnp.zeros((E, F), dtype=jnp.float32)
        b2 = jnp.zeros((E, D), dtype=jnp.float32)
        return {'h': h, 'router_w': router_w, 'w1': w1, 'b1': b1, 'w2': w2, 'b2': b2}
    _L2_ffn_all = _L2_ffn_setup()
    _L2_ffn_in = {k: v for k, v in _L2_ffn_all.items() if k in ('router_w', 'w1', 'b1', 'w2', 'b2')}
    del _L2_ffn_all

    def _L3_attn_setup():
        import jax, jax.numpy as jnp
        import numpy as np
        from jax import lax
        D_MODEL = 128
        N_HEADS = 4
        D_STATE = 64
        D_CONV = 4
        EXPAND = 2
        D_INNER = EXPAND * D_MODEL
        DT_RANK = 64
        H_DIN = D_INNER // N_HEADS
        H_DT = DT_RANK // N_HEADS
        H_DS = D_STATE // N_HEADS
        BATCH, SEQ = (2, 128)
        key = jax.random.key(seed)
        ks = jax.random.split(key, 8)
        hidden_states = jax.random.normal(ks[0], (BATCH, SEQ, D_MODEL), dtype=jnp.float32)
        s_in = 1.0 / np.sqrt(D_MODEL)
        in_proj_w = jax.random.uniform(ks[1], (2 * D_INNER, D_MODEL), minval=-s_in, maxval=s_in)
        s_c = 1.0 / np.sqrt(D_CONV)
        conv_w = jax.random.uniform(ks[2], (D_INNER, 1, D_CONV), minval=-s_c, maxval=s_c)
        conv_b = jax.random.uniform(ks[3], (D_INNER,), minval=-s_c, maxval=s_c)
        s_x = 1.0 / np.sqrt(H_DIN)
        x_proj_w = jax.random.uniform(ks[4], ((2 * H_DS + H_DT) * N_HEADS, H_DIN), minval=-s_x, maxval=s_x)
        s_dt = H_DT ** (-0.5)
        dt_proj_w = jax.random.uniform(ks[5], (D_INNER, H_DT), minval=-s_dt, maxval=s_dt)
        dt = jnp.exp(jax.random.uniform(ks[6], (D_INNER,)) * (np.log(0.1) - np.log(0.001)) + np.log(0.001))
        dt = jnp.clip(dt, 0.0001, None)
        dt_proj_b = dt + jnp.log(-jnp.expm1(-dt))
        A_log = jnp.log(jnp.tile(jnp.arange(1, H_DS + 1, dtype=jnp.float32), (D_INNER, 1)))
        Dskip = jnp.ones((D_INNER,), dtype=jnp.float32)
        out_proj_w = jax.random.uniform(ks[7], (D_MODEL, D_INNER), minval=-s_x, maxval=s_x)
        return {'hidden_states': hidden_states, 'in_proj_w': in_proj_w, 'conv_w': conv_w, 'conv_b': conv_b, 'x_proj_w': x_proj_w, 'dt_proj_w': dt_proj_w, 'dt_proj_b': dt_proj_b, 'A_log': A_log, 'Dskip': Dskip, 'out_proj_w': out_proj_w}
    _L3_attn_all = _L3_attn_setup()
    _L3_attn_in = {k: v for k, v in _L3_attn_all.items() if k in ('in_proj_w', 'conv_w', 'conv_b', 'x_proj_w', 'dt_proj_w', 'dt_proj_b', 'A_log', 'Dskip', 'out_proj_w')}
    del _L3_attn_all

    def _L3_xattn_setup():
        import jax, jax.numpy as jnp
        import numpy as np
        NUM_HEADS, NUM_KV, HEAD_DIM, WIDTH = (4, 1, 32, 128)
        MASK_FILL = -2.3819763e+38

        def _apply_rope(x, positions, max_wavelength=10000.0):
            d = x.shape[-1]
            freq_exp = 2.0 / d * jnp.arange(d // 2, dtype=jnp.float32)
            timescale = max_wavelength ** freq_exp
            radians = positions[..., None].astype(jnp.float32) / timescale
            radians = radians[..., None, :]
            sin, cos = (jnp.sin(radians), jnp.cos(radians))
            x1, x2 = jnp.split(x, 2, axis=-1)
            out = jnp.concatenate([x1 * cos - x2 * sin, x2 * cos + x1 * sin], axis=-1)
            return out.astype(x.dtype)

        def _rmsnorm(x, scale):
            var = jnp.mean(jnp.square(x.astype(jnp.float32)), axis=-1, keepdims=True)
            normed = x * jax.lax.rsqrt(var + 1e-06)
            return (normed * (1 + scale)).astype(x.dtype)
        key = jax.random.key(seed)
        ks = jax.random.split(key, 7)
        B, T, S = (8, 64, 256)
        return {'x': jax.random.normal(ks[0], (B, T, WIDTH), jnp.float32), 'mem_seq': jax.random.normal(ks[1], (B, S, WIDTH), jnp.float32), 'mem_mask': jax.random.randint(ks[2], (B, S), 0, 2).astype(bool), 'rms_scale': jax.random.normal(ks[3], (WIDTH,), jnp.float32) * 0.02, 'q_w': jax.random.normal(ks[4], (NUM_HEADS, WIDTH, HEAD_DIM), jnp.float32) / np.sqrt(WIDTH), 'kv_w': jax.random.normal(ks[5], (2, NUM_KV, WIDTH, HEAD_DIM), jnp.float32) / np.sqrt(WIDTH), 'out_w': jax.random.normal(ks[6], (NUM_HEADS, HEAD_DIM, WIDTH), jnp.float32) / np.sqrt(NUM_HEADS * HEAD_DIM)}
    _L3_xattn_all = _L3_xattn_setup()
    _L3_xattn_in = {k: v for k, v in _L3_xattn_all.items() if k in ('rms_scale', 'q_w', 'kv_w', 'out_w')}
    del _L3_xattn_all

    def _L3_ffn_setup():
        import math
        import jax, jax.numpy as jnp
        import numpy as np
        B, S, D, F, E = (8, 256, 128, 512, 8)
        CAPACITY_FACTOR = 1.0
        key = jax.random.key(seed)
        k1, k2, k3, k4 = jax.random.split(key, 4)
        x = jax.random.normal(k1, (B, S, D), dtype=jnp.float32)
        Wr = jax.random.normal(k2, (D, E), dtype=jnp.float32) * (1.0 / math.sqrt(D))
        W1 = jax.random.normal(k3, (E, D, F), dtype=jnp.float32) * (1.0 / math.sqrt(D))
        W2 = jax.random.normal(k4, (E, F, D), dtype=jnp.float32) * (1.0 / math.sqrt(F))
        return {'x': x, 'Wr': Wr, 'W1': W1, 'W2': W2}
    _L3_ffn_all = _L3_ffn_setup()
    _L3_ffn_in = {k: v for k, v in _L3_ffn_all.items() if k in ('Wr', 'W1', 'W2')}
    del _L3_ffn_all
    return {'x': x, 'ctx_1024': ctx_1024, 'mask_BxSxS2_if1': mask_BxSxS2_if1, 'mask_BxS2_bk0': mask_BxS2_bk0, 'L0_attn_Wq': _L0_attn_in['Wq'], 'L0_attn_Wk': _L0_attn_in['Wk'], 'L0_attn_Wv': _L0_attn_in['Wv'], 'L0_attn_Wb': _L0_attn_in['Wb'], 'L0_attn_conv_q_w': _L0_attn_in['conv_q_w'], 'L0_attn_conv_k_w': _L0_attn_in['conv_k_w'], 'L0_attn_conv_v_w': _L0_attn_in['conv_v_w'], 'L0_attn_local_w': _L0_attn_in['local_w'], 'L0_attn_mid_w': _L0_attn_in['mid_w'], 'L0_attn_r_w1': _L0_attn_in['r_w1'], 'L0_attn_r_b1': _L0_attn_in['r_b1'], 'L0_attn_r_w2': _L0_attn_in['r_w2'], 'L0_attn_r_b2': _L0_attn_in['r_b2'], 'L0_attn_mix_w': _L0_attn_in['mix_w'], 'L0_attn_onorm_w': _L0_attn_in['onorm_w'], 'L0_attn_Wo': _L0_attn_in['Wo'], 'L0_xattn_Wq': _L0_xattn_in['Wq'], 'L0_xattn_Wk': _L0_xattn_in['Wk'], 'L0_xattn_Wv': _L0_xattn_in['Wv'], 'L0_xattn_Wo': _L0_xattn_in['Wo'], 'L0_ffn_w_gate': _L0_ffn_in['w_gate'], 'L0_ffn_w_up': _L0_ffn_in['w_up'], 'L0_ffn_w_down': _L0_ffn_in['w_down'], 'L1_attn_w_attn': _L1_attn_in['w_attn'], 'L1_attn_b_attn': _L1_attn_in['b_attn'], 'L1_attn_w_proj': _L1_attn_in['w_proj'], 'L1_attn_b_proj': _L1_attn_in['b_proj'], 'L1_xattn_W': _L1_xattn_in['W'], 'L1_xattn_b': _L1_xattn_in['b'], 'L1_ffn_Wg': _L1_ffn_in['Wg'], 'L1_ffn_W1': _L1_ffn_in['W1'], 'L1_ffn_W2': _L1_ffn_in['W2'], 'L1_ffn_W3': _L1_ffn_in['W3'], 'L1_ffn_Ws1': _L1_ffn_in['Ws1'], 'L1_ffn_Ws2': _L1_ffn_in['Ws2'], 'L1_ffn_Ws3': _L1_ffn_in['Ws3'], 'L2_attn_W_qkv': _L2_attn_in['W_qkv'], 'L2_attn_W_out': _L2_attn_in['W_out'], 'L2_xattn_Wq': _L2_xattn_in['Wq'], 'L2_xattn_bq': _L2_xattn_in['bq'], 'L2_xattn_Wk': _L2_xattn_in['Wk'], 'L2_xattn_bk': _L2_xattn_in['bk'], 'L2_xattn_Wv': _L2_xattn_in['Wv'], 'L2_xattn_bv': _L2_xattn_in['bv'], 'L2_xattn_Wo': _L2_xattn_in['Wo'], 'L2_xattn_bo': _L2_xattn_in['bo'], 'L2_ffn_router_w': _L2_ffn_in['router_w'], 'L2_ffn_w1': _L2_ffn_in['w1'], 'L2_ffn_b1': _L2_ffn_in['b1'], 'L2_ffn_w2': _L2_ffn_in['w2'], 'L2_ffn_b2': _L2_ffn_in['b2'], 'L3_attn_in_proj_w': _L3_attn_in['in_proj_w'], 'L3_attn_conv_w': _L3_attn_in['conv_w'], 'L3_attn_conv_b': _L3_attn_in['conv_b'], 'L3_attn_x_proj_w': _L3_attn_in['x_proj_w'], 'L3_attn_dt_proj_w': _L3_attn_in['dt_proj_w'], 'L3_attn_dt_proj_b': _L3_attn_in['dt_proj_b'], 'L3_attn_A_log': _L3_attn_in['A_log'], 'L3_attn_Dskip': _L3_attn_in['Dskip'], 'L3_attn_out_proj_w': _L3_attn_in['out_proj_w'], 'L3_xattn_rms_scale': _L3_xattn_in['rms_scale'], 'L3_xattn_q_w': _L3_xattn_in['q_w'], 'L3_xattn_kv_w': _L3_xattn_in['kv_w'], 'L3_xattn_out_w': _L3_xattn_in['out_w'], 'L3_ffn_Wr': _L3_ffn_in['Wr'], 'L3_ffn_W1': _L3_ffn_in['W1'], 'L3_ffn_W2': _L3_ffn_in['W2']}

def reference(x, ctx_1024, mask_BxSxS2_if1, mask_BxS2_bk0, L0_attn_Wq, L0_attn_Wk, L0_attn_Wv, L0_attn_Wb, L0_attn_conv_q_w, L0_attn_conv_k_w, L0_attn_conv_v_w, L0_attn_local_w, L0_attn_mid_w, L0_attn_r_w1, L0_attn_r_b1, L0_attn_r_w2, L0_attn_r_b2, L0_attn_mix_w, L0_attn_onorm_w, L0_attn_Wo, L0_xattn_Wq, L0_xattn_Wk, L0_xattn_Wv, L0_xattn_Wo, L0_ffn_w_gate, L0_ffn_w_up, L0_ffn_w_down, L1_attn_w_attn, L1_attn_b_attn, L1_attn_w_proj, L1_attn_b_proj, L1_xattn_W, L1_xattn_b, L1_ffn_Wg, L1_ffn_W1, L1_ffn_W2, L1_ffn_W3, L1_ffn_Ws1, L1_ffn_Ws2, L1_ffn_Ws3, L2_attn_W_qkv, L2_attn_W_out, L2_xattn_Wq, L2_xattn_bq, L2_xattn_Wk, L2_xattn_bk, L2_xattn_Wv, L2_xattn_bv, L2_xattn_Wo, L2_xattn_bo, L2_ffn_router_w, L2_ffn_w1, L2_ffn_b1, L2_ffn_w2, L2_ffn_b2, L3_attn_in_proj_w, L3_attn_conv_w, L3_attn_conv_b, L3_attn_x_proj_w, L3_attn_dt_proj_w, L3_attn_dt_proj_b, L3_attn_A_log, L3_attn_Dskip, L3_attn_out_proj_w, L3_xattn_rms_scale, L3_xattn_q_w, L3_xattn_kv_w, L3_xattn_out_w, L3_ffn_Wr, L3_ffn_W1, L3_ffn_W2):
    import jax
    import jax.numpy as jnp

    def _L0_attn_ref(hidden_states, Wq, Wk, Wv, Wb, conv_q_w, conv_k_w, conv_v_w, local_w, mid_w, r_w1, r_b1, r_w2, r_b2, mix_w, onorm_w, Wo):
        import jax, jax.numpy as jnp
        import numpy as np
        CHUNK = 32
        FLOOR = 0.01
        EPS_MIX = 1e-05
        EPS_NORM = 1e-05

        def l2norm(x):
            return x / jnp.sqrt(jnp.sum(x * x, -1, keepdims=True) + 1e-12)

        def dw_causal_conv(x, w):
            K = w.shape[-1]
            L = x.shape[1]
            xp = jnp.pad(x, ((0, 0), (K - 1, 0), (0, 0)))
            y = jnp.zeros_like(x)
            for t in range(K):
                y = y + xp[:, t:t + L, :] * w[:, t]
            return y

        def delta_rule_chunkwise(q, k, v, beta):
            b, h, L, dk = q.shape
            dv = v.shape[-1]
            c = CHUNK
            n = L // c
            q = l2norm(q)
            k = l2norm(k)
            v = v * beta[..., None]
            kb = k * beta[..., None]
            rs = lambda x: x.reshape(b, h, n, c, -1)
            qc, kc, vc, kbc = (rs(q), rs(k), rs(v), rs(kb))
            T = -jnp.einsum('bhnid,bhnjd->bhnij', kbc, kc)
            tri_strict = jnp.tril(jnp.ones((c, c), bool), -1)
            T = jnp.where(tri_strict, T, 0.0)
            for i in range(1, c):
                T = T.at[..., i, :i].add(jnp.einsum('bhnj,bhnji->bhni', T[..., i, :], T[..., :, :i]))
            T = T + jnp.eye(c, dtype=T.dtype)
            u = jnp.einsum('bhnij,bhnjd->bhnid', T, vc)
            w = jnp.einsum('bhnij,bhnjd->bhnid', T, kbc)
            mask_incl = jnp.tril(jnp.ones((c, c), bool), 0)

            def step(S, inp):
                qi, ki, ui, wi = inp
                attn = jnp.einsum('bhid,bhjd->bhij', qi, ki)
                attn = jnp.where(mask_incl, attn, 0.0)
                u_i = ui - jnp.einsum('bhik,bhkd->bhid', wi, S)
                o_i = jnp.einsum('bhik,bhkd->bhid', qi, S) + jnp.einsum('bhij,bhjd->bhid', attn, u_i)
                S = S + jnp.einsum('bhci,bhcd->bhid', ki, u_i)
                return (S, o_i)
            S0 = jnp.zeros((b, h, dk, dv), q.dtype)
            xs = tuple((jnp.moveaxis(a, 2, 0) for a in (qc, kc, u, w)))
            S, o = jax.lax.scan(step, S0, xs)
            o = jnp.moveaxis(o, 0, 2).reshape(b, h, L, dv)
            return (o, S)
        B, L, D = hidden_states.shape
        H = mix_w.shape[0]
        dh = mix_w.shape[1]
        q = jax.nn.silu(dw_causal_conv(hidden_states @ Wq, conv_q_w))
        k = jax.nn.silu(dw_causal_conv(hidden_states @ Wk, conv_k_w))
        v = jax.nn.silu(dw_causal_conv(hidden_states @ Wv, conv_v_w))
        q4 = q.reshape(B, L, H, dh)
        k4 = k.reshape(B, L, H, dh)
        v4 = v.reshape(B, L, H, dh)
        beta = jax.nn.sigmoid(hidden_states @ Wb)
        delta_out, _ = delta_rule_chunkwise(jnp.transpose(q4, (0, 2, 1, 3)), jnp.transpose(k4, (0, 2, 1, 3)), jnp.transpose(v4, (0, 2, 1, 3)), jnp.transpose(beta, (0, 2, 1)))
        delta_out = jnp.transpose(delta_out, (0, 2, 1, 3))
        v_direct = v4
        vflat = v4.reshape(B, L, H * dh)
        local_out = dw_causal_conv(vflat, local_w).reshape(B, L, H, dh)
        mid_out = dw_causal_conv(vflat, mid_w).reshape(B, L, H, dh)
        outs = [local_out, mid_out, delta_out, v_direct]
        feats = []
        for o_ in outs:
            feats.append(o_.mean(-1))
            feats.append(jnp.var(o_, -1, ddof=1))
        for i in range(4):
            for j in range(i + 1, 4):
                feats.append((outs[i] * outs[j]).mean(-1))
        router_feat = jnp.concatenate([hidden_states] + feats, axis=-1)
        h1 = jax.nn.silu(router_feat @ r_w1 + r_b1)
        logits = (h1 @ r_w2 + r_b2).reshape(B, L, H, 4)
        p = jax.nn.softmax(logits, -1)
        p = p * (1.0 - 4.0 * FLOOR) + FLOOR
        mixed = sum((p[..., i:i + 1] * outs[i] for i in range(4)))
        rms = jnp.sqrt(jnp.mean(mixed * mixed, -1, keepdims=True) + EPS_MIX)
        mixed = mixed / rms * mix_w
        rms2 = jnp.sqrt(jnp.mean(mixed * mixed, -1, keepdims=True) + EPS_NORM)
        o_n = mixed / rms2 * onorm_w
        return o_n.reshape(B, L, H * dh) @ Wo

    def _L0_xattn_ref(q, k, v, Wq, Wk, Wv, Wo):
        import jax, jax.numpy as jnp
        import numpy as np
        N_HEADS = 16
        D_MODEL = 128
        D_K = D_MODEL // N_HEADS
        B, S, _ = q.shape

        def split_heads(x):
            return x.reshape(B, S, N_HEADS, D_K).transpose(0, 2, 1, 3)
        query = split_heads(q @ Wq.T)
        key_ = split_heads(k @ Wk.T)
        value = split_heads(v @ Wv.T)
        scores = jnp.einsum('bhqd,bhkd->bhqk', query, key_) / jnp.sqrt(jnp.asarray(D_K, dtype=query.dtype))
        attn_probs = jax.nn.softmax(scores, axis=-1)
        attn_out = jnp.einsum('bhqk,bhkd->bhqd', attn_probs, value)
        x = attn_out.transpose(0, 2, 1, 3).reshape(B, S, D_MODEL)
        return x @ Wo.T

    def _L0_ffn_ref(x, w_gate, w_up, w_down):
        import jax, jax.numpy as jnp
        import numpy as np
        DIM = 128
        HIDDEN = 384
        SCALE = 1.0 / 127.0

        def _dequant(w_int, dtype):
            return w_int.astype(dtype) * jnp.asarray(SCALE, dtype)
        wg = _dequant(w_gate, x.dtype)
        wu = _dequant(w_up, x.dtype)
        wd = _dequant(w_down, x.dtype)
        gate = jnp.einsum('bsd,hd->bsh', x, wg)
        up = jnp.einsum('bsd,hd->bsh', x, wu)
        h = jax.nn.silu(gate) * up
        return jnp.einsum('bsh,dh->bsd', h, wd)

    def _L1_attn_ref(hidden_states, w_attn, b_attn, w_proj, b_proj):
        import jax, jax.numpy as jnp
        import numpy as np
        N_EMBD = 128
        N_HEAD = 16
        SEQ = 256
        BATCH = 2
        NEG = -1000000000.0
        B, S, E = hidden_states.shape
        H = N_HEAD
        D = E // H
        qkv = hidden_states @ w_attn.T + b_attn
        q, k, v = jnp.split(qkv, 3, axis=-1)
        split = lambda t: t.reshape(B, S, H, D).transpose(0, 2, 1, 3)
        q, k, v = (split(q), split(k), split(v))
        w = jnp.einsum('bhnd,bhmd->bhnm', q, k) * jax.lax.rsqrt(float(D))
        mask = jnp.tril(jnp.ones((S, S), dtype=jnp.float32))
        w = jnp.where(mask > 0, w, NEG)
        w = jax.nn.softmax(w, axis=-1)
        attn = jnp.einsum('bhnm,bhmd->bhnd', w, v)
        attn = attn.transpose(0, 2, 1, 3).reshape(B, S, E)
        return attn @ w_proj.T + b_proj

    def _L1_xattn_ref(x1, x2, W, b):
        import jax, jax.numpy as jnp
        import numpy as np
        D1, D2, D3 = (128, 128, 128)
        d1 = x1.shape[-1]
        W1 = W[:, :d1]
        W2 = W[:, d1:]
        part1 = jnp.einsum('bld,ed->ble', x1, W1)
        part2 = jnp.einsum('bld,ed->be', x2, W2) / x2.shape[1]
        return part1 + part2[:, None, :] + b

    def _L1_ffn_ref(x, Wg, W1, W2, W3, Ws1, Ws2, Ws3):
        import jax, jax.numpy as jnp
        import numpy as np
        B, T, C = (4, 256, 128)
        E = 8
        K = 2
        H = 176
        HS = 176 * 2
        b, t, c = x.shape
        xf = x.reshape(-1, c)
        n = xf.shape[0]
        router = xf @ Wg
        top_logits, idx = jax.lax.top_k(router, K)
        probs = jax.nn.softmax(top_logits.astype(jnp.float32), axis=-1).astype(x.dtype)
        w = jnp.zeros((n, E), x.dtype).at[jnp.arange(n)[:, None], idx].add(probs)
        h = jax.nn.silu(jnp.einsum('tc,ech->eth', xf, W1)) * jnp.einsum('tc,ech->eth', xf, W2)
        y = jnp.einsum('eth,ehc,te->tc', h, W3, w)
        y = y.reshape(b, t, c)
        hs = jax.nn.silu(xf @ Ws1) * (xf @ Ws2)
        y = y + (hs @ Ws3).reshape(b, t, c)
        return y

    def _L2_attn_ref(x, W_qkv, W_out):
        import jax, jax.numpy as jnp
        import numpy as np
        D_MODEL = 128
        NUM_HEADS = 16
        HEAD_DIM = D_MODEL // NUM_HEADS
        THETA = 10000.0
        B, T = (4, 256)

        def _cos_sin(seq_len, head_dim, theta):
            freqs = 1.0 / theta ** (jnp.arange(0, head_dim, 2, dtype=jnp.float32) / head_dim)
            t = jnp.arange(seq_len, dtype=jnp.float32)
            angles = jnp.outer(t, freqs)
            return jnp.concatenate([jnp.cos(angles), jnp.sin(angles)], axis=-1)

        def _apply_rope(x, cos_sin):
            x1 = x[..., 0::2]
            x2 = x[..., 1::2]
            half = x.shape[-1] // 2
            cos = cos_sin[:, :half]
            sin = cos_sin[:, half:]
            out = jnp.stack([x1 * cos - x2 * sin, x1 * sin + x2 * cos], axis=-1)
            return out.reshape(x.shape)
        Bsz, Tlen, _ = x.shape
        qkv = jnp.einsum('bti,oi->bto', x, W_qkv)
        qkv = qkv.reshape(Bsz, Tlen, 3 * NUM_HEADS, HEAD_DIM).transpose(0, 2, 1, 3)
        q, k, v = jnp.split(qkv, 3, axis=1)
        cos_sin = _cos_sin(Tlen, HEAD_DIM, THETA)
        q = _apply_rope(q, cos_sin)
        k = _apply_rope(k, cos_sin)
        scores = jnp.einsum('bhqd,bhkd->bhqk', q, k) / np.sqrt(HEAD_DIM).astype(np.float32)
        causal = jnp.tril(jnp.ones((Tlen, Tlen), dtype=bool))
        scores = jnp.where(causal[None, None], scores, -jnp.inf)
        attn = jax.nn.softmax(scores, axis=-1)
        o = jnp.einsum('bhqk,bhkd->bhqd', attn, v)
        o = o.transpose(0, 2, 1, 3).reshape(Bsz, Tlen, D_MODEL)
        return jnp.einsum('bti,oi->bto', o, W_out)

    def _L2_xattn_ref(query, key, value, attention_mask, Wq, bq, Wk, bk, Wv, bv, Wo, bo):
        import jax, jax.numpy as jnp
        import numpy as np
        NUM_HEADS = 16
        KEY_DIM = 128
        D_MODEL = 128

        def _split_heads(x, H):
            B, S, D = x.shape
            return x.reshape(B, S, H, D // H).transpose(0, 2, 1, 3)
        H = NUM_HEADS
        dh = KEY_DIM // H
        q = _split_heads(query @ Wq + bq, H)
        k = _split_heads(key @ Wk + bk, H)
        v = _split_heads(value @ Wv + bv, H)
        scores = jnp.einsum('bhqd,bhkd->bhqk', q, k) / jnp.sqrt(jnp.float32(dh))
        mask = attention_mask[:, None, :, :].astype(scores.dtype)
        scores = scores - (1.0 - mask) * 1000000.0
        proba = jax.nn.softmax(scores, axis=-1)
        attn = jnp.einsum('bhqk,bhkd->bhqd', proba, v)
        B, _, Sq, _ = attn.shape
        merged = attn.transpose(0, 2, 1, 3).reshape(B, Sq, H * dh)
        return merged @ Wo + bo

    def _L2_ffn_ref(h, router_w, w1, b1, w2, b2):
        import jax, jax.numpy as jnp
        import numpy as np
        B, S, D, E, F = (2, 256, 128, 14, 256)
        Bb, Ss, Dd = h.shape
        x = h.reshape(-1, Dd)
        logits = x @ router_w
        assignments = jnp.argmax(logits, axis=-1)
        probs = jax.nn.softmax(logits, axis=-1)
        weights = jnp.take_along_axis(probs, assignments[:, None], axis=1)[:, 0]
        hid = jnp.einsum('nd,edf->nef', x, w1) + b1
        hid = jax.nn.gelu(hid, approximate=False)
        all_out = jnp.einsum('nef,efd->ned', hid, w2) + b2
        sel = jnp.take_along_axis(all_out, assignments[:, None, None], axis=1)[:, 0, :]
        moe_out = (sel * weights[:, None]).reshape(Bb, Ss, Dd)
        return moe_out

    def _L3_attn_ref(hidden_states, in_proj_w, conv_w, conv_b, x_proj_w, dt_proj_w, dt_proj_b, A_log, Dskip, out_proj_w):
        import jax, jax.numpy as jnp
        import numpy as np
        from jax import lax
        D_MODEL = 128
        N_HEADS = 4
        D_STATE = 64
        D_CONV = 4
        EXPAND = 2
        D_INNER = EXPAND * D_MODEL
        DT_RANK = 64
        H_DIN = D_INNER // N_HEADS
        H_DT = DT_RANK // N_HEADS
        H_DS = D_STATE // N_HEADS
        BATCH, SEQ = (2, 128)
        b, L, _ = hidden_states.shape
        xz = hidden_states @ in_proj_w.T
        x, z = jnp.split(xz, 2, axis=-1)
        xp = jnp.pad(x, ((0, 0), (D_CONV - 1, 0), (0, 0)))
        w = conv_w[:, 0, :]
        xc = conv_b
        for k in range(D_CONV):
            xc = xc + xp[:, k:k + L, :] * w[:, k]
        x = jax.nn.silu(xc)
        xh = x.reshape(b, L, N_HEADS, H_DIN)
        xw = x_proj_w.reshape(N_HEADS, 2 * H_DS + H_DT, H_DIN)
        x_dbl = jnp.einsum('hod,blhd->blho', xw, xh)
        dt_r, Bm, Cm = jnp.split(x_dbl, [H_DT, H_DT + H_DS], axis=-1)
        dtw = dt_proj_w.reshape(N_HEADS, H_DIN, H_DT)
        delta = jnp.einsum('hdr,blhr->blhd', dtw, dt_r)
        delta = jax.nn.softplus(delta + dt_proj_b.reshape(N_HEADS, H_DIN))
        A = -jnp.exp(A_log).reshape(N_HEADS, H_DIN, H_DS)

        def step(s, inp):
            d_t, u_t, B_t, C_t = inp
            dA = jnp.exp(d_t[..., None] * A)
            s = s * dA + (d_t * u_t)[..., None] * B_t[:, :, None, :]
            y_t = jnp.einsum('bhdn,bhn->bhd', s, C_t)
            return (s, y_t)
        s0 = jnp.zeros((b, N_HEADS, H_DIN, H_DS), dtype=x.dtype)
        scan_in = (delta.transpose(1, 0, 2, 3), xh.transpose(1, 0, 2, 3), Bm.transpose(1, 0, 2, 3), Cm.transpose(1, 0, 2, 3))
        _, ys = lax.scan(step, s0, scan_in)
        y = ys.transpose(1, 0, 2, 3).reshape(b, L, D_INNER)
        y = y + x * Dskip
        y = y * jax.nn.silu(z)
        out = y @ out_proj_w.T
        return out

    def _L3_xattn_ref(x, mem_seq, mem_mask, rms_scale, q_w, kv_w, out_w):
        import jax, jax.numpy as jnp
        import numpy as np
        NUM_HEADS, NUM_KV, HEAD_DIM, WIDTH = (4, 1, 32, 128)
        MASK_FILL = -2.3819763e+38

        def _apply_rope(x, positions, max_wavelength=10000.0):
            d = x.shape[-1]
            freq_exp = 2.0 / d * jnp.arange(d // 2, dtype=jnp.float32)
            timescale = max_wavelength ** freq_exp
            radians = positions[..., None].astype(jnp.float32) / timescale
            radians = radians[..., None, :]
            sin, cos = (jnp.sin(radians), jnp.cos(radians))
            x1, x2 = jnp.split(x, 2, axis=-1)
            out = jnp.concatenate([x1 * cos - x2 * sin, x2 * cos + x1 * sin], axis=-1)
            return out.astype(x.dtype)

        def _rmsnorm(x, scale):
            var = jnp.mean(jnp.square(x.astype(jnp.float32)), axis=-1, keepdims=True)
            normed = x * jax.lax.rsqrt(var + 1e-06)
            return (normed * (1 + scale)).astype(x.dtype)
        B, S, _ = mem_seq.shape
        T = x.shape[1]
        G = NUM_HEADS // NUM_KV
        xn = _rmsnorm(x, rms_scale)
        mn = _rmsnorm(mem_seq, rms_scale)
        q = jnp.einsum('BTD,NDH->BTNH', xn, q_w)
        kv = jnp.einsum('BSD,cKDH->cBSKH', mn, kv_w)
        k, v = (kv[0], kv[1])
        q_pos = jnp.broadcast_to(jnp.arange(S, T + S), (B, T))
        k_pos = jnp.broadcast_to(jnp.arange(S), (B, S))
        q = _apply_rope(q, q_pos) * HEAD_DIM ** (-0.5)
        k = _apply_rope(k, k_pos)
        q = q.reshape(B, T, NUM_KV, G, HEAD_DIM)
        logits = jnp.einsum('BTKGH,BSKH->BKGTS', q, k, preferred_element_type=jnp.float32)
        masked = jnp.where(mem_mask[:, None, None, None, :], logits, MASK_FILL)
        probs = jax.nn.softmax(masked, axis=-1).astype(x.dtype)
        enc = jnp.einsum('BKGTS,BSKH->BTKGH', probs, v).reshape(B, T, NUM_HEADS, HEAD_DIM)
        return jnp.einsum('BTNH,NHD->BTD', enc, out_w)

    def _L3_ffn_ref(x, Wr, W1, W2):
        import math
        import jax, jax.numpy as jnp
        import numpy as np
        B, S, D, F, E = (8, 256, 128, 512, 8)
        CAPACITY_FACTOR = 1.0
        b, s, d = x.shape
        t = b * s
        cap = max(math.ceil(t * CAPACITY_FACTOR / E), 1)
        xf = x.reshape(t, d)
        probs = jax.nn.softmax(xf.astype(jnp.float32) @ Wr, axis=-1)
        eidx = jnp.argmax(probs, axis=-1)
        p_tok = jnp.take_along_axis(probs, eidx[:, None], axis=1)[:, 0]
        onehot = jax.nn.one_hot(eidx, E, dtype=jnp.int32)
        rank_all = jnp.cumsum(onehot, axis=0) - onehot
        rank = jnp.take_along_axis(rank_all, eidx[:, None], axis=1)[:, 0]
        keep = rank < cap
        slot = jnp.where(keep, rank, cap)
        dispatch = jnp.zeros((E, cap + 1), dtype=jnp.int32).at[eidx, slot].set(jnp.arange(t, dtype=jnp.int32))
        valid = jnp.zeros((E, cap + 1), dtype=bool).at[eidx, slot].set(keep)
        dispatch = dispatch[:, :cap]
        valid = valid[:, :cap]
        xe = xf[dispatch]
        h = jnp.maximum(jnp.einsum('ecd,edf->ecf', xe, W1), 0.0)
        ye = jnp.einsum('ecf,efd->ecd', h, W2)
        pe = p_tok[dispatch]
        ye = ye * (pe * valid.astype(ye.dtype))[:, :, None]
        y = jnp.zeros((t, d), dtype=x.dtype).at[dispatch.reshape(-1)].add(ye.reshape(E * cap, d).astype(x.dtype))
        return y.reshape(b, s, d)
    x = x + _L0_attn_ref(_layernorm(x, axis=-1), L0_attn_Wq, L0_attn_Wk, L0_attn_Wv, L0_attn_Wb, L0_attn_conv_q_w, L0_attn_conv_k_w, L0_attn_conv_v_w, L0_attn_local_w, L0_attn_mid_w, L0_attn_r_w1, L0_attn_r_b1, L0_attn_r_w2, L0_attn_r_b2, L0_attn_mix_w, L0_attn_onorm_w, L0_attn_Wo)
    x = x + _L0_xattn_ref(_layernorm(x, axis=-1), ctx_1024, ctx_1024, L0_xattn_Wq, L0_xattn_Wk, L0_xattn_Wv, L0_xattn_Wo)
    x = x + _L0_ffn_ref(_layernorm(x, axis=-1), L0_ffn_w_gate, L0_ffn_w_up, L0_ffn_w_down)
    x = x + _L1_attn_ref(_layernorm(x, axis=-1), L1_attn_w_attn, L1_attn_b_attn, L1_attn_w_proj, L1_attn_b_proj)
    x = x + _L1_xattn_ref(_layernorm(x, axis=-1), ctx_1024, L1_xattn_W, L1_xattn_b)
    x = x + _L1_ffn_ref(_layernorm(x, axis=-1), L1_ffn_Wg, L1_ffn_W1, L1_ffn_W2, L1_ffn_W3, L1_ffn_Ws1, L1_ffn_Ws2, L1_ffn_Ws3)
    x = x + _L2_attn_ref(_layernorm(x, axis=-1), L2_attn_W_qkv, L2_attn_W_out)
    x = x + _L2_xattn_ref(_layernorm(x, axis=-1), ctx_1024, ctx_1024, mask_BxSxS2_if1, L2_xattn_Wq, L2_xattn_bq, L2_xattn_Wk, L2_xattn_bk, L2_xattn_Wv, L2_xattn_bv, L2_xattn_Wo, L2_xattn_bo)
    x = x + _L2_ffn_ref(_layernorm(x, axis=-1), L2_ffn_router_w, L2_ffn_w1, L2_ffn_b1, L2_ffn_w2, L2_ffn_b2)
    x = x + _L3_attn_ref(_layernorm(x, axis=-1), L3_attn_in_proj_w, L3_attn_conv_w, L3_attn_conv_b, L3_attn_x_proj_w, L3_attn_dt_proj_w, L3_attn_dt_proj_b, L3_attn_A_log, L3_attn_Dskip, L3_attn_out_proj_w)
    x = x + _L3_xattn_ref(_layernorm(x, axis=-1), ctx_1024, mask_BxS2_bk0, L3_xattn_rms_scale, L3_xattn_q_w, L3_xattn_kv_w, L3_xattn_out_w)
    x = x + _L3_ffn_ref(_layernorm(x, axis=-1), L3_ffn_Wr, L3_ffn_W1, L3_ffn_W2)
    return x

_drawn_inputs = setup_inputs


def setup_inputs(seed=0):
    import zlib

    import numpy as np

    out = dict(_drawn_inputs(seed))
    spreads = {'L0_attn_r_b1': (0.0, 0.1),
     'L0_attn_mix_w': (1.0, 0.2),
     'L0_attn_onorm_w': (1.0, 0.2),
     'L1_attn_b_attn': (0.0, 0.1),
     'L1_attn_b_proj': (0.0, 0.1),
     'L2_xattn_bq': (0.0, 0.1),
     'L2_xattn_bk': (0.0, 0.1),
     'L2_xattn_bv': (0.0, 0.1),
     'L2_xattn_bo': (0.0, 0.1),
     'L2_ffn_b1': (0.0, 0.1),
     'L2_ffn_b2': (0.0, 0.1),
     'L3_attn_Dskip': (1.0, 0.2)}
    factors = {}
    for name, (base, spread) in spreads.items():
        noise = np.random.default_rng([zlib.crc32(name.encode()), seed]).standard_normal(out[name].shape)
        drawn = base * np.exp(spread * noise) if base else spread * noise
        out[name] = jnp.asarray(drawn.astype(out[name].dtype))
    for name, factor in factors.items():
        out[name] = (out[name] * factor).astype(out[name].dtype)
    return out
```

```python
from contextlib import ExitStack

import numpy as np
import concourse.bass as bass
from concourse import mybir

F32 = mybir.dt.float32
BF16 = mybir.dt.bfloat16
I32 = mybir.dt.int32
U8 = mybir.dt.uint8
ACT = mybir.ActivationFunctionType
ALU = mybir.AluOpType
X = mybir.AxisListType.X

B, L, D = 32, 128, 128
G = 4
NGROUPS = B // G
N = G * L
NH, DH = 16, 8
NJ, NI = 4, 4
DELTA_H, DELTA_D = 4, 32
MID_K, LOCAL_K, CONV_K = 25, 7, 4
PAD = MID_K - 1
NFEAT = 14 * DELTA_H
RH = 2 * (D + NFEAT)
RCH = [(0, 128), (128, 128), (256, RH - 256)]
FFH = 384
E1, H1, HS1 = 8, 176, 352
C1 = E1 * H1 // 128
SCH = [(0, 128), (128, 128), (256, HS1 - 256)]
E2, F2 = 14, 256
E3, F3 = 8, 512
CAP = B * L // E3
DS = 16
SLOTS = ((0, 0), (0, 1), (0, 2), (1, 0), (1, 1), (2, 0))
SCALE16 = float(DH) ** -0.5
BIG = 1.0e30
MASK_BIG, MASK_SMALL = 999424.0, 576.0
SCRATCH = 17500
SECTIONS = ["L0_delta", "L0_cross", "L0_ffn", "L1_attn", "L1_mix", "L1_moe", "L2_attn", "L2_cross", "L2_moe",
            "L3_mamba", "L3_cross", "L3_moe"]


def host_constants():
    c = {}
    i, j = np.arange(L)[:, None], np.arange(L)[None, :]
    c["ident"] = np.eye(128, dtype=np.float32)
    levels = [1, 2, 4, 8, 16, 32, 64]
    lev = np.stack([(i // (2 * b) == j // (2 * b)) & ((i // b) % 2 == 1) & ((j // b) % 2 == 0) for b in levels])
    c["delta_masks"] = np.stack([-(i < j).astype(np.float32), -lev[0].astype(np.float32),
                                 (i <= j).astype(np.float32)], 1)
    c["level_T"] = np.ascontiguousarray(lev.transpose(2, 0, 1)).astype(np.float32)
    c["causal"] = np.where(i >= j, 0.0, -1e9).astype(np.float32)
    c["causal_T"] = np.where(i <= j, 0.0, -1e9).astype(np.float32)
    c["before_T"] = (i < j).astype(np.float32)
    c["same_head"] = (i // DELTA_D == j // DELTA_D).astype(np.float32)
    c["slot"] = (i[:, :1] % 32 // DH == np.arange(NI)[None, :]).astype(np.float32)
    c["rev"] = np.broadcast_to(16.0 - np.arange(16, dtype=np.float32), (128, 16)).copy()
    c["sel1"] = (np.arange(E1)[:, None] == np.arange(E1 * H1)[None, :] // H1).astype(np.float32)
    row = np.arange(96)[:, None, None]
    c["sel_state"] = ((row % DS == np.arange(DS)[None, :, None]) &
                      (row % 32 // DS == np.arange(128)[None, None, :] // 64)).astype(np.float32)
    c["sel_part"] = ((i[:, :1] % 32 == np.arange(NH)[None, :]) & (i[:, :1] < 96)).astype(np.float32)
    t = np.arange(L, dtype=np.float32)
    fr = (1.0 / np.float32(10000.0) ** (np.arange(0, DH, 2, dtype=np.float32) / DH)).astype(np.float32)
    ang = np.outer(t, fr).astype(np.float32)
    p = np.arange(128)
    cos, sin = np.cos(ang).T[(p % DH) // 2], np.sin(ang).T[(p % DH) // 2]
    sin = np.where(p[:, None] % 2 == 0, -sin, sin)
    c["rope2"] = np.stack([cos * SCALE16, sin * SCALE16, cos, sin], 1).astype(np.float32)
    ts = np.float32(10000.0) ** (np.float32(2.0 / 32) * np.arange(16, dtype=np.float32))
    sgn = np.where(p[:, None] % 32 < 16, -1.0, 1.0)
    out = []
    for pos, sc in ((t + L, 32.0 ** -0.5), (t, 1.0)):
        rad = (pos[:, None] / ts).astype(np.float32)
        out += [np.cos(rad).T[p % 16] * sc, np.sin(rad).T[p % 16] * sgn * sc]
    c["rope3"] = np.stack(out, 1).astype(np.float32)
    return c


def host_layout(a):
    w = {}
    cont = np.ascontiguousarray
    w["x"], w["ctx"], w["mask"] = a["x"], a["ctx_1024"], a["mask_BxSxS2_if1"]
    w["key_pad"] = a["mask_BxS2_bk0"]
    for n in ("Wq", "Wk", "Wv", "Wb", "Wo"):
        w["d_" + n] = a["L0_attn_" + n]
    w["d_Wb_wide"] = cont(np.repeat(a["L0_attn_Wb"], DELTA_D, axis=1))
    for n in ("conv_q_w", "conv_k_w", "conv_v_w", "local_w", "mid_w", "r_w1"):
        w["d_" + n] = a["L0_attn_" + n]
    w["d_r_b1"] = a["L0_attn_r_b1"][:, None]
    w["d_r_w2"] = a["L0_attn_r_w2"]
    w["d_r_b2"] = a["L0_attn_r_b2"][None, :]
    w["d_mix_w"] = cont(np.broadcast_to(a["L0_attn_mix_w"].reshape(1, D), (128, D)))
    w["d_onorm_w"] = cont(np.broadcast_to(a["L0_attn_onorm_w"][None, None, :], (128, DELTA_H, DELTA_D)).reshape(128, D))
    for n in ("Wq", "Wk", "Wv", "Wo"):
        w["x0_" + n] = cont(a["L0_xattn_" + n].T)
    w["f_gate"], w["f_up"], w["f_down"] = (cont(a["L0_ffn_w_" + n].T) for n in ("gate", "up", "down"))
    wa = cont(a["L1_attn_w_attn"].T)
    ba = a["L1_attn_b_attn"]
    for k, n in enumerate(("Wq", "Wk", "Wv")):
        w["a1_" + n] = cont(wa[:, k * D:(k + 1) * D])
    w["a1_bq"], w["a1_bk"], w["a1_bv"] = ba[:D, None], ba[D:2 * D, None], ba[None, 2 * D:]
    w["a1_Wo"], w["a1_bo"] = cont(a["L1_attn_w_proj"].T), a["L1_attn_b_proj"][None, :]
    w["m_W1"], w["m_W2"] = cont(a["L1_xattn_W"][:, :D].T), cont(a["L1_xattn_W"][:, D:].T)
    w["m_b"] = a["L1_xattn_b"][None, :]
    w["e1_Wg"] = a["L1_ffn_Wg"]
    w["e1_W1"] = cont(a["L1_ffn_W1"].transpose(1, 0, 2).reshape(D, E1 * H1))
    w["e1_W2"] = cont(a["L1_ffn_W2"].transpose(1, 0, 2).reshape(D, E1 * H1))
    w["e1_W3"] = a["L1_ffn_W3"].reshape(E1 * H1, D)
    w["e1_Ws1"], w["e1_Ws2"], w["e1_Ws3"] = (a["L1_ffn_Ws%d" % k] for k in (1, 2, 3))
    wq = cont(a["L2_attn_W_qkv"].T)
    swap = np.arange(D) ^ 1
    w["a2_Wq"], w["a2_Wk"], w["a2_Wv"] = (cont(wq[:, k * D:(k + 1) * D]) for k in range(3))
    w["a2_Wq_swap"], w["a2_Wk_swap"] = cont(w["a2_Wq"][:, swap]), cont(w["a2_Wk"][:, swap])
    w["a2_Wo"] = cont(a["L2_attn_W_out"].T)
    for n in ("Wq", "Wk", "Wv", "Wo"):
        w["x2_" + n] = a["L2_xattn_" + n]
    w["x2_bq"], w["x2_bk"] = a["L2_xattn_bq"][:, None], a["L2_xattn_bk"][:, None]
    w["x2_bv"], w["x2_bo"] = a["L2_xattn_bv"][None, :], a["L2_xattn_bo"][None, :]
    w["e2_Wr"] = a["L2_ffn_router_w"]
    w["e2_w1"] = cont(a["L2_ffn_w1"].transpose(1, 0, 2).reshape(D, E2 * F2))
    w["e2_b1"] = cont(a["L2_ffn_b1"].reshape(E2 * F2 // 128, 128).T)
    w["e2_w2"] = a["L2_ffn_w2"].reshape(E2 * F2, D)
    w["e2_b2"] = a["L2_ffn_b2"]
    w["s_in"] = cont(a["L3_attn_in_proj_w"].T)
    w["s_conv_w"] = cont(a["L3_attn_conv_w"].reshape(2, 128, 4).transpose(1, 0, 2))
    w["s_conv_b"] = cont(a["L3_attn_conv_b"].reshape(2, 128).T)
    xw = a["L3_attn_x_proj_w"].reshape(4, 3, DS, 64)
    dtw = a["L3_attn_dt_proj_w"].reshape(4, 64, DS)
    w_x = np.zeros((128, 2, 2, DS), np.float32)
    w_bc = np.zeros((128, 2, 2, 3, 2, DS), np.float32)
    w_dt = np.zeros((2 * DS, 2, 128), np.float32)
    for c in range(2):
        for h in range(2):
            w_x[64 * h:64 * h + 64, c, h, :] = xw[2 * c + h, 0].T
            w_bc[64 * h:64 * h + 64, :, c, :, h, :] = xw[2 * c + h, 1:].transpose(2, 0, 1)[:, :, None, :]
            w_dt[DS * h:DS * h + DS, c, 64 * h:64 * h + 64] = dtw[2 * c + h].T
    w["s_x"], w["s_dt"] = w_x.reshape(128, 4 * DS), w_dt.reshape(2 * DS, 256)
    w["s_bc"] = w_bc.reshape(128, 24 * DS)
    w["s_dt_b"] = cont(a["L3_attn_dt_proj_b"].reshape(2, 128).T)
    w["s_A_log"] = cont(a["L3_attn_A_log"].reshape(2, 128, DS).transpose(1, 0, 2))
    w["s_D"] = cont(a["L3_attn_Dskip"].reshape(2, 128).T)
    w["s_out"] = cont(a["L3_attn_out_proj_w"].T)
    w["x3_scale"] = a["L3_xattn_rms_scale"][:, None]
    qw = cont(a["L3_xattn_q_w"].transpose(1, 0, 2).reshape(D, 128))
    half = np.arange(128) ^ 16
    w["x3_Wq"], w["x3_Wq_swap"] = qw, cont(qw[:, half])
    kw = cont(np.tile(a["L3_xattn_kv_w"][0, 0], (1, 4)))
    w["x3_Wk"], w["x3_Wk_swap"] = kw, cont(kw[:, half])
    w["x3_Wv"] = a["L3_xattn_kv_w"][1, 0]
    w["x3_Wo"] = a["L3_xattn_out_w"].reshape(128, D)
    w["e3_Wr"] = a["L3_ffn_Wr"]
    w["e3_W1"] = cont(a["L3_ffn_W1"].transpose(1, 0, 2).reshape(D, E3 * F3))
    w["e3_W2"] = a["L3_ffn_W2"].reshape(E3 * F3, D)
    return {k: cont(v) for k, v in w.items()}


ROWS = {"d_r_w2": RCH, "e1_Ws3": SCH}
CHUNKED = {"e1_W3": C1, "s_out": 2}
STREAMED = ("x", "ctx", "mask", "key_pad", "e2_w1", "e2_w2", "e3_W1", "e3_W2")
ROUNDED = ("sel_state", "sel_part")
INTEGER = ("f_gate", "f_up", "f_down")


class Psum:

    def __init__(self, banks, filled, emptied):
        self.banks, self.filled, self.emptied = banks, filled, emptied
        self.place, self.turns, self.next = {}, [0] * 8, 0

    def open(self, pe, name, bank=None):
        if bank is None:
            bank = self.next
            self.next = (self.next + 1) % 7
        turn = self.turns[bank]
        self.turns[bank] += 1
        assert name not in self.place, name
        self.place[name] = (bank, turn)
        if turn:
            pe.wait_ge(self.emptied[bank], turn)
        return self.banks[:, bank, :]

    def bank(self, name):
        return self.banks[:, self.place[name][0], :]

    def close(self, ins, name):
        ins.then_inc(self.filled[self.place[name][0]], 1)

    def take(self, eng, name):
        bank, turn = self.place[name]
        eng.wait_ge(self.filled[bank], turn + 1)
        return self.banks[:, bank, :]

    def give(self, ins, name):
        ins.then_inc(self.emptied[self.place[name][0]], 1)

    def wait_given(self, eng, name):
        bank, turn = self.place[name]
        eng.wait_ge(self.emptied[bank], turn + 1)


class Order:

    def __init__(self, eng, sem):
        self.eng, self.sem, self.count = eng, sem, 0

    def mark(self, ins):
        self.count += 1
        ins.then_inc(self.sem, 1)
        return self.count

    def wait(self, count):
        self.eng.wait_ge(self.sem, count)

    def link(self, ins):
        self.wait(self.mark(ins))


class Scratch:

    def __init__(self, tensor):
        self.tensor, self.at = tensor, 0

    def take(self, words, dtype=F32):
        size = words if dtype == F32 else (words + 1) // 2
        ap = self.tensor[:, self.at:self.at + size]
        self.at += size
        assert self.at <= SCRATCH, self.at
        return ap if dtype == F32 else ap.bitcast(dtype)


def row_tiles(ap):
    return ap.rearrange("p (s f) -> p s f", s=G)


def spread(ap, count, axis=1):
    ap = ap.unsqueeze(axis)
    shape = list(ap.shape)
    shape[axis] = count
    return ap.broadcast_to(shape)


def build(nc, dram, out):
    with ExitStack() as st:
        def sb(name, shape, dt=F32):
            return st.enter_context(nc.sbuf_tensor(name, shape, dt))

        def sem(name):
            return st.enter_context(nc.semaphore(name))

        W = {}
        plain, chunk_loads = [], []
        experts = sb("experts", [128, 2 * E3 * F3])
        scratch = sb("scratch", [128, SCRATCH])
        for k, name in enumerate(INTEGER):
            W[name] = scratch[:, k * FFH:(k + 1) * FFH].bitcast(I32)
            if name == "f_down":
                W[name] = W[name].rearrange("p (c f) -> p c f", c=3)
                plain.append((W[name], dram[name].rearrange("(c p) f -> p c f", p=128)))
            else:
                plain.append((W[name], dram[name]))
        at = 3 * FFH
        for name in ROUNDED:
            shape = list(dram[name].shape)
            words = int(np.prod(shape[1:]))
            W[name] = scratch[0:shape[0], at:at + words]
            at += words
            flat = dram[name] if len(shape) == 2 else dram[name].rearrange("p a b -> p (a b)")
            plain.append((W[name], flat))
        sel_state, sel_part = sb("sel_state_bf", [96, DS, 128], BF16), sb("sel_part_bf", [128, NH], BF16)
        for name, t in dram.items():
            if name in STREAMED or name in INTEGER or name in ROUNDED:
                continue
            shape, dt = list(t.shape), F32
            if name in CHUNKED:
                n = CHUNKED[name]
                W[name] = sb("w_" + name, [128, n, shape[1]], dt)
                plain.append((W[name][:], t.rearrange("(c p) f -> p c f", p=128)))
            elif name in ROWS:
                W[name] = sb("w_" + name, [128, len(ROWS[name]), shape[1]], dt)
                for c, (r0, rows) in enumerate(ROWS[name]):
                    plain.append((W[name][0:rows, c, :], t[r0:r0 + rows, :]))
            elif name == "d_r_w1":
                W["d_r_w1a"] = sb("w_d_r_w1a", [128, RH])
                W["d_r_w1b"] = sb("w_d_r_w1b", [NFEAT, RH])
                plain += [(W["d_r_w1a"][:], t[0:D, :]), (W["d_r_w1b"][:], t[D:D + NFEAT, :])]
            elif name == "d_r_b1":
                W[name] = sb("w_d_r_b1", [128, 3, 1])
                for c, (r0, rows) in enumerate(RCH):
                    plain.append((W[name][0:rows, c, :], t[r0:r0 + rows, :]))
            else:
                W[name] = sb("w_" + name, shape, dt)
                plain.append((W[name][:], t))
        ident = W["ident"]
        fw = {n: sb("fw_" + n, [128, FFH] if n != "down" else [128, 3, D]) for n in ("gate", "up", "down")}
        ident_bf, ident_big, ident_small = (sb(n, [128, 128], BF16) for n in ("ident_bf", "ident_big", "ident_small"))
        causal_bf, causal_T_bf = sb("causal_bf", [128, 128], BF16), sb("causal_T_bf", [128, 128], BF16)
        ones_row = sb("ones_row", [1, 128])
        ones_sq = sb("ones_sq", [128, 128])
        ones_col = sb("ones_col", [128, 1])
        eps5, eps6, eps12 = sb("eps5", [128, 1]), sb("eps6", [128, 1]), sb("eps12", [128, 1])
        ssm_A = sb("ssm_A", [128, 2, DS])
        counts = sb("counts", [128, E3])
        scale3 = sb("scale3", [128, 1])

        xres = sb("xres", [128, G, D])
        ctx_tok = sb("ctx_tok", [128, G, D])
        ctxT = sb("ctxT", [128, N])
        ctxnT = sb("ctxnT", [128, N])
        ctx_sum = sb("ctx_sum", [128, G])
        mask_i = sb("mask_i", [128, G, L], I32)
        mask_f = sb("mask_f", [128, G, L])
        mask_bf, maskT_bf = sb("mask_bf", [128, G, L], BF16), sb("maskT_bf", [128, G, L], BF16)
        pad_row_u8 = sb("pad_row_u8", [1, N], U8)
        pad_row = sb("pad_row", [1, N])
        pad_col = sb("pad_col", [128, G])
        pad_wide = sb("pad_wide", [128, N])
        ones_first = sb("ones_first", [128, 128])
        hn = sb("hn", [128, G, D])
        hT = sb("hT", [128, N])
        stats, mv = sb("stats", [128, G, 6]), sb("mv", [128, G, 2])
        std, rstd, rms, rms2 = (sb(n, [128, G]) for n in ("std", "rstd", "rms", "rms2"))
        banks = st.enter_context(nc.psum_tensor("banks", [128, 8, 512], F32))

        s_weights, s_in, s_out, s_setup = sem("weights_loaded"), sem("group_loaded"), sem("group_stored"), sem("setup")
        s_ctx, s_e2, s_e3 = sem("context_loaded"), sem("experts2_loaded"), sem("experts3_loaded")
        filled = [sem(f"bank{b}_filled") for b in range(8)]
        emptied = [sem(f"bank{b}_emptied") for b in range(8)]
        s_dve, s_act, s_pool = sem("dve_steps"), sem("act_steps"), sem("pool_steps")
        events = {}

        def ev(name):
            if name not in events:
                events[name] = sem(name)
            return events[name]

        P = Psum(banks, filled, emptied)
        s_stored, s_stack = [sem(f"parts{k}_stored") for k in (1, 2, 3)], sem("parts_stacked")
        stack_d = [nc.dram_tensor(f"stack_{k}", (3, 128, N), BF16, kind="Internal").ap() for k in "qk"]
        stacks = {}
        ACC = 7

        def col(s):
            return slice(s * L, (s + 1) * L)

        with nc.Block(no_gpsimd_drain=True) as block:
            queues = [plain[k::2] for k in range(2)]

            @block.sync
            def _(sp):
                for dst, src in queues[0]:
                    sp.dma_start(dst, src).then_inc(s_weights, 16)

            @block.scalar
            def _(act):
                for dst, src in queues[1]:
                    act.dma_start(dst, src).then_inc(s_weights, 16)
                act.wait_ge(s_weights, 16 * len(plain))
                act.activation(ssm_A[:], W["s_A_log"][:], ACT.Exp).then_inc(s_act, 1)

            @block.gpsimd
            def _(pool):
                pool.memset(ones_row[:], 1.0)
                pool.memset(ones_sq[:], 1.0)
                pool.memset(pad_wide[:], 0.0)
                pool.memset(ones_first[:], 0.0).then_inc(s_pool, 1)
                pool.wait_ge(s_pool, 1)
                pool.memset(ones_first[0:1, :], 1.0)
                pool.memset(ones_col[:], 1.0)
                pool.memset(eps5[:], 1e-5)
                pool.memset(eps6[:], 1e-6)
                pool.memset(eps12[:], 1e-12)
                pool.memset(counts[:], 0.0).then_inc(s_setup, 1)

            @block.vector
            def _(dve):
                dve.wait_ge(s_weights, 16 * len(plain))
                for n in ("gate", "up", "down"):
                    dve.tensor_scalar(fw[n][:], W["f_" + n], float(np.float32(1.0 / 127.0)), None, ALU.mult)
                dve.tensor_copy(sel_state[:].rearrange("p a b -> p (a b)"), W["sel_state"])
                dve.tensor_copy(sel_part[:], W["sel_part"])
                dve.tensor_copy(ident_bf[:], ident[:])
                dve.tensor_scalar(ident_big[:], ident[:], MASK_BIG, None, ALU.mult)
                dve.tensor_scalar(ident_small[:], ident[:], MASK_SMALL, None, ALU.mult)
                dve.tensor_copy(causal_bf[:], W["causal"][:])
                dve.tensor_copy(causal_T_bf[:], W["causal_T"][:])
                dve.tensor_scalar(scale3[:], W["x3_scale"][:], 1.0, None, ALU.add).then_inc(s_dve, 1)
                dve.wait_ge(s_dve, 1)
                for n in ("Wq", "Wq_swap", "Wk", "Wk_swap", "Wv"):
                    w = W["x3_" + n]
                    dve.tensor_scalar(w[:], w[:], scale3[:], None, ALU.mult)
                dve.wait_ge(s_act, 1)
                dve.tensor_scalar(ssm_A[:], ssm_A[:], -1.0, None, ALU.mult).then_inc(s_setup, 1)
                dve.wait_ge(s_setup, 2)

        nc.sync.sem_clear(s_pool)
        nc.sync.sem_clear(s_dve)
        nc.sync.sem_clear(s_act)
        nc.all_engine_barrier()

        def norm_pe(pe, nm):
            t = P.open(pe, nm + ".hT")
            for s in range(G):
                pe.wait_ge(ev(nm + ".hn"), s + 1)
                last = pe.transpose(t[:, col(s)], hn[:, s, :], ident[:])
            P.close(last, nm + ".hT")

        def norm_act(act, nm, rms_too=False):
            act.wait_ge(ev(nm + ".var"), 1)
            act.activation(std[:], mv[:, :, 1], ACT.Sqrt, bias=eps5[:]).then_inc(ev(nm + ".std"), 1)
            if rms_too:
                act.wait_ge(ev(nm + ".ms"), 1)
                act.activation(rms2[:], rms[:], ACT.Sqrt, bias=eps6[:]).then_inc(ev(nm + ".rms"), 1)
            t = P.take(act, nm + ".hT")
            P.give(act.copy(hT[:], t), nm + ".hT")

        def norm_dve(dve, q, nm, rms_too=False):
            for s in range(G):
                m = q.mark(dve.bn_stats(stats[:, s, :], xres[:, s, :]))
            for s in range(G):
                q.wait(m - 3 + s)
                ins = dve.bn_aggr(mv[:, s, :], stats[:, s, :])
                if s < G - 1:
                    m2 = q.mark(ins)
            ins.then_inc(ev(nm + ".var"), 1)
            dve.wait_ge(ev(nm + ".var"), 1)
            dve.wait_ge(ev(nm + ".std"), 1)
            q.link(dve.reciprocal(rstd[:], std[:]))
            if rms_too:
                q.link(dve.tensor_tensor(rms[:], mv[:, :, 1], rstd[:], ALU.mult))
                dve.tensor_tensor(rms[:], rms[:], rstd[:], ALU.mult).then_inc(ev(nm + ".ms"), 1)
                dve.wait_ge(ev(nm + ".rms"), 1)
                q.link(dve.reciprocal(rms[:], rms2[:]))
                q.link(dve.tensor_tensor(rstd[:], rstd[:], rms[:], ALU.mult))
            for s in range(G):
                dve.tensor_scalar(hn[:, s, :], xres[:, s, :], mv[:, s, 0:1], rstd[:, s:s + 1],
                                  ALU.subtract, ALU.mult).then_inc(ev(nm + ".hn"), 1)

        def residual_dve(dve, q, name):
            t = P.take(dve, name)
            P.give(dve.tensor_tensor(xres[:].rearrange("p s f -> p (s f)"), xres[:].rearrange("p s f -> p (s f)"), t,
                                     ALU.add), name)
            P.wait_given(dve, name)

        def bias_row(pe, t, row, start=True):
            w = row.shape[-1]
            pe.matmul(t[:, 0:G * w].rearrange("p (s f) -> p s f", s=G), ones_row[:],
                      spread(row, G), start=start, stop=False, skip_group_check=True)

        def ctx_pe(pe):
            pe.wait_ge(s_ctx, 48)
            t = P.open(pe, "ctx.T")
            for s in range(G):
                last = pe.transpose(t[:, col(s)], ctx_tok[:, s, :], ident[:])
            P.close(last, "ctx.T")
            t = P.open(pe, "ctx.maskT")
            pe.wait_ge(ev("mask.f"), 1)
            for s in range(G):
                last = pe.transpose(t[:, col(s)], mask_f[:, s, :], ident[:])
            P.close(last, "ctx.maskT")
            t = P.open(pe, "ctx.pad")
            pe.wait_ge(ev("mask.pad"), 1)
            for s in range(G):
                last = pe.matmul(t[:, s:s + 1], pad_row[:, col(s)], ones_row[:, 0:1], start=True, stop=True)
            P.close(last, "ctx.pad")
            t = P.open(pe, "ctx.nT")
            pe.wait_ge(ev("ctx.n"), 1)
            for s in range(G):
                last = pe.transpose(t[:, col(s)], scratch[:, col(s)], ident[:])
            P.close(last, "ctx.nT")

        def ctx_act(act):
            act.wait_ge(s_ctx, 48)
            for s in range(G):
                last = act.activation(scratch[:, N + s * L:N + (s + 1) * L], ctx_tok[:, s, :], ACT.Square,
                                      accum_out=rms[:, s:s + 1])
            last.then_inc(ev("ctx.sq"), 1)
            act.wait_ge(ev("ctx.sq"), 1)
            act.activation(rms2[:], rms[:], ACT.Sqrt, scale=1.0 / D, bias=eps6[:]).then_inc(ev("ctx.rms"), 1)
            t = P.take(act, "ctx.T")
            P.give(act.copy(ctxT[:], t), "ctx.T")
            t = P.take(act, "ctx.maskT")
            P.give(act.copy(maskT_bf[:].rearrange("p s f -> p (s f)"), t), "ctx.maskT")
            t = P.take(act, "ctx.pad")
            P.give(act.copy(pad_col[:], t[:, 0:G]), "ctx.pad")
            t = P.take(act, "ctx.nT")
            P.give(act.copy(ctxnT[:], t), "ctx.nT")

        def ctx_dve(dve, q):
            dve.wait_ge(s_ctx, 48)
            dve.tensor_scalar(mask_f[:], mask_i[:], -1.0, None, ALU.add).then_inc(ev("mask.f"), 1)
            dve.tensor_scalar(pad_row[:], pad_row_u8[:], -1.0, BIG, ALU.add, ALU.mult).then_inc(ev("mask.pad"), 1)
            dve.wait_ge(ev("mask.f"), 1)
            q.link(dve.tensor_copy(mask_bf[:], mask_f[:]))
            dve.wait_ge(ev("mask.pad"), 1)
            q.link(dve.tensor_copy(pad_wide[0:1, :], pad_row[:]))
            dve.wait_ge(ev("ctx.rms"), 1)
            q.link(dve.reciprocal(rstd[:], rms2[:]))
            for s in range(G):
                last = dve.tensor_scalar(scratch[:, col(s)], ctx_tok[:, s, :], rstd[:, s:s + 1], None, ALU.mult)
            last.then_inc(ev("ctx.n"), 1)
            P.wait_given(dve, "ctx.T")
            q.link(dve.reduce_sum(ctx_sum[:], row_tiles(ctxT[:]), X))
            P.wait_given(dve, "ctx.nT")

        def attention16(nm, w, src=None, bias=False, bias_out=False, rope=False, mask=None):
            S = Scratch(scratch)
            qk = [S.take(N) for _ in range(2)]
            rest = [S.take(N) for _ in range(2)]
            parts = [S.take(3 * N, BF16).rearrange("p (k t) -> p k t", k=3) for _ in range(2)]
            stack = [S.take(NH // 2 * N, BF16).rearrange("p (a t) -> p a t", t=N) for _ in range(2)]
            pT = S.take(2 * NH * L).rearrange("p (b j f) -> p b j f", b=2, j=NJ)
            vaug = S.take(G * NH * (DH + 1)).rearrange("p (s h e) -> p s h e", s=G, h=NH)
            negm, mrest = (S.take(G * NH).rearrange("p (s h) -> p s h", s=G) for _ in range(2))
            mparts = S.take(N, BF16).rearrange("p (s f) -> p s f", s=G)
            mT = S.take(N, BF16)
            rden = S.take(G * NH).rearrange("p (s h) -> p s h", s=G)
            osb = S.take(N)
            oT = S.take(N)
            rq = [S.take(N) for _ in range(4)] if rope else None
            src_ap = ctxT if src == "ctx" else hT

            def head_of(j, i):
                return 8 * (j // 2) + 2 * i + j % 2

            def masking(pe, t, turned, s):
                v = row_tiles(t)
                last = None
                if mask == "causal":
                    last = pe.matmul(v, ident_bf[:], spread((causal_T_bf if turned else causal_bf)[:], NI),
                                     start=False, stop=not turned, skip_group_check=True)
                if mask == "given":
                    for c in (ident_big, ident_small):
                        last = pe.matmul(v, c[:], spread((maskT_bf if turned else mask_bf)[:, s, :], NI), start=False,
                                         stop=c is ident_small and not turned, skip_group_check=True)
                return last

            def pe_f(pe):
                norm_pe(pe, nm)
                P.wait_given(pe, nm + ".hT")
                todo = [("q", "Wq", hT), ("k", "Wk", src_ap)]
                if rope:
                    todo = [("q", "Wq", hT), ("qs", "Wq_swap", hT), ("k", "Wk", hT), ("ks", "Wk_swap", hT)]
                for name, wn, s_ in todo:
                    t = P.open(pe, f"{nm}.{name}")
                    P.close(pe.matmul(t, W[w + wn][:], s_[:], start=True, stop=True), f"{nm}.{name}")
                t = P.open(pe, nm + ".v")
                if bias:
                    bias_row(pe, t, W[w + "bv"][:])
                for s in range(G):
                    last = pe.matmul(t[:, col(s)], src_ap[:, col(s)], W[w + "Wv"][:], start=not bias, stop=True,
                                     skip_group_check=True)
                P.close(last, nm + ".v")

                def products(s, letter, lhs, rhs, close):
                    for jj in range(0, NJ, 2):
                        t = [P.open(pe, f"{nm}.{letter}{s}{jj + par}") for par in range(2)]
                        for i in range(NI):
                            for par in range(2):
                                h = head_of(jj + par, i)
                                r = slice(64 * par, 64 * par + 48)
                                last = pe.matmul(t[par][:, i * L:(i + 1) * L], lhs[r, h // 2, col(s)],
                                                 rhs[r, h // 2, col(s)], start=i == 0, stop=close,
                                                 skip_group_check=True)
                                if close and i == NI - 1:
                                    P.close(last, f"{nm}.{letter}{s}{jj + par}")

                def scores(s):
                    if s == 0:
                        pe.wait_ge(s_stack, 16 * 4 * len(SLOTS) * stacks[nm])
                    products(s, "S", stack[0], stack[1], mask is None)
                    if mask:
                        for j in range(NJ):
                            P.close(masking(pe, P.bank(f"{nm}.S{s}{j}"), False, s), f"{nm}.S{s}{j}")

                def turned(s):
                    products(s, "T", stack[1], stack[0], False)
                    pe.wait_ge(ev(nm + ".mparts"), s + 1)
                    t = P.open(pe, f"{nm}.mT{s}")
                    P.close(pe.transpose(t.bitcast(BF16)[:, 0:L], mparts[:, s, :], ident_bf[:]), f"{nm}.mT{s}")
                    for j in range(NJ):
                        masking(pe, P.bank(f"{nm}.T{s}{j}"), True, s)
                    P.wait_given(pe, f"{nm}.mT{s}")
                    for j in range(NJ):
                        t = P.bank(f"{nm}.T{s}{j}")
                        for i in range(NI):
                            a = NI * j + i
                            last = pe.matmul(t[:, i * L:(i + 1) * L], sel_part[:, a:a + 1].broadcast_to([128, 128]),
                                             mT[:, col(s)], start=False, stop=i == NI - 1, skip_group_check=True)
                        P.close(last, f"{nm}.T{s}{j}")

                def values(s):
                    if s == 0:
                        P.wait_given(pe, nm + ".v")
                        pe.wait_ge(ev(nm + ".ones"), 1)
                    t = P.open(pe, f"{nm}.O{s}")
                    for j in range(NJ):
                        P.wait_given(pe, f"{nm}.T{s}{j}")
                        for i in range(NI):
                            h = head_of(j, i)
                            last = pe.matmul(t[:, h * 9:h * 9 + 9], pT[:, s % 2, j, i * L:(i + 1) * L],
                                             vaug[:, s, h, :], start=True, stop=True, skip_group_check=True)
                    P.close(last, f"{nm}.O{s}")

                for step in range(G + 2):
                    if step < G:
                        scores(step)
                    if step >= 2:
                        values(step - 2)
                    if 1 <= step <= G:
                        turned(step - 1)
                t = P.open(pe, nm + ".oT")
                for s in range(G):
                    P.wait_given(pe, f"{nm}.O{s}")
                    last = pe.transpose(t[:, col(s)], osb[:, col(s)], ident[:])
                P.close(last, nm + ".oT")
                P.wait_given(pe, nm + ".oT")
                t = P.open(pe, nm + ".y", ACC)
                if bias_out:
                    bias_row(pe, t, W[w + "bo"][:])
                for s in range(G):
                    last = pe.matmul(t[:, col(s)], oT[:, col(s)], W[w + "Wo"][:], start=not bias_out, stop=True,
                                     skip_group_check=True)
                P.close(last, nm + ".y")

            def act_f(act, q):
                norm_act(act, nm)
                if not rope:
                    t = P.take(act, nm + ".q")
                    bq = W[w + "bq"][:] if bias else 0.0
                    P.give(act.activation(qk[0], t, ACT.Identity, bias=bq), nm + ".q")
                for k in range(2):
                    if rope:
                        act.wait_ge(ev(nm + ".sum"), k + 1)
                    else:
                        P.wait_given(act, f"{nm}.{'qk'[k]}")
                    act.copy(parts[k][:, 0, :], qk[k]).then_inc(ev(nm + ".part1"), 1)
                for k in range(2):
                    act.wait_ge(ev(nm + ".rest"), k + 1)
                    act.copy(parts[k][:, 1, :], rest[k]).then_inc(ev(nm + ".part2"), 1)
                t = P.take(act, nm + ".v")
                P.give(act.copy(vaug[:, :, :, 0:DH], t.rearrange("p (s h e) -> p s h e", s=G, h=NH)), nm + ".v")
                for s in range(G):
                    t = P.take(act, f"{nm}.mT{s}")
                    P.give(act.copy(mT[:, col(s)], t.bitcast(BF16)[:, 0:L]), f"{nm}.mT{s}")
                    if s >= 2:
                        P.take(act, f"{nm}.O{s - 2}")
                    for j in range(NJ):
                        t = P.take(act, f"{nm}.T{s}{j}")
                        P.give(act.activation(pT[:, s % 2, j, :], t, ACT.Exp), f"{nm}.T{s}{j}")
                t = P.take(act, nm + ".oT")
                P.give(act.copy(oT, t), nm + ".oT")

            def dve_f(dve, q):
                norm_dve(dve, q, nm)
                if rope:
                    for k, name in enumerate(("q", "qs", "k", "ks")):
                        t = P.take(dve, f"{nm}.{name}")
                        P.give(dve.tensor_tensor(row_tiles(rq[k]), row_tiles(t), spread(W["rope2"][:, k, :], G),
                                                 ALU.mult), f"{nm}.{name}")
                        if k % 2:
                            P.wait_given(dve, f"{nm}.{name}")
                            dve.tensor_tensor(qk[k // 2], rq[k - 1], rq[k], ALU.add).then_inc(ev(nm + ".sum"), 1)
                else:
                    t = P.take(dve, nm + ".k")
                    if bias:
                        ins = dve.tensor_scalar(qk[1], t, W[w + "bk"][:], SCALE16, ALU.add, ALU.mult)
                    else:
                        ins = dve.tensor_scalar(qk[1], t, SCALE16, None, ALU.mult)
                    P.give(ins, nm + ".k")
                for k in range(2):
                    dve.wait_ge(ev(nm + ".part1"), k + 1)
                    dve.tensor_tensor(rest[k], qk[k], parts[k][:, 0, :], ALU.subtract).then_inc(ev(nm + ".rest"), 1)
                for k in range(2):
                    dve.wait_ge(ev(nm + ".part2"), k + 1)
                    dve.tensor_tensor(parts[k][:, 2, :], rest[k], parts[k][:, 1, :],
                                      ALU.subtract).then_inc(ev(nm + ".part3"), 1)
                dve.wait_ge(ev(nm + ".ones"), 2)

                def maxima(s):
                    for j in range(NJ):
                        t = P.take(dve, f"{nm}.S{s}{j}")
                        P.give(dve.tensor_reduce(negm[:, s, NI * j:NI * j + NI], row_tiles(t), X, ALU.max,
                                                 negate=True), f"{nm}.S{s}{j}")
                    P.wait_given(dve, f"{nm}.S{s}{NJ - 1}")
                    m, r = negm[:, s, :], mrest[:, s, :]
                    q.link(dve.tensor_copy(mparts[:, s, 0:NH], m))
                    q.link(dve.tensor_tensor(r, m, mparts[:, s, 0:NH], ALU.subtract))
                    q.link(dve.tensor_copy(mparts[:, s, 32:32 + NH], r))
                    dve.tensor_tensor(mparts[:, s, 64:64 + NH], r, mparts[:, s, 32:32 + NH],
                                      ALU.subtract).then_inc(ev(nm + ".mparts"), 1)

                def divide(s):
                    t = P.take(dve, f"{nm}.O{s}")[:, 0:NH * 9].rearrange("p (h e) -> p h e", h=NH)
                    q.link(dve.reciprocal(rden[:, s, :], t[:, :, DH]))
                    P.give(dve.tensor_tensor(osb[:, col(s)].rearrange("p (h e) -> p h e", h=NH), t[:, :, 0:DH],
                                             spread(rden[:, s, :], DH, 2), ALU.mult), f"{nm}.O{s}")

                for step in range(G + 2):
                    if step < G:
                        maxima(step)
                    if step >= 2:
                        divide(step - 2)
                residual_dve(dve, q, nm + ".y")

            def pool_f(pool, q):
                pool.wait_ge(ev(nm + ".hn"), 1)
                pool.memset(vaug[:, :, :, DH:DH + 1], 1.0).then_inc(ev(nm + ".ones"), 1)
                pool.memset(mparts, 0.0).then_inc(ev(nm + ".ones"), 1)

            def sp_f(sp):
                for part in range(3):
                    for k in range(2):
                        sp.wait_ge(ev(nm + (".part1", ".part2", ".part3")[part]), k + 1)
                        sp.dma_start(stack_d[k][part], parts[k][:, part, :]).then_inc(s_stored[part], 16)
                for part in range(3):
                    sp.wait_ge(s_stored[part], 32 * turn)
                    for slot, of in enumerate(SLOTS):
                        for k in range(2):
                            if of[k] != part:
                                continue
                            for par in range(2):
                                r = 64 * par + 8 * slot
                                sp.dma_start(stack[k][r:r + DH], stack_d[k][part].rearrange(
                                    "(a b r) t -> b r a t", b=2, r=DH)[par]).then_inc(s_stack, 16)

            stacks[nm] = turn = len(stacks) + 1
            return pe_f, act_f, dve_f, pool_f, sp_f

        def nothing(*_):
            pass

        def ffn(nm):
            S = Scratch(scratch)
            nch = FFH // 128
            act_out = S.take(nch * N).rearrange("p (c t) -> p c t", c=nch)
            hid = S.take(nch * N).rearrange("p (c t) -> p c t", c=nch)

            def pe_f(pe):
                norm_pe(pe, nm)
                P.wait_given(pe, nm + ".hT")
                for c in range(nch):
                    for k in ("gate", "up"):
                        t = P.open(pe, f"{nm}.{k}{c}")
                        P.close(pe.matmul(t, fw[k][:, c * 128:(c + 1) * 128], hT[:], start=True, stop=True),
                                f"{nm}.{k}{c}")
                for c in range(nch):
                    P.wait_given(pe, f"{nm}.up{c}")
                t = P.open(pe, nm + ".y", ACC)
                for s in range(G):
                    for c in range(nch):
                        last = pe.matmul(t[:, col(s)], hid[:, c, col(s)], fw["down"][:, c, :], start=c == 0,
                                         stop=c == nch - 1, skip_group_check=True)
                P.close(last, nm + ".y")

            def act_f(act, q):
                norm_act(act, nm)
                for c in range(nch):
                    t = P.take(act, f"{nm}.gate{c}")
                    P.give(act.activation(act_out[:, c, :], t, ACT.Silu), f"{nm}.gate{c}")

            def dve_f(dve, q):
                norm_dve(dve, q, nm)
                for c in range(nch):
                    P.wait_given(dve, f"{nm}.gate{c}")
                    t = P.take(dve, f"{nm}.up{c}")
                    P.give(dve.tensor_tensor(hid[:, c, :], act_out[:, c, :], t, ALU.mult), f"{nm}.up{c}")
                residual_dve(dve, q, nm + ".y")

            return pe_f, act_f, dve_f, nothing

        def mixer(nm):
            S = Scratch(scratch)
            mean_wide = S.take(N)

            def pe_f(pe):
                norm_pe(pe, nm)
                P.wait_given(pe, nm + ".hT")
                t = P.open(pe, nm + ".y", ACC)
                bias_row(pe, t, W["m_b"][:])
                pe.wait_ge(ev(nm + ".mean"), 1)
                for s in range(G):
                    pe.matmul(t[:, col(s)], hT[:, col(s)], W["m_W1"][:], start=False, stop=False,
                              skip_group_check=True)
                    last = pe.matmul(t[:, col(s)], mean_wide[:, col(s)], W["m_W2"][:], start=False, stop=True,
                                     skip_group_check=True)
                P.close(last, nm + ".y")

            def act_f(act, q):
                norm_act(act, nm)

            def dve_f(dve, q):
                norm_dve(dve, q, nm)
                dve.tensor_scalar(row_tiles(mean_wide), spread(ctx_sum[:], L, 2), 1.0 / L, None,
                                  ALU.mult).then_inc(ev(nm + ".mean"), 1)
                residual_dve(dve, q, nm + ".y")

            return pe_f, act_f, dve_f, nothing

        def first_max(dve, q, onehot, values, top, tmp, width):
            q.link(dve.tensor_reduce(top, values, X, ALU.max))
            q.link(dve.tensor_tensor(tmp, values, spread(top, width, 2), ALU.is_ge))
            q.link(dve.tensor_tensor(tmp, tmp, spread(W["rev"][:, 0:width], G), ALU.mult))
            q.link(dve.tensor_reduce(rms[:], tmp, X, ALU.max))
            q.link(dve.tensor_tensor(onehot, tmp, spread(rms[:], width, 2), ALU.is_equal))

        def gates_pe(pe, nm, gate, width):
            pe.wait_ge(ev(nm + ".gate"), 1)
            t = P.open(pe, nm + ".gT")
            for s in range(G):
                last = pe.transpose(t[0:width, col(s)], gate[:, s, :], ident[:])
            P.close(last, nm + ".gT")

        def router_pe(pe, nm, w, width):
            t = P.open(pe, nm + ".router")
            for s in range(G):
                last = pe.matmul(t[:, s * width:(s + 1) * width], hT[:, col(s)], w, start=True, stop=True,
                                 skip_group_check=True)
            P.close(last, nm + ".router")

        def moe1(nm):
            S = Scratch(scratch)
            RING = 3
            lg, lg2, oh1, oh2, tmp, gate = (S.take(G * E1).rearrange("p (s e) -> p s e", s=G) for _ in range(6))
            top1, top2, p1, p2, ex = (S.take(G) for _ in range(5))
            gT = S.take(N)
            a_out = S.take(RING * N).rearrange("p (r t) -> p r t", r=RING)
            h_mid = S.take(RING * N).rearrange("p (r t) -> p r t", r=RING)
            hid = S.take(RING * N).rearrange("p (r t) -> p r t", r=RING)
            chunks = [(None, c, r0, rows) for c, (r0, rows) in enumerate(SCH)] + \
                     [("e", c, c * 128, 128) for c in range(C1)]

            def pe_f(pe):
                norm_pe(pe, nm)
                P.wait_given(pe, nm + ".hT")
                router_pe(pe, nm, W["e1_Wg"][:], E1)

                def up(n):
                    kind, c, r0, rows = chunks[n]
                    for k, (wa, wb) in enumerate((("e1_Ws1", "e1_W1"), ("e1_Ws2", "e1_W2"))):
                        t = P.open(pe, f"{nm}.u{k}{n}")
                        w = W[wb if kind else wa]
                        P.close(pe.matmul(t[0:rows, :], w[:, r0:r0 + rows], hT[:], start=True, stop=True),
                                f"{nm}.u{k}{n}")
                    if kind:
                        if c == 0:
                            gates_pe(pe, nm, gate, E1)
                            P.wait_given(pe, nm + ".gT")
                        t = P.open(pe, f"{nm}.g{n}")
                        P.close(pe.matmul(t, W["sel1"][:, r0:r0 + 128], gT[0:E1, :], start=True, stop=True),
                                f"{nm}.g{n}")

                def down(n):
                    kind, c, r0, rows = chunks[n]
                    P.wait_given(pe, f"{nm}.g{n}" if kind else f"{nm}.u1{n}")
                    w = W["e1_W3" if kind else "e1_Ws3"]
                    for s in range(G):
                        last = pe.matmul(acc[:, col(s)], hid[0:rows, n % RING, col(s)], w[0:rows, c, :],
                                         start=n == 0 and s == 0, stop=n == len(chunks) - 1, skip_group_check=True)
                    if n < len(chunks) - 1:
                        last.then_inc(ev(nm + ".down"), 1)
                    return last

                acc = P.open(pe, nm + ".y", ACC)
                for n in range(len(chunks) + 1):
                    if n < len(chunks):
                        up(n)
                    if n >= 1:
                        last = down(n - 1)
                P.close(last, nm + ".y")

            def act_f(act, q):
                norm_act(act, nm)
                act.wait_ge(ev(nm + ".diff"), 1)
                act.activation(ex, p1, ACT.Exp).then_inc(ev(nm + ".exp"), 1)
                for n, (kind, c, r0, rows) in enumerate(chunks):
                    t = P.take(act, f"{nm}.u0{n}")
                    if n >= RING:
                        P.wait_given(act, f"{nm}.u1{n - RING}")
                    P.give(act.activation(a_out[0:rows, n % RING, :], t[0:rows, :], ACT.Silu), f"{nm}.u0{n}")
                    if kind and c == 0:
                        t = P.take(act, nm + ".gT")
                        P.give(act.copy(gT[0:E1, :], t[0:E1, :]), nm + ".gT")

            def dve_f(dve, q):
                norm_dve(dve, q, nm)
                t = P.take(dve, nm + ".router")
                P.give(dve.tensor_copy(lg, t[:, 0:G * E1].rearrange("p (s e) -> p s e", s=G)), nm + ".router")
                P.wait_given(dve, nm + ".router")
                first_max(dve, q, oh1, lg, top1, tmp, E1)
                q.link(dve.scalar_tensor_tensor(out=lg2, in0=oh1, scalar=-BIG, in1=lg, op0=ALU.mult, op1=ALU.add))
                first_max(dve, q, oh2, lg2, top2, tmp, E1)
                dve.tensor_tensor(p1, top2, top1, ALU.subtract).then_inc(ev(nm + ".diff"), 1)
                dve.wait_ge(ev(nm + ".exp"), 1)
                q.link(dve.tensor_scalar(p1, ex, 1.0, None, ALU.add))
                q.link(dve.reciprocal(p1, p1))
                q.link(dve.tensor_tensor(p2, p1, ex, ALU.mult))
                q.link(dve.tensor_tensor(oh1, oh1, spread(p1, E1, 2), ALU.mult))
                q.link(dve.tensor_tensor(oh2, oh2, spread(p2, E1, 2), ALU.mult))
                dve.tensor_tensor(gate, oh1, oh2, ALU.add).then_inc(ev(nm + ".gate"), 1)
                for n, (kind, c, r0, rows) in enumerate(chunks):
                    P.wait_given(dve, f"{nm}.u0{n}")
                    t = P.take(dve, f"{nm}.u1{n}")
                    if n >= RING:
                        dve.wait_ge(ev(nm + ".down"), n - RING + 1)
                    dst = h_mid if kind else hid
                    P.give(dve.tensor_tensor(dst[0:rows, n % RING, :], a_out[0:rows, n % RING, :], t[0:rows, :],
                                             ALU.mult), f"{nm}.u1{n}")
                    if kind:
                        P.wait_given(dve, f"{nm}.u1{n}")
                        t = P.take(dve, f"{nm}.g{n}")
                        P.give(dve.tensor_tensor(hid[:, n % RING, :], h_mid[:, n % RING, :], t, ALU.mult),
                               f"{nm}.g{n}")
                residual_dve(dve, q, nm + ".y")

            return pe_f, act_f, dve_f, nothing

        def moe2(nm):
            S = Scratch(scratch)
            RING = 3
            lg, oh, tmp, gate = (S.take(G * E2).rearrange("p (s e) -> p s e", s=G) for _ in range(4))
            top, den = S.take(G), S.take(G)
            gT = S.take(N)
            hid = S.take(RING * 2 * N).rearrange("p (r c t) -> p r c t", r=RING, c=2)
            w1 = experts[:, 0:E2 * F2]
            w2 = experts[:, E2 * F2:2 * E2 * F2].rearrange("p (c f) -> p c f", f=D)

            def pe_f(pe):
                norm_pe(pe, nm)
                P.wait_given(pe, nm + ".hT")
                router_pe(pe, nm, W["e2_Wr"][:], E2)
                pe.wait_ge(s_e2, 32)

                def up(e):
                    for c in range(2):
                        t = P.open(pe, f"{nm}.u{e}.{c}")
                        f0 = e * F2 + c * 128
                        P.close(pe.matmul(t, w1[:, f0:f0 + 128], hT[:], start=True, stop=True), f"{nm}.u{e}.{c}")

                def down(e):
                    P.wait_given(pe, f"{nm}.u{e}.0")
                    P.wait_given(pe, f"{nm}.u{e}.1")
                    t = P.open(pe, f"{nm}.d{e}")
                    for s in range(G):
                        for c in range(2):
                            last = pe.matmul(t[:, col(s)], hid[:, e % RING, c, col(s)], w2[:, 2 * e + c, :],
                                             start=c == 0, stop=c == 1, skip_group_check=True)
                    P.close(last, f"{nm}.d{e}")

                for e in range(E2 + 1):
                    if e < E2:
                        up(e)
                    if e >= 1:
                        down(e - 1)
                gates_pe(pe, nm, gate, E2)
                P.wait_given(pe, nm + ".gT")
                t = P.open(pe, nm + ".y", ACC)
                for s in range(G):
                    last = pe.matmul(t[:, col(s)], gT[0:E2, col(s)], W["e2_b2"][:], start=True, stop=True,
                                     skip_group_check=True)
                P.close(last, nm + ".y")

            def act_f(act, q):
                norm_act(act, nm)
                act.wait_ge(ev(nm + ".diff"), 1)
                act.activation(lg, tmp, ACT.Exp).then_inc(ev(nm + ".exp"), 1)
                for e in range(E2):
                    for c in range(2):
                        t = P.take(act, f"{nm}.u{e}.{c}")
                        if e >= RING and c == 0:
                            P.take(act, f"{nm}.d{e - RING}")
                            P.take(act, f"{nm}.u{e}.{c}")
                        P.give(act.activation(hid[:, e % RING, c, :], t, ACT.Gelu,
                                              bias=W["e2_b1"][:, 2 * e + c:2 * e + c + 1]), f"{nm}.u{e}.{c}")
                t = P.take(act, nm + ".gT")
                P.give(act.copy(gT[0:E2, :], t[0:E2, :]), nm + ".gT")

            def dve_f(dve, q):
                norm_dve(dve, q, nm)
                t = P.take(dve, nm + ".router")
                P.give(dve.tensor_copy(lg, t[:, 0:G * E2].rearrange("p (s e) -> p s e", s=G)), nm + ".router")
                P.wait_given(dve, nm + ".router")
                first_max(dve, q, oh, lg, top, tmp, E2)
                dve.tensor_tensor(tmp, lg, spread(top, E2, 2), ALU.subtract).then_inc(ev(nm + ".diff"), 1)
                dve.wait_ge(ev(nm + ".exp"), 1)
                q.link(dve.tensor_reduce(den, lg, X, ALU.add))
                q.link(dve.reciprocal(den, den))
                dve.tensor_tensor(gate, oh, spread(den, E2, 2), ALU.mult).then_inc(ev(nm + ".gate"), 1)
                dve.wait_ge(ev(nm + ".gate"), 1)
                for e in range(E2):
                    t = P.take(dve, f"{nm}.d{e}")
                    for s in range(G):
                        ins = dve.scalar_tensor_tensor(out=xres[:, s, :], in0=t[:, col(s)],
                                                       scalar=gate[:, s, e:e + 1], in1=xres[:, s, :],
                                                       op0=ALU.mult, op1=ALU.add)
                    P.give(ins, f"{nm}.d{e}")
                    P.wait_given(dve, f"{nm}.d{e}")
                residual_dve(dve, q, nm + ".y")

            return pe_f, act_f, dve_f, nothing

        def moe3(nm):
            S = Scratch(scratch)
            XR, RING = 2, 4
            nch = F3 // 128
            lg, oh, tmp, gate, rank = (S.take(G * E3).rearrange("p (s e) -> p s e", s=G) for _ in range(5))
            top, den, mine = S.take(G), S.take(G), S.take(G)
            gT = S.take(N)
            xg = S.take(XR * N).rearrange("p (r t) -> p r t", r=XR)
            hid = S.take(RING * N).rearrange("p (r t) -> p r t", r=RING)
            w1 = experts[:, 0:E3 * F3]
            w2 = experts[:, E3 * F3:].rearrange("p (c f) -> p c f", f=D)
            nall = E3 * nch
            assert nch == RING

            def pe_f(pe):
                norm_pe(pe, nm)
                P.wait_given(pe, nm + ".hT")
                router_pe(pe, nm, W["e3_Wr"][:], E3)
                pe.wait_ge(ev(nm + ".diff"), 1)
                t = P.open(pe, nm + ".rank")
                for s in range(G):
                    for k in range(s):
                        pe.matmul(t[:, s * E3:(s + 1) * E3], ones_sq[:], oh[:, k, :], start=k == 0, stop=False,
                                  skip_group_check=True)
                    pe.matmul(t[:, s * E3:(s + 1) * E3], W["before_T"][:], oh[:, s, :], start=s == 0, stop=True,
                              skip_group_check=True)
                for k in range(G):
                    last = pe.matmul(t[:, G * E3:(G + 1) * E3], ones_sq[:], oh[:, k, :], start=k == 0,
                                     stop=k == G - 1, skip_group_check=True)
                P.close(last, nm + ".rank")
                gates_pe(pe, nm, gate, E3)
                P.wait_given(pe, nm + ".gT")
                pe.wait_ge(s_e3, 32)

                def feed(e):
                    t = P.open(pe, f"{nm}.g{e}")
                    P.close(pe.matmul(t, ident[0:E3, e:e + 1].broadcast_to([E3, 128]), gT[0:E3, :],
                                      start=True, stop=True), f"{nm}.g{e}")

                def up(n):
                    e = n // nch
                    if n % nch == 0:
                        P.wait_given(pe, f"{nm}.g{e}")
                    t = P.open(pe, f"{nm}.u{n}")
                    P.close(pe.matmul(t, w1[:, n * 128:(n + 1) * 128], xg[:, e % XR, :], start=True, stop=True),
                            f"{nm}.u{n}")

                def down(n):
                    P.wait_given(pe, f"{nm}.u{n}")
                    for s in range(G):
                        last = pe.matmul(acc[:, col(s)], hid[:, n % RING, col(s)], w2[:, n, :],
                                         start=n == 0 and s == 0, stop=n == nall - 1, skip_group_check=True)
                    if n < nall - 1:
                        last.then_inc(ev(nm + ".down"), 1)
                    return last

                acc = P.open(pe, nm + ".y", ACC)
                feed(0)
                for n in range(nall + 2):
                    if n < nall:
                        if n % nch == 1 and n // nch + 1 < E3:
                            feed(n // nch + 1)
                        up(n)
                    if n >= 2:
                        last = down(n - 2)
                P.close(last, nm + ".y")

            def act_f(act, q):
                norm_act(act, nm)
                act.wait_ge(ev(nm + ".diff"), 1)
                act.activation(lg, tmp, ACT.Exp).then_inc(ev(nm + ".exp"), 1)
                t = P.take(act, nm + ".gT")
                P.give(act.copy(gT[0:E3, :], t[0:E3, :]), nm + ".gT")
                for n in range(0, nall, 2):
                    relu_chunk(act, n)

            def relu_chunk(eng, n):
                if n >= RING:
                    eng.wait_ge(ev(nm + ".down"), n - RING + 1)
                t = P.take(eng, f"{nm}.u{n}")
                if n % 2 == 0:
                    ins = eng.activation(hid[:, n % RING, :], t, ACT.Relu)
                else:
                    ins = eng.tensor_scalar(hid[:, n % RING, :], t, 0.0, None, ALU.max)
                P.give(ins, f"{nm}.u{n}")

            def dve_f(dve, q):
                norm_dve(dve, q, nm)
                t = P.take(dve, nm + ".router")
                P.give(dve.tensor_copy(lg, t[:, 0:G * E3].rearrange("p (s e) -> p s e", s=G)), nm + ".router")
                P.wait_given(dve, nm + ".router")
                first_max(dve, q, oh, lg, top, tmp, E3)
                dve.tensor_tensor(tmp, lg, spread(top, E3, 2), ALU.subtract).then_inc(ev(nm + ".diff"), 1)
                dve.wait_ge(ev(nm + ".exp"), 1)
                q.link(dve.tensor_reduce(den, lg, X, ALU.add))
                q.link(dve.reciprocal(den, den))
                t = P.take(dve, nm + ".rank")
                q.link(dve.tensor_tensor(rank, t[:, 0:G * E3].rearrange("p (s e) -> p s e", s=G),
                                         spread(counts[:], G), ALU.add))
                P.give(dve.tensor_tensor(counts[:], t[:, G * E3:(G + 1) * E3], counts[:], ALU.add), nm + ".rank")
                q.link(dve.tensor_tensor(rank, rank, oh, ALU.mult))
                q.link(dve.tensor_reduce(mine, rank, X, ALU.add))
                q.link(dve.scalar_tensor_tensor(out=mine, in0=mine, scalar=float(CAP), in1=den, op0=ALU.is_lt,
                                                op1=ALU.mult))
                dve.tensor_tensor(gate, oh, spread(mine, E3, 2), ALU.mult).then_inc(ev(nm + ".gate"), 1)

                def feed(e):
                    t = P.take(dve, f"{nm}.g{e}")
                    if e >= XR:
                        P.take(dve, f"{nm}.u{(e - XR) * nch + nch - 1}")
                    P.give(dve.tensor_tensor(xg[:, e % XR, :], hT[:], t, ALU.mult), f"{nm}.g{e}")

                feed(0)
                for n in range(nall):
                    if n % nch == 1 and n // nch + 1 < E3:
                        feed(n // nch + 1)
                    if n % 2 == 1:
                        relu_chunk(dve, n)
                residual_dve(dve, q, nm + ".y")

            return pe_f, act_f, dve_f, nothing

        def cross3(nm):
            H3, DV = 4, 32
            S = Scratch(scratch)
            r = [S.take(N) for _ in range(4)]
            qT, kT = S.take(N), S.take(N)
            vaug = S.take(G * (DV + 1)).rearrange("p (s e) -> p s e", s=G)
            negm = S.take(N).rearrange("p (s h) -> p s h", s=G)
            mT = S.take(N)
            pT = S.take(2 * H3 * L).rearrange("p (b f) -> p b f", b=2)
            rden = S.take(G * H3).rearrange("p (s h) -> p s h", s=G)
            osb, oT = S.take(N), S.take(N)

            def pe_f(pe):
                norm_pe(pe, nm)
                P.wait_given(pe, nm + ".hT")
                for name, wn, src in (("q", "Wq", hT), ("qs", "Wq_swap", hT), ("k", "Wk", ctxnT),
                                      ("ks", "Wk_swap", ctxnT)):
                    t = P.open(pe, f"{nm}.{name}")
                    P.close(pe.matmul(t, W["x3_" + wn][:], src[:], start=True, stop=True), f"{nm}.{name}")
                t = P.open(pe, nm + ".v")
                for s in range(G):
                    last = pe.matmul(t[:, s * DV:(s + 1) * DV], ctxnT[:, col(s)], W["x3_Wv"][:], start=True,
                                     stop=True, skip_group_check=True)
                P.close(last, nm + ".v")
                pe.wait_ge(ev(nm + ".qk"), 1)

                def scores(s):
                    for h in range(H3):
                        t = P.open(pe, f"{nm}.S{s}{h}")
                        rr = slice(32 * h, 32 * h + 32)
                        pe.matmul(t[:, 0:L], qT[rr, col(s)], kT[rr, col(s)], start=True, stop=False,
                                  skip_group_check=True)
                        P.close(pe.matmul(t[:, 0:L], ones_first[:], pad_wide[:, col(s)], start=False, stop=True,
                                          skip_group_check=True), f"{nm}.S{s}{h}")

                def turned(s):
                    for h in range(H3):
                        P.wait_given(pe, f"{nm}.S{s}{h}")
                    t = P.open(pe, f"{nm}.mT{s}")
                    P.close(pe.transpose(t[:, 0:L], negm[:, s, :], ident[:]), f"{nm}.mT{s}")
                    P.wait_given(pe, f"{nm}.mT{s}")
                    for h in range(H3):
                        t = P.open(pe, f"{nm}.T{s}{h}")
                        rr = slice(32 * h, 32 * h + 32)
                        pe.matmul(t[:, 0:L], kT[rr, col(s)], qT[rr, col(s)], start=True, stop=False,
                                  skip_group_check=True)
                        P.close(pe.matmul(t[:, 0:L], ident[:, h:h + 1].broadcast_to([128, 128]), mT[:, col(s)],
                                          start=False, stop=True, skip_group_check=True), f"{nm}.T{s}{h}")

                def values(s):
                    if s == 0:
                        P.wait_given(pe, nm + ".v")
                    t = P.open(pe, f"{nm}.O{s}")
                    for h in range(H3):
                        P.wait_given(pe, f"{nm}.T{s}{h}")
                        last = pe.matmul(t[:, h * (DV + 1):(h + 1) * (DV + 1)], pT[:, s % 2, h * L:(h + 1) * L],
                                         vaug[:, s, :], start=True, stop=True, skip_group_check=True)
                    P.close(last, f"{nm}.O{s}")

                for step in range(G + 2):
                    if step < G:
                        scores(step)
                    if 1 <= step <= G:
                        turned(step - 1)
                    if step >= 2:
                        values(step - 2)
                t = P.open(pe, nm + ".oT")
                for s in range(G):
                    P.wait_given(pe, f"{nm}.O{s}")
                    last = pe.transpose(t[:, col(s)], osb[:, col(s)], ident[:])
                P.close(last, nm + ".oT")
                P.wait_given(pe, nm + ".oT")
                t = P.open(pe, nm + ".y", ACC)
                for s in range(G):
                    last = pe.matmul(t[:, col(s)], oT[:, col(s)], W["x3_Wo"][:], start=True, stop=True,
                                     skip_group_check=True)
                P.close(last, nm + ".y")

            def act_f(act, q):
                norm_act(act, nm, True)
                t = P.take(act, nm + ".v")
                P.give(act.copy(vaug[:, :, 0:DV], t[:, 0:G * DV].rearrange("p (s e) -> p s e", s=G)), nm + ".v")
                for s in range(G):
                    t = P.take(act, f"{nm}.mT{s}")
                    P.give(act.copy(mT[:, col(s)], t[:, 0:L]), f"{nm}.mT{s}")
                    if s >= 2:
                        P.take(act, f"{nm}.O{s - 2}")
                    for h in range(H3):
                        t = P.take(act, f"{nm}.T{s}{h}")
                        P.give(act.activation(pT[:, s % 2, h * L:(h + 1) * L], t[:, 0:L], ACT.Exp,
                                              bias=pad_col[:, s:s + 1]), f"{nm}.T{s}{h}")
                t = P.take(act, nm + ".oT")
                P.give(act.copy(oT, t), nm + ".oT")

            def dve_f(dve, q):
                norm_dve(dve, q, nm, True)
                for k, name in enumerate(("q", "qs", "k", "ks")):
                    t = P.take(dve, f"{nm}.{name}")
                    P.give(dve.tensor_tensor(row_tiles(r[k]), row_tiles(t), spread(W["rope3"][:, k, :], G),
                                             ALU.mult), f"{nm}.{name}")
                dve.wait_ge(ev(nm + ".ones"), 2)
                for step in range(G + 2):
                    if step < G:
                        s = step
                        for h in range(H3):
                            t = P.take(dve, f"{nm}.S{s}{h}")
                            P.give(dve.tensor_reduce(negm[:, s, h:h + 1], t[:, 0:L], X, ALU.max, negate=True),
                                   f"{nm}.S{s}{h}")
                    if step >= 2:
                        s = step - 2
                        t = P.take(dve, f"{nm}.O{s}")[:, 0:H3 * (DV + 1)].rearrange("p (h e) -> p h e", h=H3)
                        q.link(dve.reciprocal(rden[:, s, :], t[:, :, DV]))
                        P.give(dve.tensor_tensor(osb[:, col(s)].rearrange("p (h e) -> p h e", h=H3), t[:, :, 0:DV],
                                                 spread(rden[:, s, :], DV, 2), ALU.mult), f"{nm}.O{s}")
                residual_dve(dve, q, nm + ".y")

            def pool_f(pool, q):
                pool.wait_ge(ev(nm + ".hn"), 1)
                pool.memset(vaug[:, :, DV:DV + 1], 1.0).then_inc(ev(nm + ".ones"), 1)
                pool.memset(negm[:, :, H3:], 0.0).then_inc(ev(nm + ".ones"), 1)
                for k, name in ((0, "q"), (1, "qs"), (2, "k"), (3, "ks")):
                    P.wait_given(pool, f"{nm}.{name}")
                pool.tensor_tensor(qT, r[0], r[1], ALU.add)
                pool.tensor_tensor(kT, r[2], r[3], ALU.add).then_inc(ev(nm + ".qk"), 1)

            return pe_f, act_f, dve_f, pool_f

        def mamba(nm):
            S = Scratch(scratch)
            xpad = S.take(2 * G * (L + 3)).rearrange("p (c s t) -> p c s t", c=2, s=G)
            xc, z, dtr, delta, du, pos, neg = (S.take(2 * N).rearrange("p (c t) -> p c t", c=2) for _ in range(7))
            dstart, yacc = neg, pos
            RING = 3
            decay, inp, state, yc = (S.take(RING * N).rearrange("p (r t) -> p r t", r=RING) for _ in range(4))
            parts = S.take(4 * N, BF16).rearrange("p (k c t) -> p k c t", k=2, c=2)
            rest = S.take(4 * N).rearrange("p (k c t) -> p k c t", k=2, c=2)
            pairs = [(k, c) for c in range(2) for k in range(2)]
            steps = [(c, n) for c in range(2) for n in range(DS)]

            def pe_f(pe):
                norm_pe(pe, nm)
                P.wait_given(pe, nm + ".hT")
                for m in range(4):
                    t = P.open(pe, f"{nm}.in{m}")
                    P.close(pe.matmul(t, W["s_in"][:, m * 128:(m + 1) * 128], hT[:], start=True, stop=True),
                            f"{nm}.in{m}")
                for c in range(2):
                    pe.wait_ge(ev(nm + ".xc"), c + 1)
                    t = P.open(pe, f"{nm}.dtr{c}")
                    P.close(pe.matmul(t[0:2 * DS, :], W["s_x"][:, c * 32:c * 32 + 32], xc[:, c, :],
                                      start=True, stop=True), f"{nm}.dtr{c}")
                for k, c in pairs:
                    t = P.open(pe, f"{nm}.rows{k}{c}")
                    P.close(pe.matmul(t[0:96, :], W["s_bc"][:, (k * 2 + c) * 96:(k * 2 + c) * 96 + 96], xc[:, c, :],
                                      start=True, stop=True), f"{nm}.rows{k}{c}")
                for c in range(2):
                    P.wait_given(pe, f"{nm}.dtr{c}")
                    t = P.open(pe, f"{nm}.dt{c}")
                    P.close(pe.matmul(t, W["s_dt"][:, c * 128:(c + 1) * 128], dtr[0:2 * DS, c, :],
                                      start=True, stop=True), f"{nm}.dt{c}")
                for c, n in steps:
                    if n == 0:
                        pe.wait_ge(ev(nm + ".parts"), 2 * c + 2)
                    for k in (1, 2):
                        t = P.open(pe, f"{nm}.bc{k}.{c}.{n}")
                        P.close(pe.matmul(t, sel_state[:, n, :], parts[0:96, k - 1, c, :], start=True, stop=True),
                                f"{nm}.bc{k}.{c}.{n}")
                for c in range(2):
                    pe.wait_ge(ev(nm + ".gated"), c + 1)
                t = P.open(pe, nm + ".y", ACC)
                for s in range(G):
                    for c in range(2):
                        last = pe.matmul(t[:, col(s)], yacc[:, c, col(s)], W["s_out"][:, c, :], start=c == 0,
                                         stop=c == 1, skip_group_check=True)
                P.close(last, nm + ".y")

            def act_f(act, q):
                norm_act(act, nm)
                act.wait_ge(ev(nm + ".zero"), 1)
                for c in range(2):
                    t = P.take(act, f"{nm}.in{c}")
                    P.give(act.copy(xpad[:, c, :, 3:], row_tiles(t)), f"{nm}.in{c}")
                for c in range(2):
                    t = P.take(act, f"{nm}.in{2 + c}")
                    P.give(act.activation(z[:, c, :], t, ACT.Silu), f"{nm}.in{2 + c}")
                for c in range(2):
                    act.wait_ge(ev(nm + ".conv"), c + 1)
                    act.activation(xc[:, c, :], delta[:, c, :], ACT.Silu,
                                   bias=W["s_conv_b"][:, c:c + 1]).then_inc(ev(nm + ".xc"), 1)
                for c in range(2):
                    t = P.take(act, f"{nm}.dtr{c}")
                    P.give(act.copy(dtr[0:2 * DS, c, :], t[0:2 * DS, :]), f"{nm}.dtr{c}")
                for k, c in pairs:
                    t = P.take(act, f"{nm}.rows{k}{c}")
                    act.copy(parts[0:96, k, c, :], t[0:96, :]).then_inc(ev(nm + ".high"), 1)
                for c in range(2):
                    t = P.take(act, f"{nm}.dt{c}")
                    b = W["s_dt_b"][:, c:c + 1]
                    q.mark(act.activation(pos[:, c, :], t, ACT.Relu, bias=b))
                    P.give(act.activation(neg[:, c, :], t, ACT.Abs, bias=b), f"{nm}.dt{c}")
                P.wait_given(act, nm + ".dt1")
                q.link(act.activation(neg[:], neg[:], ACT.Exp, scale=-1.0))
                act.activation(neg[:], neg[:], ACT.Ln, bias=ones_col[:]).then_inc(ev(nm + ".soft"), 1)
                act.wait_ge(ev(nm + ".start"), 1)
                for k, (c, n) in enumerate(steps):
                    if k >= RING:
                        act.wait_ge(ev(nm + ".state"), k - RING + 1)
                    act.activation(decay[:, k % RING, :], dstart[:, c, :], ACT.Exp,
                                   scale=ssm_A[:, c, n:n + 1]).then_inc(ev(nm + ".decay"), 1)

            def dve_f(dve, q):
                norm_dve(dve, q, nm)
                w = W["s_conv_w"]
                for c in range(2):
                    P.wait_given(dve, f"{nm}.in{c}")
                for k in range(CONV_K):
                    for c in range(2):
                        dst = row_tiles(delta[:, c, :])
                        src = xpad[:, c, :, k:k + L]
                        if k == 0:
                            ins = dve.tensor_scalar(dst, src, w[:, c, k:k + 1], None, ALU.mult)
                        else:
                            q.wait(m[c])
                            ins = dve.scalar_tensor_tensor(out=dst, in0=src, scalar=w[:, c, k:k + 1], in1=dst,
                                                           op0=ALU.mult, op1=ALU.add)
                        if k == 0 and c == 0:
                            m = [0, 0]
                        if k < CONV_K - 1:
                            m[c] = q.mark(ins)
                        else:
                            ins.then_inc(ev(nm + ".conv"), 1)
                for n, (k, c) in enumerate(pairs):
                    dve.wait_ge(ev(nm + ".high"), n + 1)
                    t = P.take(dve, f"{nm}.rows{k}{c}")
                    P.give(dve.tensor_tensor(rest[0:96, k, c, :], t[0:96, :], parts[0:96, k, c, :], ALU.subtract),
                           f"{nm}.rows{k}{c}")
                dve.wait_ge(ev(nm + ".soft"), 1)
                q.link(dve.tensor_tensor(delta[:], pos[:], neg[:], ALU.add))
                q.mark(dve.tensor_tensor(du[:], delta[:], xc[:], ALU.mult))
                q.link(dve.tensor_copy(dstart[:], delta[:]))
                dve.memset(dstart[:].rearrange("p c (s t) -> p c s t", s=G)[:, :, :, 0:1],
                           BIG).then_inc(ev(nm + ".start"), 1)
                for k, (c, n) in enumerate(steps):
                    t = P.take(dve, f"{nm}.bc1.{c}.{n}")
                    P.give(dve.tensor_tensor(inp[:, k % RING, :], du[:, c, :], t, ALU.mult), f"{nm}.bc1.{c}.{n}")
                    P.wait_given(dve, f"{nm}.bc1.{c}.{n}")
                    dve.wait_ge(ev(nm + ".decay"), k + 1)
                    dve.tensor_tensor_scan(state[:, k % RING, :], decay[:, k % RING, :], inp[:, k % RING, :], 0.0,
                                           ALU.mult, ALU.add).then_inc(ev(nm + ".state"), 1)
                    dve.wait_ge(ev(nm + ".state"), k + 1)
                    if k >= RING:
                        dve.wait_ge(ev(nm + ".sum"), k - RING + 1)
                    t = P.take(dve, f"{nm}.bc2.{c}.{n}")
                    P.give(dve.tensor_tensor(yc[:, k % RING, :], state[:, k % RING, :], t, ALU.mult),
                           f"{nm}.bc2.{c}.{n}")
                residual_dve(dve, q, nm + ".y")

            def pool_f(pool, q):
                pool.wait_ge(ev(nm + ".hn"), 1)
                pool.memset(xpad[:, :, :, 0:3], 0.0).then_inc(ev(nm + ".zero"), 1)
                for n, (k, c) in enumerate(pairs):
                    P.wait_given(pool, f"{nm}.rows{k}{c}")
                    q.link(pool.tensor_copy(parts[32:64, k, c, :], rest[32:64, k, c, :]))
                    q.link(pool.tensor_copy(parts[64:96, k, c, :], rest[64:96, k, c, :]))
                    pool.tensor_tensor(parts[64:96, k, c, :], rest[64:96, k, c, :], parts[64:96, k, c, :],
                                       ALU.subtract).then_inc(ev(nm + ".parts"), 1)
                    pool.wait_ge(ev(nm + ".parts"), n + 1)
                for k, (c, n) in enumerate(steps):
                    P.wait_given(pool, f"{nm}.bc2.{c}.{n}")
                    if n == 0:
                        q.link(pool.tensor_scalar(yacc[:, c, :], xc[:, c, :], W["s_D"][:, c:c + 1], None, ALU.mult))
                    pool.tensor_tensor(yacc[:, c, :], yacc[:, c, :], yc[:, k % RING, :],
                                       ALU.add).then_inc(ev(nm + ".sum"), 1)
                    pool.wait_ge(ev(nm + ".sum"), k + 1)
                    if n == DS - 1:
                        pool.tensor_tensor(yacc[:, c, :], yacc[:, c, :], z[:, c, :],
                                           ALU.mult).then_inc(ev(nm + ".gated"), 1)

            return pe_f, act_f, dve_f, pool_f

        def delta(nm):
            S = Scratch(scratch)
            qk = S.take(2 * N).rearrange("p (k t) -> p k t", k=2)
            kb = S.take(N)
            outs = S.take(G * 4 * D).rearrange("p (s o f) -> p s o f", s=G, o=4)
            mats = S.take(G * DELTA_H * 3 * L).rearrange("p (s h m t) -> p s h m t", s=G, h=DELTA_H, m=3)
            TT, Pm, Nb = (S.take(G * N).rearrange("p (s h t) -> p s h t", s=G, h=DELTA_H) for _ in range(3))
            Z, R, U = (S.take(G * D).rearrange("p (s f) -> p s f", s=G) for _ in range(3))
            S = Scratch(scratch)
            S.at = 3 * N + G * 4 * D
            pads = S.take(3 * G * (L + 3)).rearrange("p (k s t) -> p k s t", k=3, s=G)
            vpad = S.take(G * (L + PAD)).rearrange("p (s t) -> p s t", s=G)
            conv = S.take(3 * N).rearrange("p (k s t) -> p k s t", k=3, s=G)
            smooth = S.take(2 * N).rearrange("p (k t) -> p k t", k=2)
            squares = S.take(2 * N).rearrange("p (k t) -> p k t", k=2)
            length = S.take(2 * N).rearrange("p (k t) -> p k t", k=2)
            beta, vb = S.take(N), S.take(N)
            local, mid, mid_odd = (S.take(N).rearrange("p (s t) -> p s t", s=G) for _ in range(3))
            S = Scratch(scratch)
            S.at = 3 * N + G * 4 * D
            prod = S.take(2 * 10 * D).rearrange("p (r k h e) -> p r k h e", r=2, k=10, h=DELTA_H)
            sums = S.take(G * 16).rearrange("p (s o h) -> p s o h", s=G, o=4)
            psums = S.take(G * 40).rearrange("p (s k h) -> p s k h", s=G, k=10)
            feat = S.take(G * NFEAT).rearrange("p (s k h) -> p s k h", s=G, k=14)
            tmp = S.take(G * 16).rearrange("p (s o h) -> p s o h", s=G, o=4)
            fT = S.take(N)
            h1T = S.take(3 * N).rearrange("p (c t) -> p c t", c=3)
            lg, pr = (S.take(G * 16).rearrange("p (a i) -> p a i", i=4) for _ in range(2))
            t16, ss, rr = (S.take(G * DELTA_H) for _ in range(3))
            pm = S.take(2 * 4 * D).rearrange("p (r i h e) -> p r i h e", r=2, i=4, h=DELTA_H)
            mixed, msq, oT = S.take(N), S.take(N), S.take(N)

            NT, T, AT = (lambda s, h, m=m: mats[:, s, h, m, :] for m in range(3))
            heads = range(DELTA_H)

            def hs(h):
                return slice(DELTA_D * h, DELTA_D * h + DELTA_D)

            def pe_f(pe):
                norm_pe(pe, nm)
                P.wait_given(pe, nm + ".hT")
                for name, w in (("p0", "d_Wq"), ("p1", "d_Wk"), ("p2", "d_Wv"), ("beta", "d_Wb_wide")):
                    t = P.open(pe, f"{nm}.{name}")
                    P.close(pe.matmul(t, W[w][:], hT[:], start=True, stop=True), f"{nm}.{name}")
                pe.wait_ge(ev(nm + ".sq"), 2)
                for k in range(2):
                    t = P.open(pe, f"{nm}.len{k}")
                    P.close(pe.matmul(t, W["same_head"][:], squares[:, k, :], start=True, stop=True), f"{nm}.len{k}")
                pe.wait_ge(ev(nm + ".mid"), 1)
                pe.wait_ge(ev(nm + ".kb"), 2)
                for s in range(G):
                    t = P.open(pe, f"{nm}.tok{s}")
                    for o, src in enumerate((local[:, s, :], mid[:, s, :], vb[:, col(s)], vpad[:, s, PAD:])):
                        last = pe.transpose(t[:, o * L:(o + 1) * L], src, ident[:])
                    P.close(last, f"{nm}.tok{s}")
                pe.wait_ge(ev(nm + ".unit"), 2)
                for s in range(G):
                    for h in heads:
                        t = P.open(pe, f"{nm}.M{s}{h}")
                        kh, qh, kbh = qk[hs(h), 1, col(s)], qk[hs(h), 0, col(s)], kb[hs(h), col(s)]
                        pe.matmul(t[:, 0:L], kh, kbh, start=True, stop=True, skip_group_check=True)
                        pe.matmul(t[:, L:2 * L], kbh, kh, start=True, stop=True, skip_group_check=True)
                        P.close(pe.matmul(t[:, 2 * L:3 * L], kh, qh, start=True, stop=True, skip_group_check=True),
                                f"{nm}.M{s}{h}")

                def product(name, s, lhs, rhs, width=L):
                    t = P.open(pe, f"{nm}.{name}{s}")
                    for h in heads:
                        last = pe.matmul(t[:, h * width:(h + 1) * width], lhs(h), rhs(h), start=True, stop=True,
                                         skip_group_check=True)
                    P.close(last, f"{nm}.{name}{s}")

                for lv in range(1, 6):
                    for s in range(G):
                        pe.wait_ge(ev(f"{nm}.Nb"), G * (lv - 1) + s + 1)
                        if lv == 1:
                            pe.wait_ge(ev(nm + ".T"), s + 1)
                        else:
                            P.wait_given(pe, f"{nm}.L{lv - 1}t{s}")
                        product(f"L{lv}P", s, lambda h: Nb[:, s, h, :], lambda h: T(s, h))
                    for s in range(G):
                        P.wait_given(pe, f"{nm}.L{lv}P{s}")
                        if lv < 5:
                            product(f"L{lv}T", s, lambda h: TT[:, s, h, :], lambda h: Pm[:, s, h, :])
                        product(f"L{lv}t", s, lambda h: Pm[:, s, h, :], lambda h: TT[:, s, h, :])
                for s in range(G):
                    P.wait_given(pe, f"{nm}.L5t{s}")
                    product("Z", s, lambda h: TT[:, s, h, :], lambda h: outs[:, s, 2, hs(h)], DELTA_D)
                for s in range(G):
                    P.wait_given(pe, f"{nm}.Z{s}")
                    pe.wait_ge(ev(f"{nm}.Nb"), G * 5 + s + 1)
                    product("R", s, lambda h: Nb[:, s, h, :], lambda h: Z[:, s, hs(h)], DELTA_D)
                for s in range(G):
                    P.wait_given(pe, f"{nm}.R{s}")
                    product("U", s, lambda h: TT[:, s, h, :], lambda h: R[:, s, hs(h)], DELTA_D)
                for s in range(G):
                    P.wait_given(pe, f"{nm}.U{s}")
                    product("D", s, lambda h: AT(s, h), lambda h: U[:, s, hs(h)], DELTA_D)
                pe.wait_ge(ev(nm + ".feat"), 1)
                t = P.open(pe, nm + ".fT")
                for s in range(G):
                    last = pe.transpose(t[0:NFEAT, col(s)], feat[:, s, :, :].rearrange("p k h -> p (k h)"), ident[:])
                P.close(last, nm + ".fT")
                P.wait_given(pe, nm + ".fT")
                for c, (r0, rows) in enumerate(RCH):
                    t = P.open(pe, f"{nm}.h{c}")
                    pe.matmul(t[0:rows, :], W["d_r_w1a"][:, r0:r0 + rows], hT[:], start=True, stop=False)
                    P.close(pe.matmul(t[0:rows, :], W["d_r_w1b"][0:NFEAT, r0:r0 + rows], fT[0:NFEAT, :],
                                      start=False, stop=True), f"{nm}.h{c}")
                for c in range(3):
                    P.wait_given(pe, f"{nm}.h{c}")
                t = P.open(pe, nm + ".lg")
                bias_row(pe, t, W["d_r_b2"][:])
                for s in range(G):
                    for c, (r0, rows) in enumerate(RCH):
                        last = pe.matmul(t[:, s * 16:(s + 1) * 16], h1T[0:rows, c, col(s)], W["d_r_w2"][0:rows, c, :],
                                         start=False, stop=c == 2, skip_group_check=True)
                P.close(last, nm + ".lg")
                pe.wait_ge(ev(nm + ".mixed"), 1)
                t = P.open(pe, nm + ".oT")
                for s in range(G):
                    last = pe.transpose(t[:, col(s)], mixed[:, col(s)], ident[:])
                P.close(last, nm + ".oT")
                P.wait_given(pe, nm + ".oT")
                t = P.open(pe, nm + ".y", ACC)
                for s in range(G):
                    last = pe.matmul(t[:, col(s)], oT[:, col(s)], W["d_Wo"][:], start=True, stop=True,
                                     skip_group_check=True)
                P.close(last, nm + ".y")

            def act_f(act, q):
                norm_act(act, nm)
                act.wait_ge(ev(nm + ".zero"), 1)
                for k in range(3):
                    t = P.take(act, f"{nm}.p{k}")
                    P.give(act.copy(pads[:, k, :, 3:], row_tiles(t)), f"{nm}.p{k}")
                for k in (2, 0, 1):
                    act.wait_ge(ev(nm + ".conv"), {2: 1, 0: 2, 1: 3}[k])
                    dst = vpad[:, :, PAD:] if k == 2 else row_tiles(smooth[:, k, :])
                    act.activation(dst, conv[:, k, :, :], ACT.Silu).then_inc(ev(nm + ".silu"), 1)
                act.wait_ge(ev(nm + ".silu"), 3)
                for k in range(2):
                    act.activation(squares[:, k, :], smooth[:, k, :], ACT.Square).then_inc(ev(nm + ".sq"), 1)
                t = P.take(act, nm + ".beta")
                P.give(act.activation(beta, t, ACT.Sigmoid), nm + ".beta")
                for k in range(2):
                    t = P.take(act, f"{nm}.len{k}")
                    P.give(act.activation(length[:, k, :], t, ACT.Sqrt, bias=eps12[:]), f"{nm}.len{k}")
                for s in range(G):
                    t = P.take(act, f"{nm}.tok{s}")
                    P.give(act.copy(outs[:, s, :, :].rearrange("p o f -> p (o f)"), t), f"{nm}.tok{s}")
                for lv in range(1, 6):
                    for s in range(G):
                        t = P.take(act, f"{nm}.L{lv}P{s}")
                        P.give(act.copy(Pm[:, s, :, :].rearrange("p h t -> p (h t)"), t), f"{nm}.L{lv}P{s}")
                for name, dst in (("Z", Z), ("R", R)):
                    for s in range(G):
                        t = P.take(act, f"{nm}.{name}{s}")
                        P.give(act.copy(dst[:, s, :], t[:, 0:D]), f"{nm}.{name}{s}")
                for s in range(G):
                    t = P.take(act, f"{nm}.D{s}")
                    P.give(act.copy(outs[:, s, 2, :], t[:, 0:D]), f"{nm}.D{s}")
                t = P.take(act, nm + ".fT")
                P.give(act.copy(fT[0:NFEAT, :], t[0:NFEAT, :]), nm + ".fT")
                for c, (r0, rows) in enumerate(RCH):
                    t = P.take(act, f"{nm}.h{c}")
                    P.give(act.activation(h1T[0:rows, c, :], t[0:rows, :], ACT.Silu, bias=W["d_r_b1"][0:rows, c, :]),
                           f"{nm}.h{c}")
                act.wait_ge(ev(nm + ".diff"), 1)
                act.activation(pr, lg, ACT.Exp).then_inc(ev(nm + ".exp"), 1)
                for k in range(2):
                    act.wait_ge(ev(nm + ".ss"), k + 1)
                    act.activation(rr, ss, ACT.Sqrt, scale=1.0 / DELTA_D, bias=eps5[:]).then_inc(ev(nm + ".rr"), 1)
                t = P.take(act, nm + ".oT")
                P.give(act.copy(oT, t), nm + ".oT")

            def dve_f(dve, q):
                norm_dve(dve, q, nm)
                marks = {}

                def tap(key, dst, src, w, k, done=None):
                    if key in marks:
                        q.wait(marks[key])
                        ins = dve.scalar_tensor_tensor(out=dst, in0=src, scalar=w[:, k:k + 1], in1=dst,
                                                       op0=ALU.mult, op1=ALU.add)
                    else:
                        ins = dve.tensor_scalar(dst, src, w[:, k:k + 1], None, ALU.mult)
                    if done:
                        ins.then_inc(ev(done), 1)
                    else:
                        marks[key] = q.mark(ins)

                names = ("d_conv_q_w", "d_conv_k_w", "d_conv_v_w")
                for k in range(3):
                    P.wait_given(dve, f"{nm}.p{k}")
                for tp in range(CONV_K):
                    for k in (2, 0, 1):
                        tap(k, conv[:, k, :, :], pads[:, k, :, tp:tp + L], W[names[k]], tp,
                            nm + ".conv" if tp == CONV_K - 1 else None)
                dve.wait_ge(ev(nm + ".silu"), 1)
                for n in range(13):
                    tap("even", mid, vpad[:, :, 2 * n:2 * n + L], W["d_mid_w"], 2 * n)
                    if n < 12:
                        tap("odd", mid_odd, vpad[:, :, 2 * n + 1:2 * n + 1 + L], W["d_mid_w"], 2 * n + 1)
                    if n < LOCAL_K:
                        o = PAD - LOCAL_K + 1 + n
                        tap("local", local, vpad[:, :, o:o + L], W["d_local_w"], n)
                q.wait(max(marks.values()))
                dve.tensor_tensor(mid, mid, mid_odd, ALU.add).then_inc(ev(nm + ".mid"), 1)
                for k in (1, 0):
                    P.wait_given(dve, f"{nm}.len{k}")
                    q.link(dve.reciprocal(length[:, k, :], length[:, k, :]))
                    dve.tensor_tensor(qk[:, k, :], smooth[:, k, :], length[:, k, :],
                                      ALU.mult).then_inc(ev(nm + ".unit"), 1)
                for s in range(G):
                    for h in heads:
                        t = P.take(dve, f"{nm}.M{s}{h}")
                        P.give(dve.tensor_tensor(mats[:, s, h, :, :], t[:, 0:3 * L].rearrange("p (m t) -> p m t", m=3),
                                                 W["delta_masks"][:], ALU.mult), f"{nm}.M{s}{h}")
                for lv in range(1, 6):
                    for s in range(G):
                        if lv < 5:
                            t = P.take(dve, f"{nm}.L{lv}T{s}")
                            P.give(dve.tensor_tensor(mats[:, s, :, 1, :], mats[:, s, :, 1, :], row_tiles(t), ALU.add),
                                   f"{nm}.L{lv}T{s}")
                        t = P.take(dve, f"{nm}.L{lv}t{s}")
                        P.give(dve.tensor_tensor(TT[:, s, :, :], TT[:, s, :, :], row_tiles(t), ALU.add),
                               f"{nm}.L{lv}t{s}")
                for s in range(G):
                    P.wait_given(dve, f"{nm}.Z{s}")
                    t = P.take(dve, f"{nm}.U{s}")
                    P.give(dve.tensor_tensor(U[:, s, :], Z[:, s, :], t[:, 0:D], ALU.add), f"{nm}.U{s}")
                P.wait_given(dve, f"{nm}.D{G - 1}")
                for s in range(G):
                    q.mark(dve.tensor_reduce(sums[:, s, :, :], outs[:, s, :, :].rearrange(
                        "p o (h e) -> p o h e", e=DELTA_D), X, ALU.add))
                    dve.wait_ge(ev(nm + ".prod"), s + 1)
                    dve.tensor_reduce(psums[:, s, :, :], prod[:, s % 2, :, :, :], X,
                                      ALU.add).then_inc(ev(nm + ".psum"), 1)
                dve.wait_ge(ev(nm + ".psum"), G)
                mean = feat[:, :, 0:8:2, :]
                q.link(dve.tensor_scalar(mean, sums, 1.0 / DELTA_D, None, ALU.mult))
                q.link(dve.tensor_tensor(tmp, mean, sums, ALU.mult))
                q.link(dve.tensor_tensor(tmp, psums[:, :, 0:4, :], tmp, ALU.subtract))
                dve.tensor_scalar(feat[:, :, 1:8:2, :], tmp, 1.0 / (DELTA_D - 1), None, ALU.mult)
                dve.tensor_scalar(feat[:, :, 8:14, :], psums[:, :, 4:10, :], 1.0 / DELTA_D, None,
                                  ALU.mult).then_inc(ev(nm + ".feat"), 1)
                t = P.take(dve, nm + ".lg")[:, 0:G * 16].rearrange("p (a i) -> p a i", i=4)
                q.link(dve.tensor_reduce(t16, t, X, ALU.max))
                P.give(dve.tensor_tensor(lg, t, spread(t16, 4, 2), ALU.subtract), nm + ".lg")
                P.wait_given(dve, nm + ".lg")
                dve.tensor_copy(t16, t16).then_inc(ev(nm + ".diff"), 1)
                dve.wait_ge(ev(nm + ".exp"), 1)
                q.link(dve.tensor_reduce(t16, pr, X, ALU.add))
                q.link(dve.reciprocal(t16, t16))
                q.link(dve.tensor_tensor(pr, pr, spread(t16, 4, 2), ALU.mult))
                dve.tensor_scalar(pr, pr, 1.0 - 4.0 * 0.01, 0.01, ALU.mult, ALU.add).then_inc(ev(nm + ".probs"), 1)
                for s in range(G):
                    dve.wait_ge(ev(nm + ".pm"), s + 1)
                    dve.tensor_reduce(mixed[:, col(s)].rearrange("p (h e) -> p h e", h=DELTA_H),
                                      pm[:, s % 2].rearrange("p i h e -> p h e i"), X,
                                      ALU.add).then_inc(ev(nm + ".sum"), 1)
                dve.wait_ge(ev(nm + ".sum"), G)
                hv = [a.rearrange("p (a e) -> p a e", e=DELTA_D) for a in (mixed, msq)]
                for k, w in enumerate(("d_mix_w", "d_onorm_w")):
                    q.link(dve.tensor_tensor(msq, mixed, mixed, ALU.mult))
                    dve.tensor_reduce(ss, hv[1], X, ALU.add).then_inc(ev(nm + ".ss"), 1)
                    dve.wait_ge(ev(nm + ".rr"), k + 1)
                    q.link(dve.reciprocal(t16, rr))
                    q.link(dve.tensor_tensor(hv[0], hv[0], spread(t16, DELTA_D, 2), ALU.mult))
                    ins = dve.tensor_tensor(row_tiles(mixed), row_tiles(mixed), spread(W[w][:], G), ALU.mult)
                    if k == 0:
                        q.link(ins)
                    else:
                        ins.then_inc(ev(nm + ".mixed"), 1)
                residual_dve(dve, q, nm + ".y")

            def pool_f(pool, q):
                pool.wait_ge(ev(nm + ".hn"), 1)
                pool.memset(pads[:, :, :, 0:3], 0.0)
                pool.memset(vpad[:, :, 0:PAD], 0.0).then_inc(ev(nm + ".zero"), 1)
                P.wait_given(pool, nm + ".beta")
                pool.wait_ge(ev(nm + ".silu"), 1)
                pool.tensor_tensor(row_tiles(vb), vpad[:, :, PAD:], row_tiles(beta), ALU.mult).then_inc(ev(nm + ".kb"), 1)
                pool.wait_ge(ev(nm + ".unit"), 1)
                pool.tensor_tensor(kb, qk[:, 1, :], beta, ALU.mult).then_inc(ev(nm + ".kb"), 1)

                def level(lv, s):
                    pool.tensor_tensor(Nb[:, s, :, :], mats[:, s, :, 0, :], spread(W["level_T"][:, lv, :], DELTA_H),
                                       ALU.mult).then_inc(ev(f"{nm}.Nb"), 1)

                for s in range(G):
                    for h in heads:
                        P.wait_given(pool, f"{nm}.M{s}{h}")
                    q.mark(pool.tensor_tensor(mats[:, s, :, 1, :], mats[:, s, :, 1, :], spread(ident[:], DELTA_H), ALU.add))
                    q.link(pool.tensor_tensor(TT[:, s, :, :], mats[:, s, :, 0, :],
                                              spread(W["level_T"][:, 0, :], DELTA_H), ALU.mult))
                    pool.tensor_tensor(TT[:, s, :, :], TT[:, s, :, :], spread(ident[:], DELTA_H),
                                       ALU.add).then_inc(ev(nm + ".T"), 1)
                    level(1, s)
                for lv in range(2, 7):
                    for s in range(G):
                        P.take(pool, f"{nm}.L{lv - 1}P{s}")
                        level(lv, s)
                o4 = outs.rearrange("p s o (h e) -> p s o h e", h=DELTA_H)
                P.wait_given(pool, f"{nm}.D{G - 1}")
                for s in range(G):
                    if s >= 2:
                        pool.wait_ge(ev(nm + ".psum"), s - 1)
                    o, w = o4[:, s], prod[:, s % 2]
                    pool.tensor_tensor(w[:, 0:4], o, o, ALU.mult)
                    for a, k, n in ((0, 4, 3), (1, 7, 2)):
                        for b in range(n):
                            pool.tensor_tensor(w[:, k + b], o[:, a], o[:, a + 1 + b], ALU.mult)
                    pool.tensor_tensor(w[:, 9], o[:, 2], o[:, 3], ALU.mult).then_inc(ev(nm + ".prod"), 1)
                pool.wait_ge(ev(nm + ".probs"), 1)
                pv = pr.rearrange("p (s h) i -> p s h i", s=G)
                for s in range(G):
                    if s >= 2:
                        pool.wait_ge(ev(nm + ".sum"), s - 1)
                    pool.tensor_tensor(pm[:, s % 2], o4[:, s],
                                       spread(pv[:, s].rearrange("p h i -> p i h"), DELTA_D, 3),
                                       ALU.mult).then_inc(ev(nm + ".pm"), 1)

            return pe_f, act_f, dve_f, pool_f

        sections = {
            "L0_delta": delta("d0"),
            "L0_cross": attention16("x0", "x0_", src="ctx"),
            "L0_ffn": ffn("f0"),
            "L1_attn": attention16("a1", "a1_", bias=True, bias_out=True, mask="causal"),
            "L1_mix": mixer("m1"),
            "L1_moe": moe1("e1"),
            "L2_attn": attention16("a2", "a2_", rope=True, mask="causal"),
            "L2_cross": attention16("x2", "x2_", src="ctx", bias=True, bias_out=True, mask="given"),
            "L2_moe": moe2("e2"),
            "L3_mamba": mamba("s3"),
            "L3_cross": cross3("x3"),
            "L3_moe": moe3("e3"),
        }
        last_sum = {"L0_delta": "d0.y", "L0_cross": "x0.y", "L0_ffn": "f0.y", "L1_attn": "a1.y", "L1_mix": "m1.y",
                    "L1_moe": "e1.y", "L2_attn": "a2.y", "L2_cross": "x2.y", "L2_moe": "e2.y", "L3_mamba": "s3.y",
                    "L3_cross": "x3.y", "L3_moe": "e3.y"}[SECTIONS[-1]]
        run = [sections[n] for n in SECTIONS]
        x_d = dram["x"].rearrange("(g s) t f -> g t s f", s=G)
        c_d = dram["ctx"].rearrange("(g s) t f -> g t s f", s=G)
        m_d = dram["mask"].rearrange("(g s) t f -> g t s f", s=G)
        p_d = dram["key_pad"].rearrange("(g a s) t -> g a (s t)", a=1, s=G)
        o_d = out.rearrange("(g s) t f -> g t s f", s=G)

        def load_experts3(sp):
            if "L2_moe" in SECTIONS:
                P.take(sp, "e2.y")
            sp.dma_start(experts[:, 0:E3 * F3], dram["e3_W1"]).then_inc(s_e3, 16)
            sp.dma_start(experts[:, E3 * F3:].rearrange("p (c f) -> p c f", f=D),
                         dram["e3_W2"].rearrange("(c p) f -> p c f", p=128)).then_inc(s_e3, 16)

        with nc.Fori(0, NGROUPS) as g:
            with nc.Block(no_gpsimd_drain=True) as block:
                @block.tensor
                def _(pe):
                    ctx_pe(pe)
                    for f in run:
                        f[0](pe)

                @block.scalar
                def _(act):
                    q = Order(act, s_act)
                    ctx_act(act)
                    for f in run:
                        f[1](act, q)

                @block.vector
                def _(dve):
                    q = Order(dve, s_dve)
                    ctx_dve(dve, q)
                    dve.wait_ge(s_in, 16)
                    for f in run:
                        f[2](dve, q)

                @block.gpsimd
                def _(pool):
                    q = Order(pool, s_pool)
                    for f in run:
                        f[3](pool, q)

                @block.sync
                def _(sp):
                    sp.dma_start(ctx_tok[:], c_d[g]).then_inc(s_ctx, 16)
                    sp.dma_start(xres[:], x_d[g]).then_inc(s_in, 16)
                    sp.dma_start(mask_i[:], m_d[g]).then_inc(s_ctx, 16)
                    sp.dma_start(pad_row_u8[:], p_d[g]).then_inc(s_ctx, 16)
                    if "L2_moe" in SECTIONS:
                        sp.dma_start(experts[:, 0:E2 * F2], dram["e2_w1"]).then_inc(s_e2, 16)
                        sp.dma_start(experts[:, E2 * F2:2 * E2 * F2].rearrange("p (c f) -> p c f", f=D),
                                     dram["e2_w2"].rearrange("(c p) f -> p c f", p=128)).then_inc(s_e2, 16)
                    for name, f in zip(SECTIONS, run):
                        if len(f) > 4:
                            f[4](sp)
                        if name == "L2_moe" or name == "L3_moe" and "L2_moe" not in SECTIONS:
                            load_experts3(sp)
                    P.wait_given(sp, last_sum)
                    sp.dma_start(o_d[g], xres[:]).then_inc(s_out, 16)
                    sp.wait_ge(s_out, 16)

            for s in [s_in, s_ctx, s_stack, s_e2, s_e3, s_out, s_dve, s_act, s_pool] + s_stored + filled + emptied + list(events.values()):
                nc.sync.sem_clear(s)
            nc.all_engine_barrier()


def kernel(**inputs):
    import concourse.bacc as bacc
    from concourse.bass_utils import run_bass_kernel_spmd

    arrays = host_layout({k: np.asarray(v) for k, v in inputs.items()})
    arrays.update(host_constants())
    nc = bacc.Bacc("TRN2", target_bir_lowering=False, num_devices=1)
    dram = {n: nc.dram_tensor("in_" + n, a.shape, mybir.dt.from_np(a.dtype), kind="ExternalInput").ap()
            for n, a in arrays.items()}
    out = nc.dram_tensor("out", (B, L, D), F32, kind="ExternalOutput").ap()
    build(nc, dram, out)
    r = run_bass_kernel_spmd(nc, [{"in_" + n: a for n, a in arrays.items()}], core_ids=[0])
    return r.results[0]["out"]
```

```python
from contextlib import ExitStack

import numpy as np
import concourse.bass as bass
from concourse import mybir

F32 = mybir.dt.float32
BF16 = mybir.dt.bfloat16
I32 = mybir.dt.int32
U8 = mybir.dt.uint8
ACT = mybir.ActivationFunctionType
ALU = mybir.AluOpType
X = mybir.AxisListType.X

B, L, D = 32, 128, 128
G = 2
STREAMS = 2
NGROUPS = B // (G * STREAMS)
N = G * L
NH, DH = 16, 8
NJ, NI = 4, 4
DELTA_H, DELTA_D = 4, 32
MID_K, LOCAL_K, CONV_K = 25, 7, 4
PAD = MID_K - 1
NFEAT = 14 * DELTA_H
RH = 2 * (D + NFEAT)
RCH = [(0, 128), (128, 128), (256, RH - 256)]
FFH = 384
E1, H1, HS1 = 8, 176, 352
C1 = E1 * H1 // 128
SCH = [(0, 128), (128, 128), (256, HS1 - 256)]
E2, F2 = 14, 256
E3, F3 = 8, 512
CAP = B * L // E3
RING_BANKS = 8 - STREAMS
DS = 16
SLOTS = ((0, 0), (0, 1), (0, 2), (1, 0), (1, 1), (2, 0))
SCALE16 = float(DH) ** -0.5
BIG = 1.0e30
MASK_BIG, MASK_SMALL = 999424.0, 576.0
SCRATCH = 9400
SECTIONS = ["L0_delta", "L0_cross", "L0_ffn", "L1_attn", "L1_mix", "L1_moe", "L2_attn", "L2_cross", "L2_moe",
            "L3_mamba", "L3_cross", "L3_moe"]

CH1, CH2, CH3, CHS = 2.3, 2.2, 1.1, 1.5
SPANS = {"L0_delta": 104, "L0_cross": 52, "L0_ffn": 14, "L1_attn": 52, "L1_mix": 10, "L1_moe": 50, "L2_attn": 52,
         "L2_cross": 52, "L2_moe": 46, "L3_mamba": 78, "L3_cross": 34, "L3_moe": 52}
PLACE = {n: 1 + sum(SPANS[m] for m in SECTIONS[:k]) for k, n in enumerate(SECTIONS)}
NORMED = 4
LAG = 20.5


def host_constants():
    c = {}
    i, j = np.arange(L)[:, None], np.arange(L)[None, :]
    c["ident"] = np.eye(128, dtype=np.float32)
    levels = [1, 2, 4, 8, 16, 32, 64]
    lev = np.stack([(i // (2 * b) == j // (2 * b)) & ((i // b) % 2 == 1) & ((j // b) % 2 == 0) for b in levels])
    c["delta_masks"] = np.stack([-(i < j).astype(np.float32), -lev[0].astype(np.float32),
                                 (i <= j).astype(np.float32)], 1)
    c["level_T"] = np.ascontiguousarray(lev.transpose(2, 0, 1)).astype(np.float32)
    c["causal"] = np.where(i >= j, 0.0, -1e9).astype(np.float32)
    c["causal_T"] = np.where(i <= j, 0.0, -1e9).astype(np.float32)
    c["before_T"] = (i < j).astype(np.float32)
    c["same_head"] = (i // DELTA_D == j // DELTA_D).astype(np.float32)
    c["slot"] = (i[:, :1] % 32 // DH == np.arange(NI)[None, :]).astype(np.float32)
    c["rev"] = np.broadcast_to(16.0 - np.arange(16, dtype=np.float32), (128, 16)).copy()
    c["sel1"] = (np.arange(E1)[:, None] == np.arange(E1 * H1)[None, :] // H1).astype(np.float32)
    row = np.arange(96)[:, None, None]
    c["sel_state"] = ((row % DS == np.arange(DS)[None, :, None]) &
                      (row % 32 // DS == np.arange(128)[None, None, :] // 64)).astype(np.float32)
    c["sel_part"] = ((i[:, :1] % 32 == np.arange(NH)[None, :]) & (i[:, :1] < 96)).astype(np.float32)
    t = np.arange(L, dtype=np.float32)
    fr = (1.0 / np.float32(10000.0) ** (np.arange(0, DH, 2, dtype=np.float32) / DH)).astype(np.float32)
    ang = np.outer(t, fr).astype(np.float32)
    p = np.arange(128)
    cos, sin = np.cos(ang).T[(p % DH) // 2], np.sin(ang).T[(p % DH) // 2]
    sin = np.where(p[:, None] % 2 == 0, -sin, sin)
    c["rope2"] = np.stack([cos * SCALE16, sin * SCALE16, cos, sin], 1).astype(np.float32)
    ts = np.float32(10000.0) ** (np.float32(2.0 / 32) * np.arange(16, dtype=np.float32))
    sgn = np.where(p[:, None] % 32 < 16, -1.0, 1.0)
    out = []
    for pos, sc in ((t + L, 32.0 ** -0.5), (t, 1.0)):
        rad = (pos[:, None] / ts).astype(np.float32)
        out += [np.cos(rad).T[p % 16] * sc, np.sin(rad).T[p % 16] * sgn * sc]
    c["rope3"] = np.stack(out, 1).astype(np.float32)
    return c


def host_layout(a):
    w = {}
    cont = np.ascontiguousarray
    w["x"], w["ctx"], w["mask"] = a["x"], a["ctx_1024"], a["mask_BxSxS2_if1"]
    w["key_pad"] = a["mask_BxS2_bk0"]
    for n in ("Wq", "Wk", "Wv", "Wb", "Wo"):
        w["d_" + n] = a["L0_attn_" + n]
    w["d_Wb_wide"] = cont(np.repeat(a["L0_attn_Wb"], DELTA_D, axis=1))
    for n in ("conv_q_w", "conv_k_w", "conv_v_w", "local_w", "mid_w", "r_w1"):
        w["d_" + n] = a["L0_attn_" + n]
    w["d_r_b1"] = a["L0_attn_r_b1"][:, None]
    w["d_r_w2"] = a["L0_attn_r_w2"]
    w["d_r_b2"] = a["L0_attn_r_b2"][None, :]
    w["d_mix_w"] = cont(np.broadcast_to(a["L0_attn_mix_w"].reshape(1, D), (128, D)))
    w["d_onorm_w"] = cont(np.broadcast_to(a["L0_attn_onorm_w"][None, None, :], (128, DELTA_H, DELTA_D)).reshape(128, D))
    for n in ("Wq", "Wk", "Wv", "Wo"):
        w["x0_" + n] = cont(a["L0_xattn_" + n].T)
    w["f_gate"], w["f_up"], w["f_down"] = (cont(a["L0_ffn_w_" + n].T) for n in ("gate", "up", "down"))
    wa = cont(a["L1_attn_w_attn"].T)
    ba = a["L1_attn_b_attn"]
    for k, n in enumerate(("Wq", "Wk", "Wv")):
        w["a1_" + n] = cont(wa[:, k * D:(k + 1) * D])
    w["a1_bq"], w["a1_bk"], w["a1_bv"] = ba[:D, None], ba[D:2 * D, None], ba[None, 2 * D:]
    w["a1_Wo"], w["a1_bo"] = cont(a["L1_attn_w_proj"].T), a["L1_attn_b_proj"][None, :]
    w["m_W1"], w["m_W2"] = cont(a["L1_xattn_W"][:, :D].T), cont(a["L1_xattn_W"][:, D:].T)
    w["m_b"] = a["L1_xattn_b"][None, :]
    w["e1_Wg"] = a["L1_ffn_Wg"]
    w["e1_W1"] = cont(a["L1_ffn_W1"].transpose(1, 0, 2).reshape(D, E1 * H1))
    w["e1_W2"] = cont(a["L1_ffn_W2"].transpose(1, 0, 2).reshape(D, E1 * H1))
    w["e1_W3"] = a["L1_ffn_W3"].reshape(E1 * H1, D)
    w["e1_Ws1"], w["e1_Ws2"], w["e1_Ws3"] = (a["L1_ffn_Ws%d" % k] for k in (1, 2, 3))
    wq = cont(a["L2_attn_W_qkv"].T)
    swap = np.arange(D) ^ 1
    w["a2_Wq"], w["a2_Wk"], w["a2_Wv"] = (cont(wq[:, k * D:(k + 1) * D]) for k in range(3))
    w["a2_Wq_swap"], w["a2_Wk_swap"] = cont(w["a2_Wq"][:, swap]), cont(w["a2_Wk"][:, swap])
    w["a2_Wo"] = cont(a["L2_attn_W_out"].T)
    for n in ("Wq", "Wk", "Wv", "Wo"):
        w["x2_" + n] = a["L2_xattn_" + n]
    w["x2_bq"], w["x2_bk"] = a["L2_xattn_bq"][:, None], a["L2_xattn_bk"][:, None]
    w["x2_bv"], w["x2_bo"] = a["L2_xattn_bv"][None, :], a["L2_xattn_bo"][None, :]
    w["e2_Wr"] = a["L2_ffn_router_w"]
    w["e2_w1"] = cont(a["L2_ffn_w1"].transpose(1, 0, 2).reshape(D, E2 * F2))
    w["e2_b1"] = cont(a["L2_ffn_b1"].reshape(E2 * F2 // 128, 128).T)
    w["e2_w2"] = a["L2_ffn_w2"].reshape(E2 * F2, D)
    w["e2_b2"] = a["L2_ffn_b2"]
    w["s_in"] = cont(a["L3_attn_in_proj_w"].T)
    w["s_conv_w"] = cont(a["L3_attn_conv_w"].reshape(2, 128, 4).transpose(1, 0, 2))
    w["s_conv_b"] = cont(a["L3_attn_conv_b"].reshape(2, 128).T)
    xw = a["L3_attn_x_proj_w"].reshape(4, 3, DS, 64)
    dtw = a["L3_attn_dt_proj_w"].reshape(4, 64, DS)
    w_x = np.zeros((128, 2, 2, DS), np.float32)
    w_bc = np.zeros((128, 2, 2, 3, 2, DS), np.float32)
    w_dt = np.zeros((2 * DS, 2, 128), np.float32)
    for c in range(2):
        for h in range(2):
            w_x[64 * h:64 * h + 64, c, h, :] = xw[2 * c + h, 0].T
            w_bc[64 * h:64 * h + 64, :, c, :, h, :] = xw[2 * c + h, 1:].transpose(2, 0, 1)[:, :, None, :]
            w_dt[DS * h:DS * h + DS, c, 64 * h:64 * h + 64] = dtw[2 * c + h].T
    w["s_x"], w["s_dt"] = w_x.reshape(128, 4 * DS), w_dt.reshape(2 * DS, 256)
    w["s_bc"] = w_bc.reshape(128, 24 * DS)
    w["s_dt_b"] = cont(a["L3_attn_dt_proj_b"].reshape(2, 128).T)
    w["s_A_log"] = cont(a["L3_attn_A_log"].reshape(2, 128, DS).transpose(1, 0, 2))
    w["s_D"] = cont(a["L3_attn_Dskip"].reshape(2, 128).T)
    w["s_out"] = cont(a["L3_attn_out_proj_w"].T)
    w["x3_scale"] = a["L3_xattn_rms_scale"][:, None]
    qw = cont(a["L3_xattn_q_w"].transpose(1, 0, 2).reshape(D, 128))
    half = np.arange(128) ^ 16
    w["x3_Wq"], w["x3_Wq_swap"] = qw, cont(qw[:, half])
    kw = cont(np.tile(a["L3_xattn_kv_w"][0, 0], (1, 4)))
    w["x3_Wk"], w["x3_Wk_swap"] = kw, cont(kw[:, half])
    w["x3_Wv"] = a["L3_xattn_kv_w"][1, 0]
    w["x3_Wo"] = a["L3_xattn_out_w"].reshape(128, D)
    w["e3_Wr"] = a["L3_ffn_Wr"]
    w["e3_W1"] = cont(a["L3_ffn_W1"].transpose(1, 0, 2).reshape(D, E3 * F3))
    w["e3_W2"] = a["L3_ffn_W2"].reshape(E3 * F3, D)
    return {k: cont(v) for k, v in w.items()}


ROWS = {"d_r_w2": RCH, "e1_Ws3": SCH}
CHUNKED = {"e1_W3": C1, "s_out": 2}
STREAMED = ("x", "ctx", "mask", "key_pad", "e2_w1", "e2_w2", "e3_W1", "e3_W2")
ROUNDED = ("sel_state", "sel_part")
INTEGER = ("f_gate", "f_up", "f_down")


class Psum:

    def __init__(self, banks, filled, emptied):
        self.banks, self.filled, self.emptied = banks, filled, emptied
        self.place, self.turns, self.width, self.next = {}, [0] * 8, {}, 0

    def open(self, pe, name, bank=None, width=N):
        if bank is None:
            bank = self.next
            self.next = (self.next + 1) % RING_BANKS
        turn = self.turns[bank]
        self.turns[bank] += 1
        assert name not in self.place, name
        self.place[name], self.width[name] = (bank, turn), width
        if turn:
            pe.wait_ge(self.emptied[bank], turn)
        return self.banks[:, bank, 0:self.width[name]]

    def bank(self, name):
        return self.banks[:, self.place[name][0], 0:self.width[name]]

    def close(self, ins, name):
        ins.then_inc(self.filled[self.place[name][0]], 1)

    def take(self, eng, name):
        bank, turn = self.place[name]
        eng.wait_ge(self.filled[bank], turn + 1)
        return self.banks[:, bank, 0:self.width[name]]

    def give(self, ins, name):
        ins.then_inc(self.emptied[self.place[name][0]], 1)

    def wait_given(self, eng, name):
        bank, turn = self.place[name]
        eng.wait_ge(self.emptied[bank], turn + 1)


class Order:

    def __init__(self, eng, sem):
        self.eng, self.sem, self.count = eng, sem, 0

    def mark(self, ins):
        self.count += 1
        ins.then_inc(self.sem, 1)
        return self.count

    def wait(self, count):
        self.eng.wait_ge(self.sem, count)

    def link(self, ins):
        self.wait(self.mark(ins))


class Scratch:

    def __init__(self, tensor):
        self.tensor, self.at = tensor, 0

    def take(self, words, dtype=F32):
        size = words if dtype == F32 else (words + 1) // 2
        ap = self.tensor[:, self.at:self.at + size]
        self.at += size
        assert self.at <= SCRATCH, self.at
        return ap if dtype == F32 else ap.bitcast(dtype)


def row_tiles(ap):
    return ap.rearrange("p (s f) -> p s f", f=128)


def spread(ap, count, axis=1):
    ap = ap.unsqueeze(axis)
    shape = list(ap.shape)
    shape[axis] = count
    return ap.broadcast_to(shape)


def build(nc, dram, out):
    with ExitStack() as st:
        def sb(name, shape, dt=F32):
            return st.enter_context(nc.sbuf_tensor(name, shape, dt))

        def sem(name):
            return st.enter_context(nc.semaphore(name))

        W = {}
        plain, chunk_loads = [], []
        experts = sb("experts", [128, 2 * E3 * F3])
        scratches = [sb(f"scratch{u}", [128, SCRATCH]) for u in range(STREAMS)]
        scratch = scratches[0]
        for k, name in enumerate(INTEGER):
            W[name] = scratch[:, k * FFH:(k + 1) * FFH].bitcast(I32)
            if name == "f_down":
                W[name] = W[name].rearrange("p (c f) -> p c f", c=3)
                plain.append((W[name], dram[name].rearrange("(c p) f -> p c f", p=128)))
            else:
                plain.append((W[name], dram[name]))
        at = 3 * FFH
        for name in ROUNDED:
            shape = list(dram[name].shape)
            words = int(np.prod(shape[1:]))
            W[name] = scratch[0:shape[0], at:at + words]
            at += words
            flat = dram[name] if len(shape) == 2 else dram[name].rearrange("p a b -> p (a b)")
            plain.append((W[name], flat))
        sel_state, sel_part = sb("sel_state_bf", [96, DS, 128], BF16), sb("sel_part_bf", [128, NH], BF16)
        for name, t in dram.items():
            if name in STREAMED or name in INTEGER or name in ROUNDED:
                continue
            shape, dt = list(t.shape), F32
            if name in CHUNKED:
                n = CHUNKED[name]
                W[name] = sb("w_" + name, [128, n, shape[1]], dt)
                plain.append((W[name][:], t.rearrange("(c p) f -> p c f", p=128)))
            elif name in ROWS:
                W[name] = sb("w_" + name, [128, len(ROWS[name]), shape[1]], dt)
                for c, (r0, rows) in enumerate(ROWS[name]):
                    plain.append((W[name][0:rows, c, :], t[r0:r0 + rows, :]))
            elif name == "d_r_w1":
                W["d_r_w1a"] = sb("w_d_r_w1a", [128, RH])
                W["d_r_w1b"] = sb("w_d_r_w1b", [NFEAT, RH])
                plain += [(W["d_r_w1a"][:], t[0:D, :]), (W["d_r_w1b"][:], t[D:D + NFEAT, :])]
            elif name == "d_r_b1":
                W[name] = sb("w_d_r_b1", [128, 3, 1])
                for c, (r0, rows) in enumerate(RCH):
                    plain.append((W[name][0:rows, c, :], t[r0:r0 + rows, :]))
            else:
                W[name] = sb("w_" + name, shape, dt)
                plain.append((W[name][:], t))
        ident = W["ident"]
        fw = {n: sb("fw_" + n, [128, FFH] if n != "down" else [128, 3, D]) for n in ("gate", "up", "down")}
        ident_bf, ident_big, ident_small = (sb(n, [128, 128], BF16) for n in ("ident_bf", "ident_big", "ident_small"))
        causal_bf, causal_T_bf = sb("causal_bf", [128, 128], BF16), sb("causal_T_bf", [128, 128], BF16)
        ones_row = sb("ones_row", [1, 128])
        ones_sq = sb("ones_sq", [128, 128])
        ones_col = sb("ones_col", [128, 1])
        eps5, eps6, eps12 = sb("eps5", [128, 1]), sb("eps6", [128, 1]), sb("eps12", [128, 1])
        ones_first = sb("ones_first", [128, 128])
        pad_wides = [sb(f"{u}_pad_wide", [128, N]) for u in range(STREAMS)]
        ssm_A = sb("ssm_A", [128, 2, DS])
        counts = sb("counts", [128, E3])
        scale3 = sb("scale3", [128, 1])

        banks = st.enter_context(nc.psum_tensor("banks", [128, 8, 512], F32))

        s_weights, s_setup = sem("weights_loaded"), sem("setup")
        s_e2, s_e3 = sem("experts2_loaded"), sem("experts3_loaded")
        filled = [sem(f"bank{b}_filled") for b in range(8)]
        emptied = [sem(f"bank{b}_emptied") for b in range(8)]
        s_dve, s_act, s_pool = sem("dve_steps"), sem("act_steps"), sem("pool_steps")
        events = {}

        def ev(name):
            if name not in events:
                events[name] = sem(name)
            return events[name]

        P = Psum(banks, filled, emptied)
        def col(s):
            return slice(s * L, (s + 1) * L)

        with nc.Block(no_gpsimd_drain=True) as block:
            queues = [plain[k::2] for k in range(2)]

            @block.sync
            def _(sp):
                for dst, src in queues[0]:
                    sp.dma_start(dst, src).then_inc(s_weights, 16)

            @block.scalar
            def _(act):
                for dst, src in queues[1]:
                    act.dma_start(dst, src).then_inc(s_weights, 16)
                act.wait_ge(s_weights, 16 * len(plain))
                act.activation(ssm_A[:], W["s_A_log"][:], ACT.Exp).then_inc(s_act, 1)

            @block.gpsimd
            def _(pool):
                pool.memset(ones_row[:], 1.0)
                pool.memset(ones_sq[:], 1.0)
                for wide in pad_wides:
                    pool.memset(wide[:], 0.0)
                pool.memset(ones_first[:], 0.0).then_inc(s_pool, 1)
                pool.wait_ge(s_pool, 1)
                pool.memset(ones_first[0:1, :], 1.0)
                pool.memset(ones_col[:], 1.0)
                pool.memset(eps5[:], 1e-5)
                pool.memset(eps6[:], 1e-6)
                pool.memset(eps12[:], 1e-12)
                pool.memset(counts[:], 0.0).then_inc(s_setup, 1)

            @block.vector
            def _(dve):
                dve.wait_ge(s_weights, 16 * len(plain))
                for n in ("gate", "up", "down"):
                    dve.tensor_scalar(fw[n][:], W["f_" + n], float(np.float32(1.0 / 127.0)), None, ALU.mult)
                dve.tensor_copy(sel_state[:].rearrange("p a b -> p (a b)"), W["sel_state"])
                dve.tensor_copy(sel_part[:], W["sel_part"])
                dve.tensor_copy(ident_bf[:], ident[:])
                dve.tensor_scalar(ident_big[:], ident[:], MASK_BIG, None, ALU.mult)
                dve.tensor_scalar(ident_small[:], ident[:], MASK_SMALL, None, ALU.mult)
                dve.tensor_copy(causal_bf[:], W["causal"][:])
                dve.tensor_copy(causal_T_bf[:], W["causal_T"][:])
                dve.tensor_scalar(scale3[:], W["x3_scale"][:], 1.0, None, ALU.add).then_inc(s_dve, 1)
                dve.wait_ge(s_dve, 1)
                for n in ("Wq", "Wq_swap", "Wk", "Wk_swap", "Wv"):
                    w = W["x3_" + n]
                    dve.tensor_scalar(w[:], w[:], scale3[:], None, ALU.mult)
                dve.wait_ge(s_act, 1)
                dve.tensor_scalar(ssm_A[:], ssm_A[:], -1.0, None, ALU.mult).then_inc(s_setup, 1)
                dve.wait_ge(s_setup, 2)

        nc.sync.sem_clear(s_pool)
        nc.sync.sem_clear(s_dve)
        nc.sync.sem_clear(s_act)
        nc.all_engine_barrier()

        def stream(u):
            scratch = scratches[u]
            xres = sb(f"{u}_xres", [128, G, D])
            ctx_tok = sb(f"{u}_ctx_tok", [128, G, D])
            ctxT = sb(f"{u}_ctxT", [128, N])
            ctxnT = sb(f"{u}_ctxnT", [128, N])
            ctx_sum = sb(f"{u}_ctx_sum", [128, G])
            mask_i = sb(f"{u}_mask_i", [128, G, L], I32)
            mask_f = sb(f"{u}_mask_f", [128, G, L])
            mask_bf, maskT_bf = sb(f"{u}_mask_bf", [128, G, L], BF16), sb(f"{u}_maskT_bf", [128, G, L], BF16)
            pad_row_u8 = sb(f"{u}_pad_row_u8", [1, N], U8)
            pad_row = sb(f"{u}_pad_row", [1, N])
            pad_col = sb(f"{u}_pad_col", [128, G])
            pad_wide = pad_wides[u]
            hn = sb(f"{u}_hn", [128, G, D])
            hT = sb(f"{u}_hT", [128, N])
            stats, mv = sb(f"{u}_stats", [128, G, 6]), sb(f"{u}_mv", [128, G, 2])
            std, rstd, rms, rms2 = (sb(f"{u}_{n}", [128, G]) for n in ("std", "rstd", "rms", "rms2"))
            s_in, s_out, s_ctx = sem(f"group{u}_loaded"), sem(f"group{u}_stored"), sem(f"context{u}_loaded")
            s_stored, s_stack = [sem(f"parts{k}_stored{u}") for k in (1, 2, 3)], sem(f"parts_stacked{u}")
            stack_d = [nc.dram_tensor(f"stack_{k}{u}", (3, 128, N), BF16, kind="Internal").ap() for k in "qk"]
            stacks, norms = {}, {}
            ACC = RING_BANKS + u
            ctx = f"{u}.ctx"

            shared = {}

            def share(**counts):
                base = {n: shared.get(n, 0) for n in counts}
                shared.update({n: base[n] + counts[n] for n in counts})
                return base

            def norm(nm):
                return norms.setdefault(nm, len(norms))

            def norm_pe(pe, nm):
                yield NORMED
                t = P.open(pe, nm + ".hT")
                for s in range(G):
                    pe.wait_ge(ev(f"{u}.hn"), G * norm(nm) + s + 1)
                    last = pe.transpose(t[:, col(s)], hn[:, s, :], ident[:])
                P.close(last, nm + ".hT")

            def norm_act(act, nm, rms_too=False):
                act.wait_ge(ev(f"{u}.var"), norm(nm) + 1)
                act.activation(std[:], mv[:, :, 1], ACT.Sqrt, bias=eps5[:]).then_inc(ev(f"{u}.std"), 1)
                if rms_too:
                    act.wait_ge(ev(nm + ".ms"), 1)
                    act.activation(rms2[:], rms[:], ACT.Sqrt, bias=eps6[:]).then_inc(ev(nm + ".rms"), 1)
                yield NORMED
                t = P.take(act, nm + ".hT")
                P.give(act.copy(hT[:], t), nm + ".hT")

            def norm_dve(dve, q, nm, rms_too=False):
                for s in range(G):
                    m = q.mark(dve.bn_stats(stats[:, s, :], xres[:, s, :]))
                for s in range(G):
                    q.wait(m - G + 1 + s)
                    ins = dve.bn_aggr(mv[:, s, :], stats[:, s, :])
                    if s < G - 1:
                        m2 = q.mark(ins)
                ins.then_inc(ev(f"{u}.var"), 1)
                dve.wait_ge(ev(f"{u}.var"), norm(nm) + 1)
                dve.wait_ge(ev(f"{u}.std"), norm(nm) + 1)
                q.link(dve.reciprocal(rstd[:], std[:]))
                if rms_too:
                    q.link(dve.tensor_tensor(rms[:], mv[:, :, 1], rstd[:], ALU.mult))
                    dve.tensor_tensor(rms[:], rms[:], rstd[:], ALU.mult).then_inc(ev(nm + ".ms"), 1)
                    dve.wait_ge(ev(nm + ".rms"), 1)
                    q.link(dve.reciprocal(rms[:], rms2[:]))
                    q.link(dve.tensor_tensor(rstd[:], rstd[:], rms[:], ALU.mult))
                for s in range(G):
                    dve.tensor_scalar(hn[:, s, :], xres[:, s, :], mv[:, s, 0:1], rstd[:, s:s + 1],
                                      ALU.subtract, ALU.mult).then_inc(ev(f"{u}.hn"), 1)

            def residual_dve(dve, q, name):
                t = P.take(dve, name)
                P.give(dve.tensor_tensor(xres[:].rearrange("p s f -> p (s f)"), xres[:].rearrange("p s f -> p (s f)"), t,
                                         ALU.add), name)
                P.wait_given(dve, name)

            def bias_row(pe, t, row, start=True):
                w = row.shape[-1]
                pe.matmul(t[:, 0:G * w].rearrange("p (s f) -> p s f", s=G), ones_row[:],
                          spread(row, G), start=start, stop=False, skip_group_check=True)

            def ctx_pe(pe):
                pe.wait_ge(s_ctx, 48)
                t = P.open(pe, ctx + ".T")
                for s in range(G):
                    last = pe.transpose(t[:, col(s)], ctx_tok[:, s, :], ident[:])
                P.close(last, ctx + ".T")
                t = P.open(pe, ctx + ".maskT")
                pe.wait_ge(ev(ctx + ".maskf"), 1)
                for s in range(G):
                    last = pe.transpose(t[:, col(s)], mask_f[:, s, :], ident[:])
                P.close(last, ctx + ".maskT")
                t = P.open(pe, ctx + ".pad")
                pe.wait_ge(ev(ctx + ".padrow"), 1)
                for s in range(G):
                    last = pe.matmul(t[:, s:s + 1], pad_row[:, col(s)], ones_row[:, 0:1], start=True, stop=True)
                P.close(last, ctx + ".pad")
                t = P.open(pe, ctx + ".nT")
                pe.wait_ge(ev(ctx + ".n"), 1)
                for s in range(G):
                    last = pe.transpose(t[:, col(s)], scratch[:, col(s)], ident[:])
                P.close(last, ctx + ".nT")

            def ctx_act(act, q):
                act.wait_ge(s_ctx, 48)
                for s in range(G):
                    last = act.activation(scratch[:, N + s * L:N + (s + 1) * L], ctx_tok[:, s, :], ACT.Square,
                                          accum_out=rms[:, s:s + 1])
                last.then_inc(ev(ctx + ".sq"), 1)
                act.wait_ge(ev(ctx + ".sq"), 1)
                act.activation(rms2[:], rms[:], ACT.Sqrt, scale=1.0 / D, bias=eps6[:]).then_inc(ev(ctx + ".rms"), 1)
                t = P.take(act, ctx + ".T")
                P.give(act.copy(ctxT[:], t), ctx + ".T")
                t = P.take(act, ctx + ".maskT")
                P.give(act.copy(maskT_bf[:].rearrange("p s f -> p (s f)"), t), ctx + ".maskT")
                t = P.take(act, ctx + ".pad")
                P.give(act.copy(pad_col[:], t[:, 0:G]), ctx + ".pad")
                t = P.take(act, ctx + ".nT")
                P.give(act.copy(ctxnT[:], t), ctx + ".nT")

            def ctx_dve(dve, q):
                dve.wait_ge(s_ctx, 48)
                dve.tensor_scalar(mask_f[:], mask_i[:], -1.0, None, ALU.add).then_inc(ev(ctx + ".maskf"), 1)
                dve.tensor_scalar(pad_row[:], pad_row_u8[:], -1.0, BIG, ALU.add, ALU.mult).then_inc(ev(ctx + ".padrow"), 1)
                dve.wait_ge(ev(ctx + ".maskf"), 1)
                q.link(dve.tensor_copy(mask_bf[:], mask_f[:]))
                dve.wait_ge(ev(ctx + ".padrow"), 1)
                q.link(dve.tensor_copy(pad_wide[0:1, :], pad_row[:]))
                dve.wait_ge(ev(ctx + ".rms"), 1)
                q.link(dve.reciprocal(rstd[:], rms2[:]))
                for s in range(G):
                    last = dve.tensor_scalar(scratch[:, col(s)], ctx_tok[:, s, :], rstd[:, s:s + 1], None, ALU.mult)
                last.then_inc(ev(ctx + ".n"), 1)
                P.wait_given(dve, ctx + ".T")
                q.link(dve.reduce_sum(ctx_sum[:], row_tiles(ctxT[:]), X))
                P.wait_given(dve, ctx + ".nT")

            def attention16(nm, w, src=None, bias=False, bias_out=False, rope=False, mask=None):
                base = share(sum=2 if rope else 0)
                at = stacks.setdefault(nm, len(stacks))
                S = Scratch(scratch)
                qk = [S.take(N) for _ in range(2)]
                rest = [S.take(N) for _ in range(2)]
                parts = [S.take(3 * N, BF16).rearrange("p (k t) -> p k t", k=3) for _ in range(2)]
                stack = [S.take(NH // 2 * N, BF16).rearrange("p (a t) -> p a t", t=N) for _ in range(2)]
                pT_flat = S.take(2 * NH * L)
                pT = pT_flat.rearrange("p (b j f) -> p b j f", b=2, j=NJ)
                vaug = S.take(G * NH * (DH + 1)).rearrange("p (s h e) -> p s h e", s=G, h=NH)
                negm, mrest = (S.take(G * NH).rearrange("p (s h) -> p s h", s=G) for _ in range(2))
                mparts = S.take(N, BF16).rearrange("p (s f) -> p s f", s=G)
                mT = S.take(N, BF16)
                rden = S.take(G * NH).rearrange("p (s h) -> p s h", s=G)
                osb = S.take(N)
                oT = S.take(N)
                rq = [pT_flat[:, k * N:(k + 1) * N] for k in range(4)]
                src_ap = ctxT if src == "ctx" else hT

                def head_of(j, i):
                    return 8 * (j // 2) + 2 * i + j % 2

                def masking(pe, t, turned, s):
                    v = row_tiles(t)
                    last = None
                    if mask == "causal":
                        last = pe.matmul(v, ident_bf[:], spread((causal_T_bf if turned else causal_bf)[:], NI),
                                         start=False, stop=not turned, skip_group_check=True)
                    if mask == "given":
                        for c in (ident_big, ident_small):
                            last = pe.matmul(v, c[:], spread((maskT_bf if turned else mask_bf)[:, s, :], NI), start=False,
                                             stop=c is ident_small and not turned, skip_group_check=True)
                    return last

                def pe_f(pe):
                    yield from norm_pe(pe, nm)
                    yield 5
                    P.wait_given(pe, nm + ".hT")
                    todo = [("q", "Wq", hT), ("k", "Wk", src_ap)]
                    if rope:
                        todo = [("q", "Wq", hT), ("qs", "Wq_swap", hT), ("k", "Wk", hT), ("ks", "Wk_swap", hT)]
                    for name, wn, s_ in todo:
                        t = P.open(pe, f"{nm}.{name}")
                        P.close(pe.matmul(t, W[w + wn][:], s_[:], start=True, stop=True), f"{nm}.{name}")
                    t = P.open(pe, nm + ".v")
                    if bias:
                        bias_row(pe, t, W[w + "bv"][:])
                    for s in range(G):
                        last = pe.matmul(t[:, col(s)], src_ap[:, col(s)], W[w + "Wv"][:], start=not bias, stop=True,
                                         skip_group_check=True)
                    P.close(last, nm + ".v")

                    def products(s, letter, lhs, rhs, close):
                        for jj in range(0, NJ, 2):
                            t = [P.open(pe, f"{nm}.{letter}{s}{jj + par}", width=NI * L) for par in range(2)]
                            for i in range(NI):
                                for par in range(2):
                                    h = head_of(jj + par, i)
                                    r = slice(64 * par, 64 * par + 48)
                                    last = pe.matmul(t[par][:, i * L:(i + 1) * L], lhs[r, h // 2, col(s)],
                                                     rhs[r, h // 2, col(s)], start=i == 0, stop=close,
                                                     skip_group_check=True)
                                    if close and i == NI - 1:
                                        P.close(last, f"{nm}.{letter}{s}{jj + par}")

                    def scores(s):
                        if s == 0:
                            pe.wait_ge(s_stack, 16 * 4 * len(SLOTS) * (at + 1))
                        products(s, "S", stack[0], stack[1], mask is None)
                        if mask:
                            for j in range(NJ):
                                P.close(masking(pe, P.bank(f"{nm}.S{s}{j}"), False, s), f"{nm}.S{s}{j}")

                    def turned(s):
                        products(s, "T", stack[1], stack[0], False)
                        pe.wait_ge(ev(f"{u}.mparts"), G * at + s + 1)
                        t = P.open(pe, f"{nm}.mT{s}")
                        P.close(pe.transpose(t.bitcast(BF16)[:, 0:L], mparts[:, s, :], ident_bf[:]), f"{nm}.mT{s}")
                        for j in range(NJ):
                            masking(pe, P.bank(f"{nm}.T{s}{j}"), True, s)
                        P.wait_given(pe, f"{nm}.mT{s}")
                        for j in range(NJ):
                            t = P.bank(f"{nm}.T{s}{j}")
                            for i in range(NI):
                                a = NI * j + i
                                last = pe.matmul(t[:, i * L:(i + 1) * L], sel_part[:, a:a + 1].broadcast_to([128, 128]),
                                                 mT[:, col(s)], start=False, stop=i == NI - 1, skip_group_check=True)
                            P.close(last, f"{nm}.T{s}{j}")

                    def values(s):
                        if s == 0:
                            P.wait_given(pe, nm + ".v")
                            pe.wait_ge(ev(f"{u}.ones"), 2 * at + 1)
                        t = P.open(pe, f"{nm}.O{s}")
                        for j in range(NJ):
                            P.wait_given(pe, f"{nm}.T{s}{j}")
                            for i in range(NI):
                                h = head_of(j, i)
                                last = pe.matmul(t[:, h * 9:h * 9 + 9], pT[:, s % 2, j, i * L:(i + 1) * L],
                                                 vaug[:, s, h, :], start=True, stop=True, skip_group_check=True)
                        P.close(last, f"{nm}.O{s}")

                    for step in range(G + 2):
                        yield 22 + 6 * step
                        if step < G:
                            scores(step)
                        if step >= 2:
                            values(step - 2)
                        if 1 <= step <= G:
                            turned(step - 1)
                    yield 22 + 6 * (G + 2)
                    t = P.open(pe, nm + ".oT")
                    for s in range(G):
                        P.wait_given(pe, f"{nm}.O{s}")
                        last = pe.transpose(t[:, col(s)], osb[:, col(s)], ident[:])
                    P.close(last, nm + ".oT")
                    yield 24 + 6 * (G + 2)
                    P.wait_given(pe, nm + ".oT")
                    t = P.open(pe, nm + ".y", ACC)
                    if bias_out:
                        bias_row(pe, t, W[w + "bo"][:])
                    for s in range(G):
                        last = pe.matmul(t[:, col(s)], oT[:, col(s)], W[w + "Wo"][:], start=not bias_out, stop=True,
                                         skip_group_check=True)
                    P.close(last, nm + ".y")

                def act_f(act, q):
                    yield from norm_act(act, nm)
                    yield 5
                    if not rope:
                        t = P.take(act, nm + ".q")
                        bq = W[w + "bq"][:] if bias else 0.0
                        P.give(act.activation(qk[0], t, ACT.Identity, bias=bq), nm + ".q")
                    for k in range(2):
                        if rope:
                            act.wait_ge(ev(f"{u}.sum"), base["sum"] + k + 1)
                        else:
                            P.wait_given(act, f"{nm}.{'qk'[k]}")
                        act.copy(parts[k][:, 0, :], qk[k]).then_inc(ev(f"{u}.part1"), 1)
                    for k in range(2):
                        act.wait_ge(ev(f"{u}.rest"), 2 * at + k + 1)
                        act.copy(parts[k][:, 1, :], rest[k]).then_inc(ev(f"{u}.part2"), 1)
                    t = P.take(act, nm + ".v")
                    P.give(act.copy(vaug[:, :, :, 0:DH], t.rearrange("p (s h e) -> p s h e", s=G, h=NH)), nm + ".v")
                    for s in range(G):
                        yield 22 + 6 * (s + 1)
                        t = P.take(act, f"{nm}.mT{s}")
                        P.give(act.copy(mT[:, col(s)], t.bitcast(BF16)[:, 0:L]), f"{nm}.mT{s}")
                        if s >= 2:
                            P.take(act, f"{nm}.O{s - 2}")
                        for j in range(NJ):
                            t = P.take(act, f"{nm}.T{s}{j}")
                            P.give(act.activation(pT[:, s % 2, j, :], t, ACT.Exp), f"{nm}.T{s}{j}")
                    yield 22 + 6 * (G + 2)
                    t = P.take(act, nm + ".oT")
                    P.give(act.copy(oT, t), nm + ".oT")

                def dve_f(dve, q):
                    norm_dve(dve, q, nm)
                    yield 5
                    if rope:
                        for k, name in enumerate(("q", "qs", "k", "ks")):
                            t = P.take(dve, f"{nm}.{name}")
                            P.give(dve.tensor_tensor(row_tiles(rq[k]), row_tiles(t), spread(W["rope2"][:, k, :], G),
                                                     ALU.mult), f"{nm}.{name}")
                            if k % 2:
                                P.wait_given(dve, f"{nm}.{name}")
                                dve.tensor_tensor(qk[k // 2], rq[k - 1], rq[k], ALU.add).then_inc(ev(f"{u}.sum"), 1)
                    else:
                        t = P.take(dve, nm + ".k")
                        if bias:
                            ins = dve.tensor_scalar(qk[1], t, W[w + "bk"][:], SCALE16, ALU.add, ALU.mult)
                        else:
                            ins = dve.tensor_scalar(qk[1], t, SCALE16, None, ALU.mult)
                        P.give(ins, nm + ".k")
                    for k in range(2):
                        dve.wait_ge(ev(f"{u}.part1"), 2 * at + k + 1)
                        dve.tensor_tensor(rest[k], qk[k], parts[k][:, 0, :], ALU.subtract).then_inc(ev(f"{u}.rest"), 1)
                    for k in range(2):
                        dve.wait_ge(ev(f"{u}.part2"), 2 * at + k + 1)
                        dve.tensor_tensor(parts[k][:, 2, :], rest[k], parts[k][:, 1, :],
                                          ALU.subtract).then_inc(ev(f"{u}.part3"), 1)
                    yield 22
                    dve.wait_ge(ev(f"{u}.ones"), 2 * at + 2)

                    def maxima(s):
                        for j in range(NJ):
                            t = P.take(dve, f"{nm}.S{s}{j}")
                            P.give(dve.tensor_reduce(negm[:, s, NI * j:NI * j + NI], row_tiles(t), X, ALU.max,
                                                     negate=True), f"{nm}.S{s}{j}")
                        P.wait_given(dve, f"{nm}.S{s}{NJ - 1}")
                        m, r = negm[:, s, :], mrest[:, s, :]
                        q.link(dve.tensor_copy(mparts[:, s, 0:NH], m))
                        q.link(dve.tensor_tensor(r, m, mparts[:, s, 0:NH], ALU.subtract))
                        q.link(dve.tensor_copy(mparts[:, s, 32:32 + NH], r))
                        dve.tensor_tensor(mparts[:, s, 64:64 + NH], r, mparts[:, s, 32:32 + NH],
                                          ALU.subtract).then_inc(ev(f"{u}.mparts"), 1)

                    def divide(s):
                        t = P.take(dve, f"{nm}.O{s}")[:, 0:NH * 9].rearrange("p (h e) -> p h e", h=NH)
                        q.link(dve.reciprocal(rden[:, s, :], t[:, :, DH]))
                        P.give(dve.tensor_tensor(osb[:, col(s)].rearrange("p (h e) -> p h e", h=NH), t[:, :, 0:DH],
                                                 spread(rden[:, s, :], DH, 2), ALU.mult), f"{nm}.O{s}")

                    for step in range(G + 2):
                        yield 22 + 6 * step
                        if step < G:
                            maxima(step)
                        if step >= 2:
                            divide(step - 2)
                    yield 24 + 6 * (G + 2)
                    residual_dve(dve, q, nm + ".y")

                def pool_f(pool, q):
                    pool.wait_ge(ev(f"{u}.hn"), G * norm(nm) + 1)
                    pool.memset(vaug[:, :, :, DH:DH + 1], 1.0).then_inc(ev(f"{u}.ones"), 1)
                    pool.memset(mparts, 0.0).then_inc(ev(f"{u}.ones"), 1)

                def sp_f(sp):
                    yield 5
                    for part in range(3):
                        for k in range(2):
                            sp.wait_ge(ev(f"{u}.part{part + 1}"), 2 * at + k + 1)
                            sp.dma_start(stack_d[k][part], parts[k][:, part, :]).then_inc(s_stored[part], 16)
                    yield 9
                    for part in range(3):
                        sp.wait_ge(s_stored[part], 32 * (at + 1))
                        for slot, of in enumerate(SLOTS):
                            for k in range(2):
                                if of[k] != part:
                                    continue
                                for par in range(2):
                                    r = 64 * par + 8 * slot
                                    sp.dma_start(stack[k][r:r + DH], stack_d[k][part].rearrange(
                                        "(a b r) t -> b r a t", b=2, r=DH)[par]).then_inc(s_stack, 16)

                return pe_f, act_f, dve_f, pool_f, sp_f

            def nothing(*_):
                pass

            def ffn(nm):
                S = Scratch(scratch)
                nch = FFH // 128
                act_out = S.take(nch * N).rearrange("p (c t) -> p c t", c=nch)
                hid = S.take(nch * N).rearrange("p (c t) -> p c t", c=nch)

                def pe_f(pe):
                    yield from norm_pe(pe, nm)
                    yield 5
                    P.wait_given(pe, nm + ".hT")
                    for c in range(nch):
                        for k in ("gate", "up"):
                            t = P.open(pe, f"{nm}.{k}{c}")
                            P.close(pe.matmul(t, fw[k][:, c * 128:(c + 1) * 128], hT[:], start=True, stop=True),
                                    f"{nm}.{k}{c}")
                    yield 10
                    for c in range(nch):
                        P.wait_given(pe, f"{nm}.up{c}")
                    t = P.open(pe, nm + ".y", ACC)
                    for s in range(G):
                        for c in range(nch):
                            last = pe.matmul(t[:, col(s)], hid[:, c, col(s)], fw["down"][:, c, :], start=c == 0,
                                             stop=c == nch - 1, skip_group_check=True)
                    P.close(last, nm + ".y")

                def act_f(act, q):
                    yield from norm_act(act, nm)
                    yield 5
                    for c in range(nch):
                        t = P.take(act, f"{nm}.gate{c}")
                        P.give(act.activation(act_out[:, c, :], t, ACT.Silu), f"{nm}.gate{c}")

                def dve_f(dve, q):
                    norm_dve(dve, q, nm)
                    yield 5
                    for c in range(nch):
                        P.wait_given(dve, f"{nm}.gate{c}")
                        t = P.take(dve, f"{nm}.up{c}")
                        P.give(dve.tensor_tensor(hid[:, c, :], act_out[:, c, :], t, ALU.mult), f"{nm}.up{c}")
                    yield 10
                    residual_dve(dve, q, nm + ".y")

                return pe_f, act_f, dve_f, nothing, nothing

            def mixer(nm):
                S = Scratch(scratch)
                mean_wide = S.take(N)

                def pe_f(pe):
                    yield from norm_pe(pe, nm)
                    yield 5
                    P.wait_given(pe, nm + ".hT")
                    t = P.open(pe, nm + ".y", ACC)
                    bias_row(pe, t, W["m_b"][:])
                    pe.wait_ge(ev(nm + ".mean"), 1)
                    for s in range(G):
                        pe.matmul(t[:, col(s)], hT[:, col(s)], W["m_W1"][:], start=False, stop=False,
                                  skip_group_check=True)
                        last = pe.matmul(t[:, col(s)], mean_wide[:, col(s)], W["m_W2"][:], start=False, stop=True,
                                         skip_group_check=True)
                    P.close(last, nm + ".y")

                def act_f(act, q):
                    yield from norm_act(act, nm)

                def dve_f(dve, q):
                    norm_dve(dve, q, nm)
                    yield 5
                    dve.tensor_scalar(row_tiles(mean_wide), spread(ctx_sum[:], L, 2), 1.0 / L, None,
                                      ALU.mult).then_inc(ev(nm + ".mean"), 1)
                    residual_dve(dve, q, nm + ".y")

                return pe_f, act_f, dve_f, nothing, nothing

            def first_max(dve, q, onehot, values, top, tmp, width):
                q.link(dve.tensor_reduce(top, values, X, ALU.max))
                q.link(dve.tensor_tensor(tmp, values, spread(top, width, 2), ALU.is_ge))
                q.link(dve.tensor_tensor(tmp, tmp, spread(W["rev"][:, 0:width], G), ALU.mult))
                q.link(dve.tensor_reduce(rms[:], tmp, X, ALU.max))
                q.link(dve.tensor_tensor(onehot, tmp, spread(rms[:], width, 2), ALU.is_equal))

            def gates_pe(pe, nm, gate, width, base):
                pe.wait_ge(ev(f"{u}.gate"), base["gate"] + 1)
                t = P.open(pe, nm + ".gT")
                for s in range(G):
                    last = pe.transpose(t[0:width, col(s)], gate[:, s, :], ident[:])
                P.close(last, nm + ".gT")

            def router_pe(pe, nm, w, width):
                t = P.open(pe, nm + ".router")
                for s in range(G):
                    last = pe.matmul(t[:, s * width:(s + 1) * width], hT[:, col(s)], w, start=True, stop=True,
                                     skip_group_check=True)
                P.close(last, nm + ".router")

            def moe1(nm):
                S = Scratch(scratch)
                base = share(diff=1, exp=1, gate=1, down=len(SCH) + C1 - 1)
                RING = 3
                lg, lg2, oh1, oh2, tmp, gate = (S.take(G * E1).rearrange("p (s e) -> p s e", s=G) for _ in range(6))
                top1, top2, p1, p2, ex = (S.take(G) for _ in range(5))
                gT = S.take(N)
                a_out = S.take(RING * N).rearrange("p (r t) -> p r t", r=RING)
                h_mid = S.take(RING * N).rearrange("p (r t) -> p r t", r=RING)
                hid = S.take(RING * N).rearrange("p (r t) -> p r t", r=RING)
                chunks = [(None, c, r0, rows) for c, (r0, rows) in enumerate(SCH)] + \
                         [("e", c, c * 128, 128) for c in range(C1)]

                def pe_f(pe):
                    yield from norm_pe(pe, nm)
                    yield 5
                    P.wait_given(pe, nm + ".hT")
                    router_pe(pe, nm, W["e1_Wg"][:], E1)

                    def up(n):
                        kind, c, r0, rows = chunks[n]
                        for k, (wa, wb) in enumerate((("e1_Ws1", "e1_W1"), ("e1_Ws2", "e1_W2"))):
                            t = P.open(pe, f"{nm}.u{k}{n}")
                            w = W[wb if kind else wa]
                            P.close(pe.matmul(t[0:rows, :], w[:, r0:r0 + rows], hT[:], start=True, stop=True),
                                    f"{nm}.u{k}{n}")
                        if kind:
                            if c == 0:
                                gates_pe(pe, nm, gate, E1, base)
                                P.wait_given(pe, nm + ".gT")
                            t = P.open(pe, f"{nm}.g{n}")
                            P.close(pe.matmul(t, W["sel1"][:, r0:r0 + 128], gT[0:E1, :], start=True, stop=True),
                                    f"{nm}.g{n}")

                    def down(n):
                        kind, c, r0, rows = chunks[n]
                        P.wait_given(pe, f"{nm}.g{n}" if kind else f"{nm}.u1{n}")
                        w = W["e1_W3" if kind else "e1_Ws3"]
                        for s in range(G):
                            last = pe.matmul(acc[:, col(s)], hid[0:rows, n % RING, col(s)], w[0:rows, c, :],
                                             start=n == 0 and s == 0, stop=n == len(chunks) - 1, skip_group_check=True)
                        if n < len(chunks) - 1:
                            last.then_inc(ev(f"{u}.down"), 1)
                        return last

                    acc = P.open(pe, nm + ".y", ACC)
                    for n in range(len(chunks) + 1):
                        yield CH1 * n + 8
                        if n < len(chunks):
                            up(n)
                        if n >= 1:
                            last = down(n - 1)
                    P.close(last, nm + ".y")

                def act_f(act, q):
                    yield from norm_act(act, nm)
                    yield 5
                    act.wait_ge(ev(f"{u}.diff"), base["diff"] + 1)
                    act.activation(ex, p1, ACT.Exp).then_inc(ev(f"{u}.exp"), 1)
                    for n, (kind, c, r0, rows) in enumerate(chunks):
                        yield CH1 * n + 8
                        t = P.take(act, f"{nm}.u0{n}")
                        if n >= RING:
                            P.wait_given(act, f"{nm}.u1{n - RING}")
                        P.give(act.activation(a_out[0:rows, n % RING, :], t[0:rows, :], ACT.Silu), f"{nm}.u0{n}")
                        if kind and c == 0:
                            t = P.take(act, nm + ".gT")
                            P.give(act.copy(gT[0:E1, :], t[0:E1, :]), nm + ".gT")

                def dve_f(dve, q):
                    norm_dve(dve, q, nm)
                    yield 5
                    t = P.take(dve, nm + ".router")
                    P.give(dve.tensor_copy(lg, t[:, 0:G * E1].rearrange("p (s e) -> p s e", s=G)), nm + ".router")
                    P.wait_given(dve, nm + ".router")
                    first_max(dve, q, oh1, lg, top1, tmp, E1)
                    q.link(dve.scalar_tensor_tensor(out=lg2, in0=oh1, scalar=-BIG, in1=lg, op0=ALU.mult, op1=ALU.add))
                    first_max(dve, q, oh2, lg2, top2, tmp, E1)
                    dve.tensor_tensor(p1, top2, top1, ALU.subtract).then_inc(ev(f"{u}.diff"), 1)
                    dve.wait_ge(ev(f"{u}.exp"), base["exp"] + 1)
                    q.link(dve.tensor_scalar(p1, ex, 1.0, None, ALU.add))
                    q.link(dve.reciprocal(p1, p1))
                    q.link(dve.tensor_tensor(p2, p1, ex, ALU.mult))
                    q.link(dve.tensor_tensor(oh1, oh1, spread(p1, E1, 2), ALU.mult))
                    q.link(dve.tensor_tensor(oh2, oh2, spread(p2, E1, 2), ALU.mult))
                    dve.tensor_tensor(gate, oh1, oh2, ALU.add).then_inc(ev(f"{u}.gate"), 1)
                    for n, (kind, c, r0, rows) in enumerate(chunks):
                        yield CH1 * n + 8
                        P.wait_given(dve, f"{nm}.u0{n}")
                        t = P.take(dve, f"{nm}.u1{n}")
                        if n >= RING:
                            dve.wait_ge(ev(f"{u}.down"), base["down"] + n - RING + 1)
                        dst = h_mid if kind else hid
                        P.give(dve.tensor_tensor(dst[0:rows, n % RING, :], a_out[0:rows, n % RING, :], t[0:rows, :],
                                                 ALU.mult), f"{nm}.u1{n}")
                        if kind:
                            P.wait_given(dve, f"{nm}.u1{n}")
                            t = P.take(dve, f"{nm}.g{n}")
                            P.give(dve.tensor_tensor(hid[:, n % RING, :], h_mid[:, n % RING, :], t, ALU.mult),
                                   f"{nm}.g{n}")
                    yield CH1 * len(chunks) + 8
                    residual_dve(dve, q, nm + ".y")

                return pe_f, act_f, dve_f, nothing, nothing

            def moe2(nm):
                S = Scratch(scratch)
                base = share(diff=1, exp=1, gate=1)
                RING = 3
                lg, oh, tmp, gate = (S.take(G * E2).rearrange("p (s e) -> p s e", s=G) for _ in range(4))
                top, den = S.take(G), S.take(G)
                gT = S.take(N)
                hid = S.take(RING * 2 * N).rearrange("p (r c t) -> p r c t", r=RING, c=2)
                w1 = experts[:, 0:E2 * F2]
                w2 = experts[:, E2 * F2:2 * E2 * F2].rearrange("p (c f) -> p c f", f=D)

                def pe_f(pe):
                    yield from norm_pe(pe, nm)
                    yield 5
                    P.wait_given(pe, nm + ".hT")
                    router_pe(pe, nm, W["e2_Wr"][:], E2)
                    pe.wait_ge(s_e2, 32)

                    def up(e):
                        for c in range(2):
                            t = P.open(pe, f"{nm}.u{e}.{c}")
                            f0 = e * F2 + c * 128
                            P.close(pe.matmul(t, w1[:, f0:f0 + 128], hT[:], start=True, stop=True), f"{nm}.u{e}.{c}")

                    def down(e):
                        P.wait_given(pe, f"{nm}.u{e}.0")
                        P.wait_given(pe, f"{nm}.u{e}.1")
                        t = P.open(pe, f"{nm}.d{e}")
                        for s in range(G):
                            for c in range(2):
                                last = pe.matmul(t[:, col(s)], hid[:, e % RING, c, col(s)], w2[:, 2 * e + c, :],
                                                 start=c == 0, stop=c == 1, skip_group_check=True)
                        P.close(last, f"{nm}.d{e}")

                    for e in range(E2 + 1):
                        yield CH2 * e + 8
                        if e < E2:
                            up(e)
                        if e >= 1:
                            down(e - 1)
                    yield CH2 * E2 + 10
                    gates_pe(pe, nm, gate, E2, base)
                    P.wait_given(pe, nm + ".gT")
                    t = P.open(pe, nm + ".y", ACC)
                    for s in range(G):
                        last = pe.matmul(t[:, col(s)], gT[0:E2, col(s)], W["e2_b2"][:], start=True, stop=True,
                                         skip_group_check=True)
                    P.close(last, nm + ".y")

                def act_f(act, q):
                    yield from norm_act(act, nm)
                    yield 5
                    act.wait_ge(ev(f"{u}.diff"), base["diff"] + 1)
                    act.activation(lg, tmp, ACT.Exp).then_inc(ev(f"{u}.exp"), 1)
                    for e in range(E2):
                        yield CH2 * e + 8
                        for c in range(2):
                            t = P.take(act, f"{nm}.u{e}.{c}")
                            if e >= RING and c == 0:
                                P.take(act, f"{nm}.d{e - RING}")
                                P.take(act, f"{nm}.u{e}.{c}")
                            P.give(act.activation(hid[:, e % RING, c, :], t, ACT.Gelu,
                                                  bias=W["e2_b1"][:, 2 * e + c:2 * e + c + 1]), f"{nm}.u{e}.{c}")
                    yield CH2 * E2 + 10
                    t = P.take(act, nm + ".gT")
                    P.give(act.copy(gT[0:E2, :], t[0:E2, :]), nm + ".gT")

                def dve_f(dve, q):
                    norm_dve(dve, q, nm)
                    yield 5
                    t = P.take(dve, nm + ".router")
                    P.give(dve.tensor_copy(lg, t[:, 0:G * E2].rearrange("p (s e) -> p s e", s=G)), nm + ".router")
                    P.wait_given(dve, nm + ".router")
                    first_max(dve, q, oh, lg, top, tmp, E2)
                    dve.tensor_tensor(tmp, lg, spread(top, E2, 2), ALU.subtract).then_inc(ev(f"{u}.diff"), 1)
                    dve.wait_ge(ev(f"{u}.exp"), base["exp"] + 1)
                    q.link(dve.tensor_reduce(den, lg, X, ALU.add))
                    q.link(dve.reciprocal(den, den))
                    dve.tensor_tensor(gate, oh, spread(den, E2, 2), ALU.mult).then_inc(ev(f"{u}.gate"), 1)
                    dve.wait_ge(ev(f"{u}.gate"), base["gate"] + 1)
                    for e in range(E2):
                        yield CH2 * (e + 1) + 8
                        t = P.take(dve, f"{nm}.d{e}")
                        for s in range(G):
                            ins = dve.scalar_tensor_tensor(out=xres[:, s, :], in0=t[:, col(s)],
                                                           scalar=gate[:, s, e:e + 1], in1=xres[:, s, :],
                                                           op0=ALU.mult, op1=ALU.add)
                        P.give(ins, f"{nm}.d{e}")
                        P.wait_given(dve, f"{nm}.d{e}")
                    yield CH2 * E2 + 10
                    residual_dve(dve, q, nm + ".y")

                return pe_f, act_f, dve_f, nothing, nothing

            def moe3(nm):
                S = Scratch(scratch)
                base = share(diff=1, exp=1, gate=1, down=E3 * (F3 // 128) - 1)
                XR, RING = 2, 4
                nch = F3 // 128
                lg, oh, tmp, gate, rank = (S.take(G * E3).rearrange("p (s e) -> p s e", s=G) for _ in range(5))
                top, den, mine = S.take(G), S.take(G), S.take(G)
                gT = S.take(N)
                xg = S.take(XR * N).rearrange("p (r t) -> p r t", r=XR)
                hid = S.take(RING * N).rearrange("p (r t) -> p r t", r=RING)
                w1 = experts[:, 0:E3 * F3]
                w2 = experts[:, E3 * F3:].rearrange("p (c f) -> p c f", f=D)
                nall = E3 * nch
                assert nch == RING

                def pe_f(pe):
                    yield from norm_pe(pe, nm)
                    yield 5
                    P.wait_given(pe, nm + ".hT")
                    router_pe(pe, nm, W["e3_Wr"][:], E3)
                    pe.wait_ge(ev(f"{u}.diff"), base["diff"] + 1)
                    t = P.open(pe, nm + ".rank")
                    for s in range(G):
                        for k in range(s):
                            pe.matmul(t[:, s * E3:(s + 1) * E3], ones_sq[:], oh[:, k, :], start=k == 0, stop=False,
                                      skip_group_check=True)
                        pe.matmul(t[:, s * E3:(s + 1) * E3], W["before_T"][:], oh[:, s, :], start=s == 0, stop=True,
                                  skip_group_check=True)
                    for k in range(G):
                        last = pe.matmul(t[:, G * E3:(G + 1) * E3], ones_sq[:], oh[:, k, :], start=k == 0,
                                         stop=k == G - 1, skip_group_check=True)
                    P.close(last, nm + ".rank")
                    gates_pe(pe, nm, gate, E3, base)
                    P.wait_given(pe, nm + ".gT")
                    pe.wait_ge(s_e3, 32)

                    def feed(e):
                        t = P.open(pe, f"{nm}.g{e}")
                        P.close(pe.matmul(t, ident[0:E3, e:e + 1].broadcast_to([E3, 128]), gT[0:E3, :],
                                          start=True, stop=True), f"{nm}.g{e}")

                    def up(n):
                        e = n // nch
                        if n % nch == 0:
                            P.wait_given(pe, f"{nm}.g{e}")
                        t = P.open(pe, f"{nm}.u{n}")
                        P.close(pe.matmul(t, w1[:, n * 128:(n + 1) * 128], xg[:, e % XR, :], start=True, stop=True),
                                f"{nm}.u{n}")

                    def down(n):
                        P.wait_given(pe, f"{nm}.u{n}")
                        for s in range(G):
                            last = pe.matmul(acc[:, col(s)], hid[:, n % RING, col(s)], w2[:, n, :],
                                             start=n == 0 and s == 0, stop=n == nall - 1, skip_group_check=True)
                        if n < nall - 1:
                            last.then_inc(ev(f"{u}.down"), 1)
                        return last

                    yield 12
                    acc = P.open(pe, nm + ".y", ACC)
                    feed(0)
                    for n in range(nall + 2):
                        yield CH3 * n + 12
                        if n < nall:
                            if n % nch == 1 and n // nch + 1 < E3:
                                feed(n // nch + 1)
                            up(n)
                        if n >= 2:
                            last = down(n - 2)
                    P.close(last, nm + ".y")

                def act_f(act, q):
                    yield from norm_act(act, nm)
                    yield 5
                    act.wait_ge(ev(f"{u}.diff"), base["diff"] + 1)
                    act.activation(lg, tmp, ACT.Exp).then_inc(ev(f"{u}.exp"), 1)
                    t = P.take(act, nm + ".gT")
                    P.give(act.copy(gT[0:E3, :], t[0:E3, :]), nm + ".gT")
                    for n in range(0, nall, 2):
                        yield CH3 * n + 12
                        relu_chunk(act, n)

                def relu_chunk(eng, n):
                    if n >= RING:
                        eng.wait_ge(ev(f"{u}.down"), base["down"] + n - RING + 1)
                    t = P.take(eng, f"{nm}.u{n}")
                    if n % 2 == 0:
                        ins = eng.activation(hid[:, n % RING, :], t, ACT.Relu)
                    else:
                        ins = eng.tensor_scalar(hid[:, n % RING, :], t, 0.0, None, ALU.max)
                    P.give(ins, f"{nm}.u{n}")

                def dve_f(dve, q):
                    norm_dve(dve, q, nm)
                    yield 5
                    t = P.take(dve, nm + ".router")
                    P.give(dve.tensor_copy(lg, t[:, 0:G * E3].rearrange("p (s e) -> p s e", s=G)), nm + ".router")
                    P.wait_given(dve, nm + ".router")
                    first_max(dve, q, oh, lg, top, tmp, E3)
                    dve.tensor_tensor(tmp, lg, spread(top, E3, 2), ALU.subtract).then_inc(ev(f"{u}.diff"), 1)
                    dve.wait_ge(ev(f"{u}.exp"), base["exp"] + 1)
                    q.link(dve.tensor_reduce(den, lg, X, ALU.add))
                    q.link(dve.reciprocal(den, den))
                    t = P.take(dve, nm + ".rank")
                    q.link(dve.tensor_tensor(rank, t[:, 0:G * E3].rearrange("p (s e) -> p s e", s=G),
                                             spread(counts[:], G), ALU.add))
                    P.give(dve.tensor_tensor(counts[:], t[:, G * E3:(G + 1) * E3], counts[:], ALU.add), nm + ".rank")
                    q.link(dve.tensor_tensor(rank, rank, oh, ALU.mult))
                    q.link(dve.tensor_reduce(mine, rank, X, ALU.add))
                    q.link(dve.scalar_tensor_tensor(out=mine, in0=mine, scalar=float(CAP), in1=den, op0=ALU.is_lt,
                                                    op1=ALU.mult))
                    dve.tensor_tensor(gate, oh, spread(mine, E3, 2), ALU.mult).then_inc(ev(f"{u}.gate"), 1)

                    def feed(e):
                        t = P.take(dve, f"{nm}.g{e}")
                        if e >= XR:
                            P.take(dve, f"{nm}.u{(e - XR) * nch + nch - 1}")
                        P.give(dve.tensor_tensor(xg[:, e % XR, :], hT[:], t, ALU.mult), f"{nm}.g{e}")

                    yield 12
                    feed(0)
                    for n in range(nall):
                        yield CH3 * n + 12
                        if n % nch == 1 and n // nch + 1 < E3:
                            feed(n // nch + 1)
                        if n % 2 == 1:
                            relu_chunk(dve, n)
                    yield CH3 * (nall + 1) + 12
                    residual_dve(dve, q, nm + ".y")

                return pe_f, act_f, dve_f, nothing, nothing

            def cross3(nm):
                H3, DV = 4, 32
                S = Scratch(scratch)
                r = [S.take(N) for _ in range(4)]
                qT, kT = S.take(N), S.take(N)
                vaug = S.take(G * (DV + 1)).rearrange("p (s e) -> p s e", s=G)
                negm = S.take(N).rearrange("p (s h) -> p s h", s=G)
                mT = S.take(N)
                pT = S.take(2 * H3 * L).rearrange("p (b f) -> p b f", b=2)
                rden = S.take(G * H3).rearrange("p (s h) -> p s h", s=G)
                osb, oT = S.take(N), S.take(N)

                def pe_f(pe):
                    yield from norm_pe(pe, nm)
                    yield 5
                    P.wait_given(pe, nm + ".hT")
                    for name, wn, src in (("q", "Wq", hT), ("qs", "Wq_swap", hT), ("k", "Wk", ctxnT),
                                          ("ks", "Wk_swap", ctxnT)):
                        t = P.open(pe, f"{nm}.{name}")
                        P.close(pe.matmul(t, W["x3_" + wn][:], src[:], start=True, stop=True), f"{nm}.{name}")
                    t = P.open(pe, nm + ".v")
                    for s in range(G):
                        last = pe.matmul(t[:, s * DV:(s + 1) * DV], ctxnT[:, col(s)], W["x3_Wv"][:], start=True,
                                         stop=True, skip_group_check=True)
                    P.close(last, nm + ".v")
                    yield 10
                    pe.wait_ge(ev(nm + ".qk"), 1)

                    def scores(s):
                        for h in range(H3):
                            t = P.open(pe, f"{nm}.S{s}{h}")
                            rr = slice(32 * h, 32 * h + 32)
                            pe.matmul(t[:, 0:L], qT[rr, col(s)], kT[rr, col(s)], start=True, stop=False,
                                      skip_group_check=True)
                            P.close(pe.matmul(t[:, 0:L], ones_first[:], pad_wide[:, col(s)], start=False, stop=True,
                                              skip_group_check=True), f"{nm}.S{s}{h}")

                    def turned(s):
                        for h in range(H3):
                            P.wait_given(pe, f"{nm}.S{s}{h}")
                        t = P.open(pe, f"{nm}.mT{s}")
                        P.close(pe.transpose(t[:, 0:L], negm[:, s, :], ident[:]), f"{nm}.mT{s}")
                        P.wait_given(pe, f"{nm}.mT{s}")
                        for h in range(H3):
                            t = P.open(pe, f"{nm}.T{s}{h}")
                            rr = slice(32 * h, 32 * h + 32)
                            pe.matmul(t[:, 0:L], kT[rr, col(s)], qT[rr, col(s)], start=True, stop=False,
                                      skip_group_check=True)
                            P.close(pe.matmul(t[:, 0:L], ident[:, h:h + 1].broadcast_to([128, 128]), mT[:, col(s)],
                                              start=False, stop=True, skip_group_check=True), f"{nm}.T{s}{h}")

                    def values(s):
                        if s == 0:
                            P.wait_given(pe, nm + ".v")
                        t = P.open(pe, f"{nm}.O{s}")
                        for h in range(H3):
                            P.wait_given(pe, f"{nm}.T{s}{h}")
                            last = pe.matmul(t[:, h * (DV + 1):(h + 1) * (DV + 1)], pT[:, s % 2, h * L:(h + 1) * L],
                                             vaug[:, s, :], start=True, stop=True, skip_group_check=True)
                        P.close(last, f"{nm}.O{s}")

                    for step in range(G + 2):
                        yield 12 + 4 * step
                        if step < G:
                            scores(step)
                        if 1 <= step <= G:
                            turned(step - 1)
                        if step >= 2:
                            values(step - 2)
                    yield 12 + 4 * (G + 2)
                    t = P.open(pe, nm + ".oT")
                    for s in range(G):
                        P.wait_given(pe, f"{nm}.O{s}")
                        last = pe.transpose(t[:, col(s)], osb[:, col(s)], ident[:])
                    P.close(last, nm + ".oT")
                    yield 14 + 4 * (G + 2)
                    P.wait_given(pe, nm + ".oT")
                    t = P.open(pe, nm + ".y", ACC)
                    for s in range(G):
                        last = pe.matmul(t[:, col(s)], oT[:, col(s)], W["x3_Wo"][:], start=True, stop=True,
                                         skip_group_check=True)
                    P.close(last, nm + ".y")

                def act_f(act, q):
                    yield from norm_act(act, nm, True)
                    yield 5
                    t = P.take(act, nm + ".v")
                    P.give(act.copy(vaug[:, :, 0:DV], t[:, 0:G * DV].rearrange("p (s e) -> p s e", s=G)), nm + ".v")
                    for s in range(G):
                        yield 12 + 4 * (s + 1)
                        t = P.take(act, f"{nm}.mT{s}")
                        P.give(act.copy(mT[:, col(s)], t[:, 0:L]), f"{nm}.mT{s}")
                        if s >= 2:
                            P.take(act, f"{nm}.O{s - 2}")
                        for h in range(H3):
                            t = P.take(act, f"{nm}.T{s}{h}")
                            P.give(act.activation(pT[:, s % 2, h * L:(h + 1) * L], t[:, 0:L], ACT.Exp,
                                                  bias=pad_col[:, s:s + 1]), f"{nm}.T{s}{h}")
                    yield 12 + 4 * (G + 2)
                    t = P.take(act, nm + ".oT")
                    P.give(act.copy(oT, t), nm + ".oT")

                def dve_f(dve, q):
                    norm_dve(dve, q, nm, True)
                    yield 5
                    for k, name in enumerate(("q", "qs", "k", "ks")):
                        t = P.take(dve, f"{nm}.{name}")
                        P.give(dve.tensor_tensor(row_tiles(r[k]), row_tiles(t), spread(W["rope3"][:, k, :], G),
                                                 ALU.mult), f"{nm}.{name}")
                    dve.wait_ge(ev(nm + ".ones"), 2)
                    for step in range(G + 2):
                        yield 12 + 4 * step
                        if step < G:
                            s = step
                            for h in range(H3):
                                t = P.take(dve, f"{nm}.S{s}{h}")
                                P.give(dve.tensor_reduce(negm[:, s, h:h + 1], t[:, 0:L], X, ALU.max, negate=True),
                                       f"{nm}.S{s}{h}")
                        if step >= 2:
                            s = step - 2
                            t = P.take(dve, f"{nm}.O{s}")[:, 0:H3 * (DV + 1)].rearrange("p (h e) -> p h e", h=H3)
                            q.link(dve.reciprocal(rden[:, s, :], t[:, :, DV]))
                            P.give(dve.tensor_tensor(osb[:, col(s)].rearrange("p (h e) -> p h e", h=H3), t[:, :, 0:DV],
                                                     spread(rden[:, s, :], DV, 2), ALU.mult), f"{nm}.O{s}")
                    yield 14 + 4 * (G + 2)
                    residual_dve(dve, q, nm + ".y")

                def pool_f(pool, q):
                    pool.wait_ge(ev(f"{u}.hn"), G * norm(nm) + 1)
                    pool.memset(vaug[:, :, DV:DV + 1], 1.0).then_inc(ev(nm + ".ones"), 1)
                    pool.memset(negm[:, :, H3:], 0.0).then_inc(ev(nm + ".ones"), 1)
                    yield 5
                    for k, name in ((0, "q"), (1, "qs"), (2, "k"), (3, "ks")):
                        P.wait_given(pool, f"{nm}.{name}")
                    pool.tensor_tensor(qT, r[0], r[1], ALU.add)
                    pool.tensor_tensor(kT, r[2], r[3], ALU.add).then_inc(ev(nm + ".qk"), 1)

                return pe_f, act_f, dve_f, pool_f, nothing

            def mamba(nm):
                S = Scratch(scratch)
                base = share(zero=1, conv=2, sum=DS)
                xpad = S.take(2 * G * (L + 3)).rearrange("p (c s t) -> p c s t", c=2, s=G)
                xc, z, delta, du, pos, neg = (S.take(2 * N).rearrange("p (c t) -> p c t", c=2) for _ in range(6))
                dstart, yacc = neg, pos
                dtr = du
                RING = 2
                rings = S.take(4 * RING * 2 * N)
                decay, inp, state, yc = (rings[:, k * RING * 2 * N:(k + 1) * RING * 2 * N].rearrange(
                    "p (r j t) -> p r j t", r=RING, j=2) for k in range(4))
                ysum = S.take(4 * N).rearrange("p (c j t) -> p c j t", c=2, j=2)
                parts = S.take(4 * N, BF16).rearrange("p (k c t) -> p k c t", k=2, c=2)
                rest = rings[:, 0:4 * N].rearrange("p (k c t) -> p k c t", k=2, c=2)
                pairs = [(k, c) for c in range(2) for k in range(2)]
                steps = [(c, n) for c in range(2) for n in range(0, DS, 2)]

                def pe_f(pe):
                    yield from norm_pe(pe, nm)
                    yield 5
                    P.wait_given(pe, nm + ".hT")
                    for m in range(4):
                        t = P.open(pe, f"{nm}.in{m}")
                        P.close(pe.matmul(t, W["s_in"][:, m * 128:(m + 1) * 128], hT[:], start=True, stop=True),
                                f"{nm}.in{m}")
                    yield 9
                    for c in range(2):
                        pe.wait_ge(ev(nm + ".xc"), c + 1)
                        t = P.open(pe, f"{nm}.dtr{c}")
                        P.close(pe.matmul(t[0:2 * DS, :], W["s_x"][:, c * 32:c * 32 + 32], xc[:, c, :],
                                          start=True, stop=True), f"{nm}.dtr{c}")
                    for k, c in pairs:
                        t = P.open(pe, f"{nm}.rows{k}{c}")
                        P.close(pe.matmul(t[0:96, :], W["s_bc"][:, (k * 2 + c) * 96:(k * 2 + c) * 96 + 96], xc[:, c, :],
                                          start=True, stop=True), f"{nm}.rows{k}{c}")
                    for c in range(2):
                        P.wait_given(pe, f"{nm}.dtr{c}")
                        t = P.open(pe, f"{nm}.dt{c}")
                        P.close(pe.matmul(t, W["s_dt"][:, c * 128:(c + 1) * 128], dtr[0:2 * DS, c, :],
                                          start=True, stop=True), f"{nm}.dt{c}")
                    for c, n in steps:
                        yield 24 + CHS * (16 * c + n)
                        if n == 0:
                            pe.wait_ge(ev(nm + ".parts"), 1)
                        for k in (1, 2):
                            t = P.open(pe, f"{nm}.bc{k}.{c}.{n}", width=2 * N)
                            for j in range(2):
                                last = pe.matmul(t[:, j * N:(j + 1) * N], sel_state[:, n + j, :],
                                                 parts[0:96, k - 1, c, :], start=True, stop=True,
                                                 skip_group_check=True)
                            P.close(last, f"{nm}.bc{k}.{c}.{n}")
                    yield 25 + CHS * 32
                    pe.wait_ge(ev(nm + ".gated"), 1)
                    t = P.open(pe, nm + ".y", ACC)
                    for s in range(G):
                        for c in range(2):
                            last = pe.matmul(t[:, col(s)], yacc[:, c, col(s)], W["s_out"][:, c, :], start=c == 0,
                                             stop=c == 1, skip_group_check=True)
                    P.close(last, nm + ".y")

                def act_f(act, q):
                    yield from norm_act(act, nm)
                    yield 5
                    act.wait_ge(ev(f"{u}.zero"), base["zero"] + 1)
                    for c in range(2):
                        t = P.take(act, f"{nm}.in{c}")
                        P.give(act.copy(xpad[:, c, :, 3:], row_tiles(t)), f"{nm}.in{c}")
                    for c in range(2):
                        t = P.take(act, f"{nm}.in{2 + c}")
                        P.give(act.activation(z[:, c, :], t, ACT.Silu), f"{nm}.in{2 + c}")
                    for c in range(2):
                        act.wait_ge(ev(f"{u}.conv"), base["conv"] + c + 1)
                        act.activation(xc[:, c, :], delta[:, c, :], ACT.Silu,
                                       bias=W["s_conv_b"][:, c:c + 1]).then_inc(ev(nm + ".xc"), 1)
                    yield 9
                    for c in range(2):
                        t = P.take(act, f"{nm}.dtr{c}")
                        P.give(act.copy(dtr[0:2 * DS, c, :], t[0:2 * DS, :]), f"{nm}.dtr{c}")
                    for k, c in pairs:
                        t = P.take(act, f"{nm}.rows{k}{c}")
                        act.copy(parts[0:96, k, c, :], t[0:96, :]).then_inc(ev(nm + ".high"), 1)
                    act.wait_ge(ev(nm + ".high"), 4)
                    for k, c in pairs:
                        P.wait_given(act, f"{nm}.rows{k}{c}")
                    act.copy(parts[32:64], rest[32:64])
                    act.copy(parts[64:96], rest[64:96]).then_inc(ev(nm + ".high"), 1)
                    for c in range(2):
                        t = P.take(act, f"{nm}.dt{c}")
                        b = W["s_dt_b"][:, c:c + 1]
                        q.mark(act.activation(pos[:, c, :], t, ACT.Relu, bias=b))
                        P.give(act.activation(neg[:, c, :], t, ACT.Abs, bias=b), f"{nm}.dt{c}")
                    P.wait_given(act, nm + ".dt1")
                    q.link(act.activation(neg[:], neg[:], ACT.Exp, scale=-1.0))
                    act.activation(neg[:], neg[:], ACT.Ln, bias=ones_col[:]).then_inc(ev(nm + ".soft"), 1)
                    yield 24
                    act.wait_ge(ev(nm + ".start"), 1)
                    for k, (c, n) in enumerate(steps):
                        yield 24 + CHS * (16 * c + n)
                        if k >= RING:
                            act.wait_ge(ev(nm + ".state"), k - RING + 1)
                        for j in range(2):
                            ins = act.activation(decay[:, k % RING, j, :], dstart[:, c, :], ACT.Exp,
                                                 scale=ssm_A[:, c, n + j:n + j + 1])
                        ins.then_inc(ev(nm + ".decay"), 1)

                def dve_f(dve, q):
                    norm_dve(dve, q, nm)
                    yield 5
                    w = W["s_conv_w"]
                    for c in range(2):
                        P.wait_given(dve, f"{nm}.in{c}")
                    for k in range(CONV_K):
                        for c in range(2):
                            dst = row_tiles(delta[:, c, :])
                            src = xpad[:, c, :, k:k + L]
                            if k == 0:
                                ins = dve.tensor_scalar(dst, src, w[:, c, k:k + 1], None, ALU.mult)
                            else:
                                q.wait(m[c])
                                ins = dve.scalar_tensor_tensor(out=dst, in0=src, scalar=w[:, c, k:k + 1], in1=dst,
                                                               op0=ALU.mult, op1=ALU.add)
                            if k == 0 and c == 0:
                                m = [0, 0]
                            if k < CONV_K - 1:
                                m[c] = q.mark(ins)
                            else:
                                ins.then_inc(ev(f"{u}.conv"), 1)
                    yield 9
                    for n, (k, c) in enumerate(pairs):
                        dve.wait_ge(ev(nm + ".high"), n + 1)
                        t = P.take(dve, f"{nm}.rows{k}{c}")
                        P.give(dve.tensor_tensor(rest[0:96, k, c, :], t[0:96, :], parts[0:96, k, c, :], ALU.subtract),
                               f"{nm}.rows{k}{c}")
                    dve.wait_ge(ev(nm + ".high"), 5)
                    dve.tensor_tensor(parts[64:96], rest[64:96], parts[64:96],
                                      ALU.subtract).then_inc(ev(nm + ".parts"), 1)
                    dve.wait_ge(ev(nm + ".parts"), 1)
                    dve.wait_ge(ev(nm + ".soft"), 1)
                    q.link(dve.tensor_tensor(delta[:], pos[:], neg[:], ALU.add))
                    q.mark(dve.tensor_tensor(du[:], delta[:], xc[:], ALU.mult))
                    q.link(dve.tensor_copy(dstart[:], delta[:]))
                    dve.memset(dstart[:].rearrange("p c (s t) -> p c s t", s=G)[:, :, :, 0:1],
                               BIG).then_inc(ev(nm + ".start"), 1)
                    for k, (c, n) in enumerate(steps):
                        yield 24 + CHS * (16 * c + n)
                        t = P.take(dve, f"{nm}.bc1.{c}.{n}").rearrange("p (j t) -> p j t", j=2)
                        P.give(dve.tensor_tensor(inp[:, k % RING], spread(du[:, c, :], 2), t, ALU.mult),
                               f"{nm}.bc1.{c}.{n}")
                        P.wait_given(dve, f"{nm}.bc1.{c}.{n}")
                        dve.wait_ge(ev(nm + ".decay"), k + 1)
                        flat = [r[:, k % RING].rearrange("p j t -> p (j t)") for r in (state, decay, inp)]
                        dve.tensor_tensor_scan(*flat, 0.0, ALU.mult, ALU.add).then_inc(ev(nm + ".state"), 1)
                        dve.wait_ge(ev(nm + ".state"), k + 1)
                        if k >= RING:
                            dve.wait_ge(ev(f"{u}.sum"), base["sum"] + k - RING + 1)
                        t = P.take(dve, f"{nm}.bc2.{c}.{n}").rearrange("p (j t) -> p j t", j=2)
                        P.give(dve.tensor_tensor(yc[:, k % RING], state[:, k % RING], t, ALU.mult),
                               f"{nm}.bc2.{c}.{n}")
                    yield 25 + CHS * 32
                    dve.wait_ge(ev(f"{u}.sum"), base["sum"] + DS)
                    q.link(dve.tensor_tensor(yacc, ysum[:, :, 0, :], ysum[:, :, 1, :], ALU.add))
                    dve.tensor_tensor(yacc, yacc, z, ALU.mult).then_inc(ev(nm + ".gated"), 1)
                    residual_dve(dve, q, nm + ".y")

                def pool_f(pool, q):
                    pool.wait_ge(ev(f"{u}.hn"), G * norm(nm) + 1)
                    pool.memset(xpad[:, :, :, 0:3], 0.0).then_inc(ev(f"{u}.zero"), 1)
                    yield 9
                    pool.wait_ge(ev(nm + ".xc"), 2)
                    for c in range(2):
                        q.link(pool.tensor_scalar(ysum[:, c, 0, :], xc[:, c, :], W["s_D"][:, c:c + 1], None, ALU.mult))
                    q.link(pool.memset(ysum[:, :, 1, :], 0.0))
                    for k, (c, n) in enumerate(steps):
                        yield 24 + CHS * (16 * c + n)
                        P.wait_given(pool, f"{nm}.bc2.{c}.{n}")
                        pool.tensor_tensor(ysum[:, c], ysum[:, c], yc[:, k % RING], ALU.add).then_inc(ev(f"{u}.sum"), 1)
                        pool.wait_ge(ev(f"{u}.sum"), base["sum"] + k + 1)

                return pe_f, act_f, dve_f, pool_f, nothing

            def delta(nm):
                S = Scratch(scratch)
                base = share(diff=1, exp=1, zero=1, conv=3, sum=G)
                qk = S.take(2 * N).rearrange("p (k t) -> p k t", k=2)
                kb = S.take(N)
                outs = S.take(G * 4 * D).rearrange("p (s o f) -> p s o f", s=G, o=4)
                mats = S.take(G * DELTA_H * 3 * L).rearrange("p (s h m t) -> p s h m t", s=G, h=DELTA_H, m=3)
                TT, Pm, Nb = (S.take(G * DELTA_H * L).rearrange("p (s h t) -> p s h t", s=G, h=DELTA_H) for _ in range(3))
                Z, R, U = (S.take(G * D).rearrange("p (s f) -> p s f", s=G) for _ in range(3))
                S = Scratch(scratch)
                S.at = 3 * N + G * 4 * D
                pads = S.take(3 * G * (L + 3)).rearrange("p (k s t) -> p k s t", k=3, s=G)
                vpad = S.take(G * (L + PAD)).rearrange("p (s t) -> p s t", s=G)
                conv = S.take(3 * N).rearrange("p (k s t) -> p k s t", k=3, s=G)
                smooth = S.take(2 * N).rearrange("p (k t) -> p k t", k=2)
                squares = S.take(2 * N).rearrange("p (k t) -> p k t", k=2)
                length = S.take(2 * N).rearrange("p (k t) -> p k t", k=2)
                beta, vb = S.take(N), S.take(N)
                local, mid, mid_odd = (S.take(N).rearrange("p (s t) -> p s t", s=G) for _ in range(3))
                S = Scratch(scratch)
                S.at = 3 * N + G * 4 * D
                prod = S.take(2 * 10 * D).rearrange("p (r k h e) -> p r k h e", r=2, k=10, h=DELTA_H)
                sums = S.take(G * 16).rearrange("p (s o h) -> p s o h", s=G, o=4)
                psums = S.take(G * 40).rearrange("p (s k h) -> p s k h", s=G, k=10)
                feat = S.take(G * NFEAT).rearrange("p (s k h) -> p s k h", s=G, k=14)
                tmp = S.take(G * 16).rearrange("p (s o h) -> p s o h", s=G, o=4)
                fT = S.take(N)
                h1T = S.take(3 * N).rearrange("p (c t) -> p c t", c=3)
                lg, pr = (S.take(G * 16).rearrange("p (a i) -> p a i", i=4) for _ in range(2))
                t16, ss, rr = (S.take(G * DELTA_H) for _ in range(3))
                pm = S.take(2 * 4 * D).rearrange("p (r i h e) -> p r i h e", r=2, i=4, h=DELTA_H)
                mixed, msq, oT = S.take(N), S.take(N), S.take(N)

                NT, T, AT = (lambda s, h, m=m: mats[:, s, h, m, :] for m in range(3))
                heads = range(DELTA_H)

                def hs(h):
                    return slice(DELTA_D * h, DELTA_D * h + DELTA_D)

                def pe_f(pe):
                    yield from norm_pe(pe, nm)
                    yield 5
                    P.wait_given(pe, nm + ".hT")
                    for name, w in (("p0", "d_Wq"), ("p1", "d_Wk"), ("p2", "d_Wv"), ("beta", "d_Wb_wide")):
                        t = P.open(pe, f"{nm}.{name}")
                        P.close(pe.matmul(t, W[w][:], hT[:], start=True, stop=True), f"{nm}.{name}")
                    yield 12
                    pe.wait_ge(ev(nm + ".sq"), 2)
                    for k in range(2):
                        t = P.open(pe, f"{nm}.len{k}")
                        P.close(pe.matmul(t, W["same_head"][:], squares[:, k, :], start=True, stop=True), f"{nm}.len{k}")
                    yield 20
                    pe.wait_ge(ev(nm + ".mid"), 1)
                    pe.wait_ge(ev(nm + ".kb"), 2)
                    for s in range(G):
                        t = P.open(pe, f"{nm}.tok{s}", width=4 * L)
                        for o, src in enumerate((local[:, s, :], mid[:, s, :], vb[:, col(s)], vpad[:, s, PAD:])):
                            last = pe.transpose(t[:, o * L:(o + 1) * L], src, ident[:])
                        P.close(last, f"{nm}.tok{s}")
                    yield 24
                    pe.wait_ge(ev(nm + ".unit"), 2)
                    for s in range(G):
                        for h in heads:
                            t = P.open(pe, f"{nm}.M{s}{h}", width=3 * L)
                            kh, qh, kbh = qk[hs(h), 1, col(s)], qk[hs(h), 0, col(s)], kb[hs(h), col(s)]
                            pe.matmul(t[:, 0:L], kh, kbh, start=True, stop=True, skip_group_check=True)
                            pe.matmul(t[:, L:2 * L], kbh, kh, start=True, stop=True, skip_group_check=True)
                            P.close(pe.matmul(t[:, 2 * L:3 * L], kh, qh, start=True, stop=True, skip_group_check=True),
                                    f"{nm}.M{s}{h}")

                    def product(name, s, lhs, rhs, width=L):
                        t = P.open(pe, f"{nm}.{name}{s}", width=DELTA_H * width)
                        for h in heads:
                            last = pe.matmul(t[:, h * width:(h + 1) * width], lhs(h), rhs(h), start=True, stop=True,
                                             skip_group_check=True)
                        P.close(last, f"{nm}.{name}{s}")

                    for lv in range(1, 6):
                        yield 34 + 8 * (lv - 1)
                        for s in range(G):
                            pe.wait_ge(ev(f"{nm}.Nb"), G * (lv - 1) + s + 1)
                            if lv == 1:
                                pe.wait_ge(ev(nm + ".T"), s + 1)
                            else:
                                P.wait_given(pe, f"{nm}.L{lv - 1}t{s}")
                            product(f"L{lv}P", s, lambda h: Nb[:, s, h, :], lambda h: T(s, h))
                        for s in range(G):
                            P.wait_given(pe, f"{nm}.L{lv}P{s}")
                            if lv < 5:
                                product(f"L{lv}T", s, lambda h: TT[:, s, h, :], lambda h: Pm[:, s, h, :])
                            product(f"L{lv}t", s, lambda h: Pm[:, s, h, :], lambda h: TT[:, s, h, :])
                    yield 74
                    for s in range(G):
                        P.wait_given(pe, f"{nm}.L5t{s}")
                        product("Z", s, lambda h: TT[:, s, h, :], lambda h: outs[:, s, 2, hs(h)], DELTA_D)
                    for s in range(G):
                        P.wait_given(pe, f"{nm}.Z{s}")
                        pe.wait_ge(ev(f"{nm}.Nb"), G * 5 + s + 1)
                        product("R", s, lambda h: Nb[:, s, h, :], lambda h: Z[:, s, hs(h)], DELTA_D)
                    for s in range(G):
                        P.wait_given(pe, f"{nm}.R{s}")
                        product("U", s, lambda h: TT[:, s, h, :], lambda h: R[:, s, hs(h)], DELTA_D)
                    for s in range(G):
                        P.wait_given(pe, f"{nm}.U{s}")
                        product("D", s, lambda h: AT(s, h), lambda h: U[:, s, hs(h)], DELTA_D)
                    yield 82
                    pe.wait_ge(ev(nm + ".feat"), 1)
                    t = P.open(pe, nm + ".fT")
                    for s in range(G):
                        last = pe.transpose(t[0:NFEAT, col(s)], feat[:, s, :, :].rearrange("p k h -> p (k h)"), ident[:])
                    P.close(last, nm + ".fT")
                    P.wait_given(pe, nm + ".fT")
                    for c, (r0, rows) in enumerate(RCH):
                        t = P.open(pe, f"{nm}.h{c}")
                        pe.matmul(t[0:rows, :], W["d_r_w1a"][:, r0:r0 + rows], hT[:], start=True, stop=False)
                        P.close(pe.matmul(t[0:rows, :], W["d_r_w1b"][0:NFEAT, r0:r0 + rows], fT[0:NFEAT, :],
                                          start=False, stop=True), f"{nm}.h{c}")
                    for c in range(3):
                        P.wait_given(pe, f"{nm}.h{c}")
                    yield 92
                    t = P.open(pe, nm + ".lg")
                    bias_row(pe, t, W["d_r_b2"][:])
                    for s in range(G):
                        for c, (r0, rows) in enumerate(RCH):
                            last = pe.matmul(t[:, s * 16:(s + 1) * 16], h1T[0:rows, c, col(s)], W["d_r_w2"][0:rows, c, :],
                                             start=False, stop=c == 2, skip_group_check=True)
                    P.close(last, nm + ".lg")
                    yield 100
                    pe.wait_ge(ev(nm + ".mixed"), 1)
                    t = P.open(pe, nm + ".oT")
                    for s in range(G):
                        last = pe.transpose(t[:, col(s)], mixed[:, col(s)], ident[:])
                    P.close(last, nm + ".oT")
                    P.wait_given(pe, nm + ".oT")
                    t = P.open(pe, nm + ".y", ACC)
                    for s in range(G):
                        last = pe.matmul(t[:, col(s)], oT[:, col(s)], W["d_Wo"][:], start=True, stop=True,
                                         skip_group_check=True)
                    P.close(last, nm + ".y")

                def act_f(act, q):
                    yield from norm_act(act, nm)
                    yield 5
                    act.wait_ge(ev(f"{u}.zero"), base["zero"] + 1)
                    for k in range(3):
                        t = P.take(act, f"{nm}.p{k}")
                        P.give(act.copy(pads[:, k, :, 3:], row_tiles(t)), f"{nm}.p{k}")
                    t = P.take(act, nm + ".beta")
                    P.give(act.activation(beta, t, ACT.Sigmoid), nm + ".beta")
                    for k in (2, 0, 1):
                        act.wait_ge(ev(f"{u}.conv"), base["conv"] + {2: 1, 0: 2, 1: 3}[k])
                        dst = vpad[:, :, PAD:] if k == 2 else row_tiles(smooth[:, k, :])
                        act.activation(dst, conv[:, k, :, :], ACT.Silu).then_inc(ev(nm + ".silu"), 1)
                    act.wait_ge(ev(nm + ".silu"), 3)
                    for k in range(2):
                        act.activation(squares[:, k, :], smooth[:, k, :], ACT.Square).then_inc(ev(nm + ".sq"), 1)
                    yield 12
                    for k in range(2):
                        t = P.take(act, f"{nm}.len{k}")
                        P.give(act.activation(length[:, k, :], t, ACT.Sqrt, bias=eps12[:]), f"{nm}.len{k}")
                    yield 20
                    for s in range(G):
                        t = P.take(act, f"{nm}.tok{s}")
                        P.give(act.copy(outs[:, s, :, :].rearrange("p o f -> p (o f)"), t), f"{nm}.tok{s}")
                    for lv in range(1, 6):
                        yield 34 + 8 * (lv - 1)
                        for s in range(G):
                            t = P.take(act, f"{nm}.L{lv}P{s}")
                            P.give(act.copy(Pm[:, s, :, :].rearrange("p h t -> p (h t)"), t), f"{nm}.L{lv}P{s}")
                    yield 74
                    for name, dst in (("Z", Z), ("R", R)):
                        for s in range(G):
                            t = P.take(act, f"{nm}.{name}{s}")
                            P.give(act.copy(dst[:, s, :], t[:, 0:D]), f"{nm}.{name}{s}")
                    for s in range(G):
                        t = P.take(act, f"{nm}.D{s}")
                        P.give(act.copy(outs[:, s, 2, :], t[:, 0:D]), f"{nm}.D{s}")
                    yield 82
                    t = P.take(act, nm + ".fT")
                    P.give(act.copy(fT[0:NFEAT, :], t[0:NFEAT, :]), nm + ".fT")
                    for c, (r0, rows) in enumerate(RCH):
                        t = P.take(act, f"{nm}.h{c}")
                        P.give(act.activation(h1T[0:rows, c, :], t[0:rows, :], ACT.Silu, bias=W["d_r_b1"][0:rows, c, :]),
                               f"{nm}.h{c}")
                    yield 92
                    act.wait_ge(ev(f"{u}.diff"), base["diff"] + 1)
                    act.activation(pr, lg, ACT.Exp).then_inc(ev(f"{u}.exp"), 1)
                    yield 97
                    for k in range(2):
                        act.wait_ge(ev(nm + ".ss"), k + 1)
                        act.activation(rr, ss, ACT.Sqrt, scale=1.0 / DELTA_D, bias=eps5[:]).then_inc(ev(nm + ".rr"), 1)
                    yield 100
                    t = P.take(act, nm + ".oT")
                    P.give(act.copy(oT, t), nm + ".oT")

                def dve_f(dve, q):
                    norm_dve(dve, q, nm)
                    yield 5
                    marks = {}

                    def tap(key, dst, src, w, k, done=None):
                        if key in marks:
                            q.wait(marks[key])
                            ins = dve.scalar_tensor_tensor(out=dst, in0=src, scalar=w[:, k:k + 1], in1=dst,
                                                           op0=ALU.mult, op1=ALU.add)
                        else:
                            ins = dve.tensor_scalar(dst, src, w[:, k:k + 1], None, ALU.mult)
                        if done:
                            ins.then_inc(ev(done), 1)
                        else:
                            marks[key] = q.mark(ins)

                    names = ("d_conv_q_w", "d_conv_k_w", "d_conv_v_w")
                    for k in range(3):
                        P.wait_given(dve, f"{nm}.p{k}")
                    for tp in range(CONV_K):
                        for k in (2, 0, 1):
                            tap(k, conv[:, k, :, :], pads[:, k, :, tp:tp + L], W[names[k]], tp,
                                f"{u}.conv" if tp == CONV_K - 1 else None)
                    yield 12
                    dve.wait_ge(ev(nm + ".silu"), 1)
                    for n in range(13):
                        tap("even", mid, vpad[:, :, 2 * n:2 * n + L], W["d_mid_w"], 2 * n)
                        if n < 12:
                            tap("odd", mid_odd, vpad[:, :, 2 * n + 1:2 * n + 1 + L], W["d_mid_w"], 2 * n + 1)
                        if n < LOCAL_K:
                            o = PAD - LOCAL_K + 1 + n
                            tap("local", local, vpad[:, :, o:o + L], W["d_local_w"], n)
                    q.wait(max(marks.values()))
                    dve.tensor_tensor(mid, mid, mid_odd, ALU.add).then_inc(ev(nm + ".mid"), 1)
                    yield 20
                    for k in (1, 0):
                        P.wait_given(dve, f"{nm}.len{k}")
                        q.link(dve.reciprocal(length[:, k, :], length[:, k, :]))
                        dve.tensor_tensor(qk[:, k, :], smooth[:, k, :], length[:, k, :],
                                          ALU.mult).then_inc(ev(nm + ".unit"), 1)
                    yield 24
                    for s in range(G):
                        for h in heads:
                            t = P.take(dve, f"{nm}.M{s}{h}")
                            P.give(dve.tensor_tensor(mats[:, s, h, :, :], t[:, 0:3 * L].rearrange("p (m t) -> p m t", m=3),
                                                     W["delta_masks"][:], ALU.mult), f"{nm}.M{s}{h}")
                    for lv in range(1, 6):
                        yield 34 + 8 * (lv - 1)
                        for s in range(G):
                            if lv < 5:
                                t = P.take(dve, f"{nm}.L{lv}T{s}")
                                P.give(dve.tensor_tensor(mats[:, s, :, 1, :], mats[:, s, :, 1, :], row_tiles(t), ALU.add),
                                       f"{nm}.L{lv}T{s}")
                            t = P.take(dve, f"{nm}.L{lv}t{s}")
                            P.give(dve.tensor_tensor(TT[:, s, :, :], TT[:, s, :, :], row_tiles(t), ALU.add),
                                   f"{nm}.L{lv}t{s}")
                    yield 74
                    for s in range(G):
                        P.wait_given(dve, f"{nm}.Z{s}")
                        t = P.take(dve, f"{nm}.U{s}")
                        P.give(dve.tensor_tensor(U[:, s, :], Z[:, s, :], t[:, 0:D], ALU.add), f"{nm}.U{s}")
                    yield 82
                    P.wait_given(dve, f"{nm}.D{G - 1}")
                    for s in range(G):
                        q.mark(dve.tensor_reduce(sums[:, s, :, :], outs[:, s, :, :].rearrange(
                            "p o (h e) -> p o h e", e=DELTA_D), X, ALU.add))
                        dve.wait_ge(ev(nm + ".prod"), s + 1)
                        dve.tensor_reduce(psums[:, s, :, :], prod[:, s % 2, :, :, :], X,
                                          ALU.add).then_inc(ev(nm + ".psum"), 1)
                    dve.wait_ge(ev(nm + ".psum"), G)
                    mean = feat[:, :, 0:8:2, :]
                    q.link(dve.tensor_scalar(mean, sums, 1.0 / DELTA_D, None, ALU.mult))
                    q.link(dve.tensor_tensor(tmp, mean, sums, ALU.mult))
                    q.link(dve.tensor_tensor(tmp, psums[:, :, 0:4, :], tmp, ALU.subtract))
                    dve.tensor_scalar(feat[:, :, 1:8:2, :], tmp, 1.0 / (DELTA_D - 1), None, ALU.mult)
                    dve.tensor_scalar(feat[:, :, 8:14, :], psums[:, :, 4:10, :], 1.0 / DELTA_D, None,
                                      ALU.mult).then_inc(ev(nm + ".feat"), 1)
                    yield 92
                    t = P.take(dve, nm + ".lg")[:, 0:G * 16].rearrange("p (a i) -> p a i", i=4)
                    q.link(dve.tensor_reduce(t16, t, X, ALU.max))
                    P.give(dve.tensor_tensor(lg, t, spread(t16, 4, 2), ALU.subtract), nm + ".lg")
                    P.wait_given(dve, nm + ".lg")
                    dve.tensor_copy(t16, t16).then_inc(ev(f"{u}.diff"), 1)
                    dve.wait_ge(ev(f"{u}.exp"), base["exp"] + 1)
                    q.link(dve.tensor_reduce(t16, pr, X, ALU.add))
                    q.link(dve.reciprocal(t16, t16))
                    q.link(dve.tensor_tensor(pr, pr, spread(t16, 4, 2), ALU.mult))
                    dve.tensor_scalar(pr, pr, 1.0 - 4.0 * 0.01, 0.01, ALU.mult, ALU.add).then_inc(ev(nm + ".probs"), 1)
                    for s in range(G):
                        dve.wait_ge(ev(nm + ".pm"), s + 1)
                        dve.tensor_reduce(mixed[:, col(s)].rearrange("p (h e) -> p h e", h=DELTA_H),
                                          pm[:, s % 2].rearrange("p i h e -> p h e i"), X,
                                          ALU.add).then_inc(ev(f"{u}.sum"), 1)
                    yield 97
                    dve.wait_ge(ev(f"{u}.sum"), base["sum"] + G)
                    hv = [a.rearrange("p (a e) -> p a e", e=DELTA_D) for a in (mixed, msq)]
                    for k, w in enumerate(("d_mix_w", "d_onorm_w")):
                        q.link(dve.tensor_tensor(msq, mixed, mixed, ALU.mult))
                        dve.tensor_reduce(ss, hv[1], X, ALU.add).then_inc(ev(nm + ".ss"), 1)
                        dve.wait_ge(ev(nm + ".rr"), k + 1)
                        q.link(dve.reciprocal(t16, rr))
                        q.link(dve.tensor_tensor(hv[0], hv[0], spread(t16, DELTA_D, 2), ALU.mult))
                        ins = dve.tensor_tensor(row_tiles(mixed), row_tiles(mixed), spread(W[w][:], G), ALU.mult)
                        if k == 0:
                            q.link(ins)
                        else:
                            ins.then_inc(ev(nm + ".mixed"), 1)
                    yield 100
                    residual_dve(dve, q, nm + ".y")

                def pool_f(pool, q):
                    pool.wait_ge(ev(f"{u}.hn"), G * norm(nm) + 1)
                    pool.memset(pads[:, :, :, 0:3], 0.0)
                    pool.memset(vpad[:, :, 0:PAD], 0.0).then_inc(ev(f"{u}.zero"), 1)
                    yield 5
                    P.wait_given(pool, nm + ".beta")
                    pool.wait_ge(ev(nm + ".silu"), 1)
                    pool.tensor_tensor(row_tiles(vb), vpad[:, :, PAD:], row_tiles(beta), ALU.mult).then_inc(ev(nm + ".kb"), 1)
                    yield 20
                    pool.wait_ge(ev(nm + ".unit"), 1)
                    pool.tensor_tensor(kb, qk[:, 1, :], beta, ALU.mult).then_inc(ev(nm + ".kb"), 1)

                    def level(lv, s):
                        pool.tensor_tensor(Nb[:, s, :, :], mats[:, s, :, 0, :], spread(W["level_T"][:, lv, :], DELTA_H),
                                           ALU.mult).then_inc(ev(f"{nm}.Nb"), 1)

                    yield 24
                    for s in range(G):
                        for h in heads:
                            P.wait_given(pool, f"{nm}.M{s}{h}")
                        q.mark(pool.tensor_tensor(mats[:, s, :, 1, :], mats[:, s, :, 1, :], spread(ident[:], DELTA_H), ALU.add))
                        q.link(pool.tensor_tensor(TT[:, s, :, :], mats[:, s, :, 0, :],
                                                  spread(W["level_T"][:, 0, :], DELTA_H), ALU.mult))
                        pool.tensor_tensor(TT[:, s, :, :], TT[:, s, :, :], spread(ident[:], DELTA_H),
                                           ALU.add).then_inc(ev(nm + ".T"), 1)
                        level(1, s)
                    for lv in range(2, 7):
                        yield 34 + 8 * (lv - 2)
                        for s in range(G):
                            P.take(pool, f"{nm}.L{lv - 1}P{s}")
                            level(lv, s)
                    o4 = outs.rearrange("p s o (h e) -> p s o h e", h=DELTA_H)
                    yield 82
                    P.wait_given(pool, f"{nm}.D{G - 1}")
                    for s in range(G):
                        if s >= 2:
                            pool.wait_ge(ev(nm + ".psum"), s - 1)
                        o, w = o4[:, s], prod[:, s % 2]
                        pool.tensor_tensor(w[:, 0:4], o, o, ALU.mult)
                        for a, k, n in ((0, 4, 3), (1, 7, 2)):
                            for b in range(n):
                                pool.tensor_tensor(w[:, k + b], o[:, a], o[:, a + 1 + b], ALU.mult)
                        pool.tensor_tensor(w[:, 9], o[:, 2], o[:, 3], ALU.mult).then_inc(ev(nm + ".prod"), 1)
                    yield 92
                    pool.wait_ge(ev(nm + ".probs"), 1)
                    pv = pr.rearrange("p (s h) i -> p s h i", s=G)
                    for s in range(G):
                        if s >= 2:
                            pool.wait_ge(ev(f"{u}.sum"), base["sum"] + s - 1)
                        pool.tensor_tensor(pm[:, s % 2], o4[:, s],
                                           spread(pv[:, s].rearrange("p h i -> p i h"), DELTA_D, 3),
                                           ALU.mult).then_inc(ev(nm + ".pm"), 1)

                return pe_f, act_f, dve_f, pool_f, nothing
            sections = {
                "L0_delta": delta(f"{u}d0"),
                "L0_cross": attention16(f"{u}x0", "x0_", src="ctx"),
                "L0_ffn": ffn(f"{u}f0"),
                "L1_attn": attention16(f"{u}a1", "a1_", bias=True, bias_out=True, mask="causal"),
                "L1_mix": mixer(f"{u}m1"),
                "L1_moe": moe1(f"{u}e1"),
                "L2_attn": attention16(f"{u}a2", "a2_", rope=True, mask="causal"),
                "L2_cross": attention16(f"{u}x2", "x2_", src="ctx", bias=True, bias_out=True, mask="given"),
                "L2_moe": moe2(f"{u}e2"),
                "L3_mamba": mamba(f"{u}s3"),
                "L3_cross": cross3(f"{u}x3"),
                "L3_moe": moe3(f"{u}e3"),
            }
            last_sum = {"L0_delta": "d0", "L0_cross": "x0", "L0_ffn": "f0", "L1_attn": "a1", "L1_mix": "m1",
                        "L1_moe": "e1", "L2_attn": "a2", "L2_cross": "x2", "L2_moe": "e2", "L3_mamba": "s3",
                        "L3_cross": "x3", "L3_moe": "e3"}[SECTIONS[-1]]
            x_d, c_d, m_d, o_d = (a.rearrange("(g u s) t f -> u g t s f", u=STREAMS, s=G)[u]
                                  for a in (dram["x"], dram["ctx"], dram["mask"], out))
            p_d = dram["key_pad"].rearrange("(g u a s) t -> u g a (s t)", u=STREAMS, a=1, s=G)[u]

            def load(sp, g):
                sp.dma_start(ctx_tok[:], c_d[g]).then_inc(s_ctx, 16)
                sp.dma_start(xres[:], x_d[g]).then_inc(s_in, 16)
                sp.dma_start(mask_i[:], m_d[g]).then_inc(s_ctx, 16)
                sp.dma_start(pad_row_u8[:], p_d[g]).then_inc(s_ctx, 16)

            def store(sp, g):
                P.wait_given(sp, f"{u}{last_sum}.y")
                sp.dma_start(o_d[g], xres[:]).then_inc(s_out, 16)
                sp.wait_ge(s_out, 16)

            def steps(engine, *args):
                yield 0.0
                context[engine](*args)
                for name in SECTIONS:
                    start = PLACE[name]
                    yield start
                    labels = sections[name][engine](*args)
                    if labels is not None:
                        for part in labels:
                            yield start + part

            def wait_in(dve):
                dve.wait_ge(s_in, 16)

            context = {0: ctx_pe, 1: ctx_act, 2: lambda dve, q: (ctx_dve(dve, q), wait_in(dve)), 3: nothing, 4: nothing}
            sems = [s_in, s_out, s_ctx, s_stack] + s_stored
            return load, store, steps, sems

        groups = [stream(u) for u in range(STREAMS)]

        def in_turns(engine, *args):
            runs = [g[2](engine, *args) for g in groups]
            place = [next(r) + LAG * u for u, r in enumerate(runs)]
            while any(p is not None for p in place):
                p, u = min((p, u) for u, p in enumerate(place) if p is not None)
                p = next(runs[u], None)
                place[u] = None if p is None else p + LAG * u

        def load_experts3(sp):
            if "L2_moe" in SECTIONS:
                for u in range(STREAMS):
                    P.take(sp, f"{u}e2.y")
            sp.dma_start(experts[:, 0:E3 * F3], dram["e3_W1"]).then_inc(s_e3, 16)
            sp.dma_start(experts[:, E3 * F3:].rearrange("p (c f) -> p c f", f=D),
                         dram["e3_W2"].rearrange("(c p) f -> p c f", p=128)).then_inc(s_e3, 16)

        with nc.Fori(0, NGROUPS) as g:
            with nc.Block(no_gpsimd_drain=True) as block:
                @block.tensor
                def _(pe):
                    in_turns(0, pe)

                @block.scalar
                def _(act):
                    in_turns(1, act, Order(act, s_act))

                @block.vector
                def _(dve):
                    in_turns(2, dve, Order(dve, s_dve))

                @block.gpsimd
                def _(pool):
                    in_turns(3, pool, Order(pool, s_pool))

                @block.sync
                def _(sp):
                    for load, _, _, _ in groups:
                        load(sp, g)
                    if "L2_moe" in SECTIONS:
                        sp.dma_start(experts[:, 0:E2 * F2], dram["e2_w1"]).then_inc(s_e2, 16)
                        sp.dma_start(experts[:, E2 * F2:2 * E2 * F2].rearrange("p (c f) -> p c f", f=D),
                                     dram["e2_w2"].rearrange("(c p) f -> p c f", p=128)).then_inc(s_e2, 16)
                    in_turns(4, sp)
                    if "L3_moe" in SECTIONS:
                        load_experts3(sp)
                    for _, store, _, _ in groups:
                        store(sp, g)

            for s in [s_e2, s_e3, s_dve, s_act, s_pool] + [s for g4 in groups for s in g4[3]] + filled + emptied + \
                    list(events.values()):
                nc.sync.sem_clear(s)
            nc.all_engine_barrier()


def kernel(**inputs):
    import concourse.bacc as bacc
    from concourse.bass_utils import run_bass_kernel_spmd

    arrays = host_layout({k: np.asarray(v) for k, v in inputs.items()})
    arrays.update(host_constants())
    nc = bacc.Bacc("TRN2", target_bir_lowering=False, num_devices=1)
    dram = {n: nc.dram_tensor("in_" + n, a.shape, mybir.dt.from_np(a.dtype), kind="ExternalInput").ap()
            for n, a in arrays.items()}
    out = nc.dram_tensor("out", (B, L, D), F32, kind="ExternalOutput").ap()
    build(nc, dram, out)
    r = run_bass_kernel_spmd(nc, [{"in_" + n: a for n, a in arrays.items()}], core_ids=[0])
    return r.results[0]["out"]
```

```python
from contextlib import ExitStack

import numpy as np
import concourse.bass as bass
from concourse import mybir

F32 = mybir.dt.float32
BF16 = mybir.dt.bfloat16
I32 = mybir.dt.int32
U8 = mybir.dt.uint8
U32 = mybir.dt.uint32
ACT = mybir.ActivationFunctionType
ALU = mybir.AluOpType
X = mybir.AxisListType.X

B, L, D = 32, 128, 128
G = 2
STREAMS = 2
NGROUPS = B // (G * STREAMS)
N = G * L
NH, DH = 16, 8
NJ, NI = 4, 4
DELTA_H, DELTA_D = 4, 32
MID_K, LOCAL_K, CONV_K = 25, 7, 4
PAD = MID_K - 1
NFEAT = 14 * DELTA_H
RH = 2 * (D + NFEAT)
RCH = [(0, 128), (128, 128), (256, RH - 256)]
FFH = 384
E1, H1, HS1 = 8, 176, 352
C1 = E1 * H1 // 128
SCH = [(0, 128), (128, 128), (256, HS1 - 256)]
E2, F2 = 14, 256
E3, F3 = 8, 512
CAP = B * L // E3
LOT3 = 4
LOTC = min(16, NGROUPS * STREAMS * G)
RING_BANKS = 8 - STREAMS
DS = 16
SLOTS = ((slice(0, 3), slice(1, 6, 2)), (slice(3, 5), slice(2, 5, 2)), (slice(5, 6), slice(0, 1)))
SCALE16 = float(DH) ** -0.5
BIG = 1.0e30
MASK_BIG, MASK_SMALL = 999424.0, 576.0
SCRATCH = 9888
PERM = [16 * (p % 8) + 8 * (p // 64) + p // 8 % 8 for p in range(128)]
SECTIONS = ["L0_delta", "L0_cross", "L0_ffn", "L1_attn", "L1_mix", "L1_moe", "L2_attn", "L2_cross", "L2_moe",
            "L3_mamba", "L3_cross", "L3_moe"]

CH1, CH2, CHS = 2.415, 2.75, 1.568
SPANS = {"L0_delta": 105.5, "L0_cross": 52, "L0_ffn": 13, "L1_attn": 68.5, "L1_mix": 10, "L1_moe": 42.81,
         "L2_attn": 52, "L2_cross": 54, "L2_moe": 49.5, "L3_mamba": 78, "L3_cross": 34, "L3_moe": 6}
PLACE = {n: 1 + sum(SPANS[m] for m in SECTIONS[:k]) for k, n in enumerate(SECTIONS)}
STACKED, SEQ16, SEQ3, LEVEL = 22, 6.6, 3.36, 8
NORMED = 3
LAG = 20.5


def host_constants():
    c = {}
    i, j = np.arange(L)[:, None], np.arange(L)[None, :]
    c["ident"] = np.eye(128, dtype=np.float32)
    levels = [1, 2, 4, 8, 16, 32, 64]
    lev = np.stack([(i // (2 * b) == j // (2 * b)) & ((i // b) % 2 == 1) & ((j // b) % 2 == 0) for b in levels])
    c["delta_masks"] = np.stack([-(i < j).astype(np.float32), -lev[0].astype(np.float32),
                                 (i <= j).astype(np.float32)], 1)
    c["level_T"] = np.ascontiguousarray(lev.transpose(2, 0, 1)).astype(np.float32)
    c["causal"] = np.where(i >= j, 0.0, -1e9).astype(np.float32)
    c["causal_T"] = np.where(i <= j, 0.0, -1e9).astype(np.float32)
    c["before_T"] = (i < j).astype(np.float32)
    c["same_head"] = (i // DELTA_D == j // DELTA_D).astype(np.float32)
    c["first_place"] = np.broadcast_to(CAP * np.arange(E3, dtype=np.float32), (128, E3)).copy()
    c["rev"] = np.broadcast_to(16.0 - np.arange(16, dtype=np.float32), (128, 16)).copy()
    c["sel1"] = (np.arange(E1)[:, None] == np.arange(E1 * H1)[None, :] // H1).astype(np.float32)
    row = np.arange(96)[:, None, None]
    c["sel_state"] = ((row % DS == np.arange(DS)[None, :, None]) &
                      (row % 32 // DS == np.arange(128)[None, None, :] // 64)).astype(np.float32)
    c["sel_part"] = ((i[:, :1] % 32 == np.arange(NH)[None, :]) & (i[:, :1] < 96)).astype(np.float32)
    t = np.arange(L, dtype=np.float32)
    fr = (1.0 / np.float32(10000.0) ** (np.arange(0, DH, 2, dtype=np.float32) / DH)).astype(np.float32)
    ang = np.outer(t, fr).astype(np.float32)
    p = np.arange(128)
    r = p // DH % DH
    cos, sin = np.cos(ang).T[r // 2], np.sin(ang).T[r // 2]
    sin = np.where(r[:, None] % 2 == 0, -sin, sin)
    c["rope2"] = np.stack([cos * SCALE16, sin * SCALE16, cos, sin], 1).astype(np.float32)
    ts = np.float32(10000.0) ** (np.float32(2.0 / 32) * np.arange(16, dtype=np.float32))
    sgn = np.where(p[:, None] % 32 < 16, -1.0, 1.0)
    out = []
    for pos, sc in ((t + L, 32.0 ** -0.5), (t, 1.0)):
        rad = (pos[:, None] / ts).astype(np.float32)
        out += [np.cos(rad).T[p % 16] * sc, np.sin(rad).T[p % 16] * sgn * sc]
    c["rope3"] = np.stack(out, 1).astype(np.float32)
    return c


def host_layout(a):
    w = {}
    cont = np.ascontiguousarray
    w["x"], w["ctx"], w["mask"] = a["x"], a["ctx_1024"], a["mask_BxSxS2_if1"]
    w["key_pad"] = a["mask_BxS2_bk0"]
    for n in ("Wq", "Wk", "Wv", "Wb", "Wo"):
        w["d_" + n] = a["L0_attn_" + n]
    w["d_Wb_wide"] = cont(np.repeat(a["L0_attn_Wb"], DELTA_D, axis=1))
    for n in ("conv_q_w", "conv_k_w", "conv_v_w", "local_w", "mid_w", "r_w1"):
        w["d_" + n] = a["L0_attn_" + n]
    w["d_r_b1"] = a["L0_attn_r_b1"][:, None]
    w["d_r_w2"] = a["L0_attn_r_w2"]
    w["d_r_b2"] = a["L0_attn_r_b2"][None, :]
    w["d_mix_w"] = cont(np.broadcast_to(a["L0_attn_mix_w"].reshape(1, D), (128, D)))
    w["d_onorm_w"] = cont(np.broadcast_to(a["L0_attn_onorm_w"][None, None, :], (128, DELTA_H, DELTA_D)).reshape(128, D))
    for n in ("Wq", "Wk", "Wv", "Wo"):
        w["x0_" + n] = cont(a["L0_xattn_" + n].T)
    w["f_gate"], w["f_up"], w["f_down"] = (cont(a["L0_ffn_w_" + n].T) for n in ("gate", "up", "down"))
    wa = cont(a["L1_attn_w_attn"].T)
    ba = a["L1_attn_b_attn"]
    for k, n in enumerate(("Wq", "Wk", "Wv")):
        w["a1_" + n] = cont(wa[:, k * D:(k + 1) * D])
    w["a1_bq"], w["a1_bk"], w["a1_bv"] = ba[:D, None], ba[D:2 * D, None], ba[None, 2 * D:]
    w["a1_Wo"], w["a1_bo"] = cont(a["L1_attn_w_proj"].T), a["L1_attn_b_proj"][None, :]
    w["m_W1"], w["m_W2"] = cont(a["L1_xattn_W"][:, :D].T), cont(a["L1_xattn_W"][:, D:].T)
    w["m_b"] = a["L1_xattn_b"][None, :]
    w["e1_Wg"] = a["L1_ffn_Wg"]
    w["e1_W1"] = cont(a["L1_ffn_W1"].transpose(1, 0, 2).reshape(D, E1 * H1))
    w["e1_W2"] = cont(a["L1_ffn_W2"].transpose(1, 0, 2).reshape(D, E1 * H1))
    w["e1_W3"] = a["L1_ffn_W3"].reshape(E1 * H1, D)
    w["e1_Ws1"], w["e1_Ws2"], w["e1_Ws3"] = (a["L1_ffn_Ws%d" % k] for k in (1, 2, 3))
    wq = cont(a["L2_attn_W_qkv"].T)
    swap = np.arange(D) ^ 1
    w["a2_Wq"], w["a2_Wk"], w["a2_Wv"] = (cont(wq[:, k * D:(k + 1) * D]) for k in range(3))
    w["a2_Wq_swap"], w["a2_Wk_swap"] = cont(w["a2_Wq"][:, swap]), cont(w["a2_Wk"][:, swap])
    w["a2_Wo"] = cont(a["L2_attn_W_out"].T)
    for n in ("Wq", "Wk", "Wv", "Wo"):
        w["x2_" + n] = a["L2_xattn_" + n]
    w["x2_bq"], w["x2_bk"] = a["L2_xattn_bq"][:, None], a["L2_xattn_bk"][:, None]
    w["x2_bv"], w["x2_bo"] = a["L2_xattn_bv"][None, :], a["L2_xattn_bo"][None, :]
    w["e2_Wr"] = a["L2_ffn_router_w"]
    w["e2_w1"] = cont(a["L2_ffn_w1"].transpose(1, 0, 2).reshape(D, E2 * F2))
    w["e2_b1"] = cont(a["L2_ffn_b1"].reshape(E2 * F2 // 128, 128).T)
    w["e2_w2"] = a["L2_ffn_w2"].reshape(E2 * F2, D)
    w["e2_b2"] = a["L2_ffn_b2"]
    w["s_in"] = cont(a["L3_attn_in_proj_w"].T)
    w["s_conv_w"] = cont(a["L3_attn_conv_w"].reshape(2, 128, 4).transpose(1, 0, 2))
    w["s_conv_b"] = cont(a["L3_attn_conv_b"].reshape(2, 128).T)
    xw = a["L3_attn_x_proj_w"].reshape(4, 3, DS, 64)
    dtw = a["L3_attn_dt_proj_w"].reshape(4, 64, DS)
    w_x = np.zeros((128, 2, 2, DS), np.float32)
    w_bc = np.zeros((128, 2, 2, 3, 2, DS), np.float32)
    w_dt = np.zeros((2 * DS, 2, 128), np.float32)
    for c in range(2):
        for h in range(2):
            w_x[64 * h:64 * h + 64, c, h, :] = xw[2 * c + h, 0].T
            w_bc[64 * h:64 * h + 64, :, c, :, h, :] = xw[2 * c + h, 1:].transpose(2, 0, 1)[:, :, None, :]
            w_dt[DS * h:DS * h + DS, c, 64 * h:64 * h + 64] = dtw[2 * c + h].T
    w["s_x"], w["s_dt"] = w_x.reshape(128, 4 * DS), w_dt.reshape(2 * DS, 256)
    w["s_bc"] = w_bc.reshape(128, 24 * DS)
    w["s_dt_b"] = cont(a["L3_attn_dt_proj_b"].reshape(2, 128).T)
    w["s_A_log"] = cont(a["L3_attn_A_log"].reshape(2, 128, DS).transpose(1, 0, 2))
    w["s_D"] = cont(a["L3_attn_Dskip"].reshape(2, 128).T)
    w["s_out"] = cont(a["L3_attn_out_proj_w"].T)
    w["x3_scale"] = a["L3_xattn_rms_scale"][:, None]
    qw = cont(a["L3_xattn_q_w"].transpose(1, 0, 2).reshape(D, 128))
    half = np.arange(128) ^ 16
    w["x3_Wq"], w["x3_Wq_swap"] = qw, cont(qw[:, half])
    kw = cont(np.tile(a["L3_xattn_kv_w"][0, 0], (1, 4)))
    w["x3_Wk"], w["x3_Wk_swap"] = kw, cont(kw[:, half])
    w["x3_Wv"] = a["L3_xattn_kv_w"][1, 0]
    w["x3_Wo"] = a["L3_xattn_out_w"].reshape(128, D)
    w["e3_Wr"] = a["L3_ffn_Wr"]
    w["e3_W1"] = cont(a["L3_ffn_W1"].transpose(1, 0, 2).reshape(D, E3 * F3))
    w["e3_W2"] = a["L3_ffn_W2"].reshape(E3 * F3, D)
    for n in ("x0_", "a1_", "a2_", "x2_"):
        for m in ("Wq", "Wk", "Wq_swap", "Wk_swap"):
            if n + m in w:
                w[n + m] = w[n + m][:, PERM]
        for m in ("bq", "bk"):
            if n + m in w:
                w[n + m] = w[n + m][PERM]
    return {k: cont(v) for k, v in w.items()}


ROWS = {"d_r_w2": RCH, "e1_Ws3": SCH}
CHUNKED = {"e1_W3": C1, "s_out": 2}
STREAMED = ("x", "ctx", "mask", "key_pad", "e2_w1", "e2_w2", "e3_W1", "e3_W2")
ROUNDED = ("sel_state", "sel_part")
LATE = ("x0_", "a1_", "m_", "e1_", "a2_", "x2_", "e2_", "s_", "e3_")
INTEGER = ("f_gate", "f_up", "f_down")


class Psum:

    def __init__(self, banks, filled, emptied):
        self.banks, self.filled, self.emptied = banks, filled, emptied
        self.place, self.turns, self.width, self.next = {}, [0] * 8, {}, 0

    def open(self, pe, name, bank=None, width=N):
        if bank is None:
            bank = self.next
            self.next = (self.next + 1) % RING_BANKS
        turn = self.turns[bank]
        self.turns[bank] += 1
        assert name not in self.place, name
        self.place[name], self.width[name] = (bank, turn), width
        if turn:
            pe.wait_ge(self.emptied[bank], turn)
        return self.banks[:, bank, 0:self.width[name]]

    def bank(self, name):
        return self.banks[:, self.place[name][0], 0:self.width[name]]

    def close(self, ins, name):
        ins.then_inc(self.filled[self.place[name][0]], 1)

    def take(self, eng, name):
        bank, turn = self.place[name]
        eng.wait_ge(self.filled[bank], turn + 1)
        return self.banks[:, bank, 0:self.width[name]]

    def give(self, ins, name):
        ins.then_inc(self.emptied[self.place[name][0]], 1)

    def wait_given(self, eng, name):
        bank, turn = self.place[name]
        eng.wait_ge(self.emptied[bank], turn + 1)


class Order:

    def __init__(self, eng, sem):
        self.eng, self.sem, self.count = eng, sem, 0

    def mark(self, ins):
        self.count += 1
        ins.then_inc(self.sem, 1)
        return self.count

    def wait(self, count):
        self.eng.wait_ge(self.sem, count)

    def link(self, ins):
        self.wait(self.mark(ins))


class Scratch:

    def __init__(self, tensor):
        self.tensor, self.at = tensor, 0

    def take(self, words, dtype=F32):
        size = words if dtype == F32 else (words + 1) // 2
        ap = self.tensor[:, self.at:self.at + size]
        self.at += size
        assert self.at <= SCRATCH, self.at
        return ap if dtype == F32 else ap.bitcast(dtype)


def row_tiles(ap):
    return ap.rearrange("p (s f) -> p s f", f=128)


def spread(ap, count, axis=1):
    ap = ap.unsqueeze(axis)
    shape = list(ap.shape)
    shape[axis] = count
    return ap.broadcast_to(shape)


def build(nc, dram, out):
    with ExitStack() as st:
        def sb(name, shape, dt=F32):
            return st.enter_context(nc.sbuf_tensor(name, shape, dt))

        def sem(name):
            return st.enter_context(nc.semaphore(name))

        W = {}
        plain, late_loads = [], []
        experts = sb("experts", [128, 2 * E2 * F2])
        scratches = [sb(f"scratch{u}", [128, SCRATCH]) for u in range(STREAMS)]
        scratch = scratches[0]
        for k, name in enumerate(INTEGER):
            W[name] = scratch[:, k * FFH:(k + 1) * FFH].bitcast(I32)
            if name == "f_down":
                W[name] = W[name].rearrange("p (c f) -> p c f", c=3)
                plain.append((W[name], dram[name].rearrange("(c p) f -> p c f", p=128)))
            else:
                plain.append((W[name], dram[name]))
        at = 3 * FFH
        for name in ROUNDED:
            shape = list(dram[name].shape)
            words = int(np.prod(shape[1:]))
            W[name] = scratch[0:shape[0], at:at + words]
            at += words
            flat = dram[name] if len(shape) == 2 else dram[name].rearrange("p a b -> p (a b)")
            plain.append((W[name], flat))
        sel_state, sel_part = sb("sel_state_bf", [96, DS, 128], BF16), sb("sel_part_bf", [128, NH], BF16)
        early_loads = plain
        for name, t in dram.items():
            plain = late_loads if name.startswith(LATE) and name != "s_A_log" else early_loads
            if name in STREAMED or name in INTEGER or name in ROUNDED:
                continue
            shape, dt = list(t.shape), F32
            if name in CHUNKED:
                n = CHUNKED[name]
                W[name] = sb("w_" + name, [128, n, shape[1]], dt)
                plain.append((W[name][:], t.rearrange("(c p) f -> p c f", p=128)))
            elif name in ROWS:
                W[name] = sb("w_" + name, [128, len(ROWS[name]), shape[1]], dt)
                for c, (r0, rows) in enumerate(ROWS[name]):
                    plain.append((W[name][0:rows, c, :], t[r0:r0 + rows, :]))
            elif name == "d_r_w1":
                W["d_r_w1a"] = sb("w_d_r_w1a", [128, RH])
                W["d_r_w1b"] = sb("w_d_r_w1b", [NFEAT, RH])
                plain += [(W["d_r_w1a"][:], t[0:D, :]), (W["d_r_w1b"][:], t[D:D + NFEAT, :])]
            elif name == "d_r_b1":
                W[name] = sb("w_d_r_b1", [128, 3, 1])
                for c, (r0, rows) in enumerate(RCH):
                    plain.append((W[name][0:rows, c, :], t[r0:r0 + rows, :]))
            else:
                W[name] = sb("w_" + name, shape, dt)
                plain.append((W[name][:], t))
        plain = early_loads
        ident = W["ident"]
        fw = {n: sb("fw_" + n, [128, FFH] if n != "down" else [128, 3, D]) for n in ("gate", "up", "down")}
        ident_bf, ident_big, ident_small = (sb(n, [128, 128], BF16) for n in ("ident_bf", "ident_big", "ident_small"))
        causal_bf, causal_T_bf = sb("causal_bf", [128, 128], BF16), sb("causal_T_bf", [128, 128], BF16)
        ones_row = sb("ones_row", [1, 128])
        ones_sq = sb("ones_sq", [128, 128])
        ones_col = sb("ones_col", [128, 1])
        eps5, eps6, eps12 = sb("eps5", [128, 1]), sb("eps6", [128, 1]), sb("eps12", [128, 1])
        ones_first = sb("ones_first", [128, 128])
        pad_wides = [sb(f"{u}_pad_wide", [128, N]) for u in range(STREAMS)]
        ssm_A = sb("ssm_A", [128, 2, DS])
        counts = sb("counts", [128, E3])
        scale3 = sb("scale3", [128, 1])

        banks = st.enter_context(nc.psum_tensor("banks", [128, 8, 512], F32))

        s_weights, s_setup = sem("weights_loaded"), sem("setup")
        s_late, s_e2 = sem("late_weights_loaded"), sem("experts2_loaded")
        filled = [sem(f"bank{b}_filled") for b in range(8)]
        emptied = [sem(f"bank{b}_emptied") for b in range(8)]
        s_dve, s_act, s_pool = sem("dve_steps"), sem("act_steps"), sem("pool_steps")
        events = {}

        def ev(name):
            if name not in events:
                events[name] = sem(name)
            return events[name]

        P = Psum(banks, filled, emptied)
        def col(s):
            return slice(s * L, (s + 1) * L)

        expert_in = nc.dram_tensor("expert_in", (E3 * CAP, D), F32, kind="Internal").ap()
        expert_out = nc.dram_tensor("expert_out", (E3 * CAP, D), F32, kind="Internal").ap()
        res_d = nc.dram_tensor("residual", (B, L, D), F32, kind="Internal").ap()
        place_d = nc.dram_tensor("places", (B // G, 128, G), U32, kind="Internal").ap()
        s_zero = sem("rows_cleared")

        zeros = scratches[1][:, 0:D]
        with nc.Block(no_gpsimd_drain=True) as block:
            queues = [plain[k::2] for k in range(2)]

            @block.sync
            def _(sp):
                for dst, src in queues[0]:
                    sp.dma_start(dst, src).then_inc(s_weights, 16)
                sp.wait_ge(s_weights, 16 * len(plain))
                for dst, src in late_loads:
                    sp.dma_start(dst, src).then_inc(s_late, 16)
                if "L2_moe" in SECTIONS:
                    sp.dma_start(experts[:, 0:E2 * F2], dram["e2_w1"]).then_inc(s_e2, 16)
                    w2 = experts[:, E2 * F2:2 * E2 * F2].rearrange("p (c f) -> p c f", f=D)
                    w2_d = dram["e2_w2"].rearrange("(c p) f -> p c f", p=128)
                    for c in (slice(0, E2), slice(E2, 2 * E2)):
                        sp.dma_start(w2[:, c], w2_d[:, c]).then_inc(s_e2, 16)
                sp.wait_ge(s_pool, 1)
                sp.dma_start(expert_in.rearrange("(p c) f -> p c f", p=128),
                             spread(zeros, E3 * CAP // 128)).then_inc(s_zero, 16)

            @block.scalar
            def _(act):
                for dst, src in queues[1]:
                    act.dma_start(dst, src).then_inc(s_weights, 16)
                act.wait_ge(s_weights, 16 * len(plain))
                act.activation(ssm_A[:], W["s_A_log"][:], ACT.Exp).then_inc(s_act, 1)

            @block.gpsimd
            def _(pool):
                pool.memset(ones_row[:], 1.0)
                pool.memset(ones_sq[:], 1.0)
                for wide in pad_wides:
                    pool.memset(wide[:], 0.0)
                pool.memset(zeros, 0.0)
                pool.memset(ones_first[:], 0.0).then_inc(s_pool, 1)
                pool.wait_ge(s_pool, 1)
                pool.memset(ones_first[0:1, :], 1.0)
                pool.memset(ones_col[:], 1.0)
                pool.memset(eps5[:], 1e-5)
                pool.memset(eps6[:], 1e-6)
                pool.memset(eps12[:], 1e-12)
                pool.memset(counts[:], 0.0).then_inc(s_setup, 1)

            @block.vector
            def _(dve):
                dve.wait_ge(s_weights, 16 * len(plain))
                for n in ("gate", "up", "down"):
                    dve.tensor_scalar(fw[n][:], W["f_" + n], float(np.float32(1.0 / 127.0)), None, ALU.mult)
                dve.tensor_copy(sel_state[:].rearrange("p a b -> p (a b)"), W["sel_state"])
                dve.tensor_copy(sel_part[:], W["sel_part"])
                dve.tensor_copy(ident_bf[:], ident[:])
                dve.tensor_scalar(ident_big[:], ident[:], MASK_BIG, None, ALU.mult)
                dve.tensor_scalar(ident_small[:], ident[:], MASK_SMALL, None, ALU.mult)
                dve.tensor_copy(causal_bf[:], W["causal"][:])
                dve.tensor_copy(causal_T_bf[:], W["causal_T"][:])
                dve.tensor_scalar(scale3[:], W["x3_scale"][:], 1.0, None, ALU.add).then_inc(s_dve, 1)
                dve.wait_ge(s_dve, 1)
                for n in ("Wq", "Wq_swap", "Wk", "Wk_swap", "Wv"):
                    w = W["x3_" + n]
                    dve.tensor_scalar(w[:], w[:], scale3[:], None, ALU.mult)
                dve.wait_ge(s_act, 1)
                dve.tensor_scalar(ssm_A[:], ssm_A[:], -1.0, None, ALU.mult).then_inc(s_setup, 1)
                dve.wait_ge(s_setup, 2)

        nc.sync.sem_clear(s_pool)
        nc.sync.sem_clear(s_dve)
        nc.sync.sem_clear(s_act)
        nc.all_engine_barrier()

        def stream(u):
            scratch = scratches[u]
            xres = sb(f"{u}_xres", [128, G, D])
            ctx_tok = sb(f"{u}_ctx_tok", [128, G, D])
            ctxT = sb(f"{u}_ctxT", [128, N])
            ctxnT = sb(f"{u}_ctxnT", [128, N])
            ctx_sum = sb(f"{u}_ctx_sum", [128, G])
            mask_i = sb(f"{u}_mask_i", [128, G, L], I32)
            mask_f = sb(f"{u}_mask_f", [128, G, L])
            mask_bf, maskT_bf = sb(f"{u}_mask_bf", [128, G, L], BF16), sb(f"{u}_maskT_bf", [128, G, L], BF16)
            pad_row_u8 = sb(f"{u}_pad_row_u8", [1, N], U8)
            pad_row = sb(f"{u}_pad_row", [1, N])
            pad_col = sb(f"{u}_pad_col", [128, G])
            pad_wide = pad_wides[u]
            hn = sb(f"{u}_hn", [128, G, D])
            hT = sb(f"{u}_hT", [128, N])
            stats, mv = sb(f"{u}_stats", [128, G, 6]), sb(f"{u}_mv", [128, G, 2])
            std, rstd, rms, rms2 = (sb(f"{u}_{n}", [128, G]) for n in ("std", "rstd", "rms", "rms2"))
            place = sb(f"{u}_place", [128, G], U32)
            s_scatter = sem(f"rows_placed{u}")
            s_in, s_out, s_ctx = sem(f"group{u}_loaded"), sem(f"group{u}_stored"), sem(f"context{u}_loaded")
            s_stored, s_stack = sem(f"parts_stored{u}"), sem(f"parts_stacked{u}")
            stack_d = [nc.dram_tensor(f"stack_{k}{u}", (2, 6, 64, N), BF16, kind="Internal").ap() for k in "qk"]
            stacks, norms = {}, {}
            ACC = RING_BANKS + u
            ctx = f"{u}.ctx"

            shared = {}

            def share(**counts):
                base = {n: shared.get(n, 0) for n in counts}
                shared.update({n: base[n] + counts[n] for n in counts})
                return base

            def norm(nm):
                return norms.setdefault(nm, len(norms))

            def norm_pe(pe, nm):
                yield NORMED
                t = P.open(pe, nm + ".hT")
                for s in range(G):
                    pe.wait_ge(ev(f"{u}.hn"), G * norm(nm) + s + 1)
                    last = pe.transpose(t[:, col(s)], hn[:, s, :], ident[:])
                P.close(last, nm + ".hT")

            def norm_act(act, nm, rms_too=False):
                act.wait_ge(ev(f"{u}.var"), norm(nm) + 1)
                act.activation(std[:], mv[:, :, 1], ACT.Sqrt, bias=eps5[:]).then_inc(ev(f"{u}.std"), 1)
                if rms_too:
                    act.wait_ge(ev(nm + ".ms"), 1)
                    act.activation(rms2[:], rms[:], ACT.Sqrt, bias=eps6[:]).then_inc(ev(nm + ".rms"), 1)
                yield NORMED
                t = P.take(act, nm + ".hT")
                P.give(act.copy(hT[:], t), nm + ".hT")

            def norm_dve(dve, q, nm, rms_too=False):
                for s in range(G):
                    m = q.mark(dve.bn_stats(stats[:, s, :], xres[:, s, :]))
                for s in range(G):
                    q.wait(m - G + 1 + s)
                    ins = dve.bn_aggr(mv[:, s, :], stats[:, s, :])
                    if s < G - 1:
                        m2 = q.mark(ins)
                ins.then_inc(ev(f"{u}.var"), 1)
                dve.wait_ge(ev(f"{u}.var"), norm(nm) + 1)
                dve.wait_ge(ev(f"{u}.std"), norm(nm) + 1)
                q.link(dve.reciprocal(rstd[:], std[:]))
                if rms_too:
                    q.link(dve.tensor_tensor(rms[:], mv[:, :, 1], rstd[:], ALU.mult))
                    dve.tensor_tensor(rms[:], rms[:], rstd[:], ALU.mult).then_inc(ev(nm + ".ms"), 1)
                    dve.wait_ge(ev(nm + ".rms"), 1)
                    q.link(dve.reciprocal(rms[:], rms2[:]))
                    q.link(dve.tensor_tensor(rstd[:], rstd[:], rms[:], ALU.mult))
                for s in range(G):
                    dve.tensor_scalar(hn[:, s, :], xres[:, s, :], mv[:, s, 0:1], rstd[:, s:s + 1],
                                      ALU.subtract, ALU.mult).then_inc(ev(f"{u}.hn"), 1)

            def residual_dve(dve, q, name):
                t = P.take(dve, name)
                P.give(dve.tensor_tensor(xres[:].rearrange("p s f -> p (s f)"), xres[:].rearrange("p s f -> p (s f)"), t,
                                         ALU.add), name)
                P.wait_given(dve, name)

            def bias_row(pe, t, row, start=True):
                w = row.shape[-1]
                pe.matmul(t[:, 0:G * w].rearrange("p (s f) -> p s f", s=G), ones_row[:],
                          spread(row, G), start=start, stop=False, skip_group_check=True)

            def ctx_pe(pe):
                pe.wait_ge(s_ctx, 48)
                t = P.open(pe, ctx + ".T")
                for s in range(G):
                    last = pe.transpose(t[:, col(s)], ctx_tok[:, s, :], ident[:])
                P.close(last, ctx + ".T")
                t = P.open(pe, ctx + ".maskT")
                pe.wait_ge(ev(ctx + ".maskf"), 1)
                for s in range(G):
                    last = pe.transpose(t[:, col(s)], mask_f[:, s, :], ident[:])
                P.close(last, ctx + ".maskT")
                t = P.open(pe, ctx + ".pad")
                pe.wait_ge(ev(ctx + ".padrow"), 1)
                for s in range(G):
                    last = pe.matmul(t[:, s:s + 1], pad_row[:, col(s)], ones_row[:, 0:1], start=True, stop=True)
                P.close(last, ctx + ".pad")
                t = P.open(pe, ctx + ".nT")
                pe.wait_ge(ev(ctx + ".n"), 1)
                for s in range(G):
                    last = pe.transpose(t[:, col(s)], scratch[:, col(s)], ident[:])
                P.close(last, ctx + ".nT")

            def ctx_act(act, q):
                act.wait_ge(s_ctx, 48)
                for s in range(G):
                    last = act.activation(scratch[:, N + s * L:N + (s + 1) * L], ctx_tok[:, s, :], ACT.Square,
                                          accum_out=rms[:, s:s + 1])
                last.then_inc(ev(ctx + ".sq"), 1)
                act.wait_ge(ev(ctx + ".sq"), 1)
                act.activation(rms2[:], rms[:], ACT.Sqrt, scale=1.0 / D, bias=eps6[:]).then_inc(ev(ctx + ".rms"), 1)
                t = P.take(act, ctx + ".T")
                P.give(act.copy(ctxT[:], t), ctx + ".T")
                t = P.take(act, ctx + ".maskT")
                P.give(act.copy(maskT_bf[:].rearrange("p s f -> p (s f)"), t), ctx + ".maskT")
                t = P.take(act, ctx + ".pad")
                P.give(act.copy(pad_col[:], t[:, 0:G]), ctx + ".pad")
                t = P.take(act, ctx + ".nT")
                P.give(act.copy(ctxnT[:], t), ctx + ".nT")

            def ctx_dve(dve, q):
                dve.wait_ge(s_ctx, 48)
                dve.tensor_scalar(mask_f[:], mask_i[:], -1.0, None, ALU.add).then_inc(ev(ctx + ".maskf"), 1)
                dve.tensor_scalar(pad_row[:], pad_row_u8[:], -1.0, BIG, ALU.add, ALU.mult).then_inc(ev(ctx + ".padrow"), 1)
                dve.wait_ge(ev(ctx + ".maskf"), 1)
                q.link(dve.tensor_copy(mask_bf[:], mask_f[:]))
                dve.wait_ge(ev(ctx + ".padrow"), 1)
                q.link(dve.tensor_copy(pad_wide[0:1, :], pad_row[:]))
                dve.wait_ge(ev(ctx + ".rms"), 1)
                q.link(dve.reciprocal(rstd[:], rms2[:]))
                for s in range(G):
                    last = dve.tensor_scalar(scratch[:, col(s)], ctx_tok[:, s, :], rstd[:, s:s + 1], None, ALU.mult)
                last.then_inc(ev(ctx + ".n"), 1)
                P.wait_given(dve, ctx + ".T")
                q.link(dve.reduce_sum(ctx_sum[:], row_tiles(ctxT[:]), X))
                P.wait_given(dve, ctx + ".nT")

            def attention16(nm, w, src=None, bias=False, bias_out=False, rope=False, mask=None):
                base = share(sum=2 if rope else 0)
                at = stacks.setdefault(nm, len(stacks))
                S = Scratch(scratch)
                qk = [S.take(N) for _ in range(2)]
                rest = [S.take(N) for _ in range(2)]
                parts = [S.take(3 * N, BF16).rearrange("p (k t) -> p k t", k=3) for _ in range(2)]
                stack = [S.take(NH // 2 * N, BF16).rearrange("p (a t) -> p a t", t=N) for _ in range(2)]
                pT_flat = S.take(2 * NH * L)
                pT = pT_flat.rearrange("p (b j f) -> p b j f", b=2, j=NJ)
                vaug = S.take(G * NH * (DH + 1)).rearrange("p (s h e) -> p s h e", s=G, h=NH)
                negm, mrest = (S.take(G * NH).rearrange("p (s h) -> p s h", s=G) for _ in range(2))
                mparts = S.take(N, BF16).rearrange("p (s f) -> p s f", s=G)
                mT = S.take(N, BF16)
                rden = S.take(G * NH).rearrange("p (s h) -> p s h", s=G)
                osb = S.take(N)
                oT = S.take(N)
                rq = [pT_flat[:, k * N:(k + 1) * N] for k in range(4)]
                src_ap = ctxT if src == "ctx" else hT

                def head_of(j, i):
                    return 8 * (j // 2) + 2 * i + j % 2

                def masking(pe, t, turned, s):
                    v = row_tiles(t)
                    last = None
                    if mask == "causal":
                        last = pe.matmul(v, ident_bf[:], spread((causal_T_bf if turned else causal_bf)[:], NI),
                                         start=False, stop=not turned, skip_group_check=True)
                    if mask == "given":
                        for c in (ident_big, ident_small):
                            last = pe.matmul(v, c[:], spread((maskT_bf if turned else mask_bf)[:, s, :], NI), start=False,
                                             stop=c is ident_small and not turned, skip_group_check=True)
                    return last

                def pe_f(pe):
                    yield from norm_pe(pe, nm)
                    yield 5
                    P.wait_given(pe, nm + ".hT")
                    todo = [("q", "Wq", hT), ("k", "Wk", src_ap)]
                    if rope:
                        todo = [("q", "Wq", hT), ("qs", "Wq_swap", hT), ("k", "Wk", hT), ("ks", "Wk_swap", hT)]
                    for name, wn, s_ in todo:
                        t = P.open(pe, f"{nm}.{name}")
                        P.close(pe.matmul(t, W[w + wn][:], s_[:], start=True, stop=True), f"{nm}.{name}")
                    t = P.open(pe, nm + ".v")
                    if bias:
                        bias_row(pe, t, W[w + "bv"][:])
                    for s in range(G):
                        last = pe.matmul(t[:, col(s)], src_ap[:, col(s)], W[w + "Wv"][:], start=not bias, stop=True,
                                         skip_group_check=True)
                    P.close(last, nm + ".v")

                    def products(s, letter, lhs, rhs, close):
                        for jj in range(0, NJ, 2):
                            t = [P.open(pe, f"{nm}.{letter}{s}{jj + par}", width=NI * L) for par in range(2)]
                            for i in range(NI):
                                for par in range(2):
                                    h = head_of(jj + par, i)
                                    r = slice(64 * par, 64 * par + 48)
                                    last = pe.matmul(t[par][:, i * L:(i + 1) * L], lhs[r, h // 2, col(s)],
                                                     rhs[r, h // 2, col(s)], start=i == 0, stop=close,
                                                     skip_group_check=True)
                                    if close and i == NI - 1:
                                        P.close(last, f"{nm}.{letter}{s}{jj + par}")

                    def scores(s):
                        if s == 0:
                            pe.wait_ge(s_stack, 16 * 4 * (at + 1))
                        products(s, "S", stack[0], stack[1], mask is None)
                        if mask:
                            for j in range(NJ):
                                P.close(masking(pe, P.bank(f"{nm}.S{s}{j}"), False, s), f"{nm}.S{s}{j}")

                    def turned(s):
                        products(s, "T", stack[1], stack[0], False)
                        pe.wait_ge(ev(f"{u}.mparts"), G * at + s + 1)
                        t = P.open(pe, f"{nm}.mT{s}")
                        P.close(pe.transpose(t.bitcast(BF16)[:, 0:L], mparts[:, s, :], ident_bf[:]), f"{nm}.mT{s}")
                        for j in range(NJ):
                            masking(pe, P.bank(f"{nm}.T{s}{j}"), True, s)
                        P.wait_given(pe, f"{nm}.mT{s}")
                        for j in range(NJ):
                            t = P.bank(f"{nm}.T{s}{j}")
                            for i in range(NI):
                                a = NI * j + i
                                last = pe.matmul(t[:, i * L:(i + 1) * L], sel_part[:, a:a + 1].broadcast_to([128, 128]),
                                                 mT[:, col(s)], start=False, stop=i == NI - 1, skip_group_check=True)
                            P.close(last, f"{nm}.T{s}{j}")

                    def values(s):
                        if s == 0:
                            P.wait_given(pe, nm + ".v")
                            pe.wait_ge(ev(f"{u}.ones"), 2 * at + 1)
                        t = P.open(pe, f"{nm}.O{s}")
                        for j in range(NJ):
                            P.wait_given(pe, f"{nm}.T{s}{j}")
                            for i in range(NI):
                                h = head_of(j, i)
                                last = pe.matmul(t[:, h * 9:h * 9 + 9], pT[:, s % 2, j, i * L:(i + 1) * L],
                                                 vaug[:, s, h, :], start=True, stop=True, skip_group_check=True)
                        P.close(last, f"{nm}.O{s}")

                    for step in range(G + 2):
                        yield STACKED + SEQ16 * step
                        if step < G:
                            scores(step)
                        if step >= 2:
                            values(step - 2)
                        if 1 <= step <= G:
                            turned(step - 1)
                    yield STACKED + SEQ16 * (G + 2)
                    t = P.open(pe, nm + ".oT")
                    for s in range(G):
                        P.wait_given(pe, f"{nm}.O{s}")
                        last = pe.transpose(t[:, col(s)], osb[:, col(s)], ident[:])
                    P.close(last, nm + ".oT")
                    yield STACKED + SEQ16 * (G + 2) + 2
                    P.wait_given(pe, nm + ".oT")
                    t = P.open(pe, nm + ".y", ACC)
                    if bias_out:
                        bias_row(pe, t, W[w + "bo"][:])
                    for s in range(G):
                        last = pe.matmul(t[:, col(s)], oT[:, col(s)], W[w + "Wo"][:], start=not bias_out, stop=True,
                                         skip_group_check=True)
                    P.close(last, nm + ".y")

                def act_f(act, q):
                    yield from norm_act(act, nm)
                    yield 5
                    if not rope:
                        t = P.take(act, nm + ".q")
                        bq = W[w + "bq"][:] if bias else 0.0
                        P.give(act.activation(qk[0], t, ACT.Identity, bias=bq), nm + ".q")
                    for k in range(2):
                        if rope:
                            act.wait_ge(ev(f"{u}.sum"), base["sum"] + k + 1)
                        else:
                            P.wait_given(act, f"{nm}.{'qk'[k]}")
                        act.copy(parts[k][:, 0, :], qk[k]).then_inc(ev(f"{u}.part1"), 1)
                    for k in range(2):
                        act.wait_ge(ev(f"{u}.rest"), 2 * at + k + 1)
                        act.copy(parts[k][:, 1, :], rest[k]).then_inc(ev(f"{u}.part2"), 1)
                    t = P.take(act, nm + ".v")
                    P.give(act.copy(vaug[:, :, :, 0:DH], t.rearrange("p (s h e) -> p s h e", s=G, h=NH)), nm + ".v")
                    for s in range(G):
                        yield STACKED + SEQ16 * (s + 1)
                        t = P.take(act, f"{nm}.mT{s}")
                        P.give(act.copy(mT[:, col(s)], t.bitcast(BF16)[:, 0:L]), f"{nm}.mT{s}")
                        if s >= 2:
                            P.take(act, f"{nm}.O{s - 2}")
                        for j in range(NJ):
                            t = P.take(act, f"{nm}.T{s}{j}")
                            P.give(act.activation(pT[:, s % 2, j, :], t, ACT.Exp), f"{nm}.T{s}{j}")
                    yield STACKED + SEQ16 * (G + 2)
                    t = P.take(act, nm + ".oT")
                    P.give(act.copy(oT, t), nm + ".oT")

                def dve_f(dve, q):
                    norm_dve(dve, q, nm)
                    yield 5
                    if rope:
                        for k, name in enumerate(("q", "qs", "k", "ks")):
                            t = P.take(dve, f"{nm}.{name}")
                            P.give(dve.tensor_tensor(row_tiles(rq[k]), row_tiles(t), spread(W["rope2"][:, k, :], G),
                                                     ALU.mult), f"{nm}.{name}")
                            if k % 2:
                                P.wait_given(dve, f"{nm}.{name}")
                                dve.tensor_tensor(qk[k // 2], rq[k - 1], rq[k], ALU.add).then_inc(ev(f"{u}.sum"), 1)
                    else:
                        t = P.take(dve, nm + ".k")
                        if bias:
                            ins = dve.tensor_scalar(qk[1], t, W[w + "bk"][:], SCALE16, ALU.add, ALU.mult)
                        else:
                            ins = dve.tensor_scalar(qk[1], t, SCALE16, None, ALU.mult)
                        P.give(ins, nm + ".k")
                    for k in range(2):
                        dve.wait_ge(ev(f"{u}.part1"), 2 * at + k + 1)
                        dve.tensor_tensor(rest[k], qk[k], parts[k][:, 0, :], ALU.subtract).then_inc(ev(f"{u}.rest"), 1)
                    for k in range(2):
                        dve.wait_ge(ev(f"{u}.part2"), 2 * at + k + 1)
                        dve.tensor_tensor(parts[k][:, 2, :], rest[k], parts[k][:, 1, :],
                                          ALU.subtract).then_inc(ev(f"{u}.part3"), 1)
                    yield STACKED
                    dve.wait_ge(ev(f"{u}.ones"), 2 * at + 2)

                    def maxima(s):
                        for j in range(NJ):
                            t = P.take(dve, f"{nm}.S{s}{j}")
                            P.give(dve.tensor_reduce(negm[:, s, NI * j:NI * j + NI], row_tiles(t), X, ALU.max,
                                                     negate=True), f"{nm}.S{s}{j}")
                        P.wait_given(dve, f"{nm}.S{s}{NJ - 1}")
                        m, r = negm[:, s, :], mrest[:, s, :]
                        q.link(dve.tensor_copy(mparts[:, s, 0:NH], m))
                        q.link(dve.tensor_tensor(r, m, mparts[:, s, 0:NH], ALU.subtract))
                        q.link(dve.tensor_copy(mparts[:, s, 32:32 + NH], r))
                        dve.tensor_tensor(mparts[:, s, 64:64 + NH], r, mparts[:, s, 32:32 + NH],
                                          ALU.subtract).then_inc(ev(f"{u}.mparts"), 1)

                    def divide(s):
                        t = P.take(dve, f"{nm}.O{s}")[:, 0:NH * 9].rearrange("p (h e) -> p h e", h=NH)
                        q.link(dve.reciprocal(rden[:, s, :], t[:, :, DH]))
                        P.give(dve.tensor_tensor(osb[:, col(s)].rearrange("p (h e) -> p h e", h=NH), t[:, :, 0:DH],
                                                 spread(rden[:, s, :], DH, 2), ALU.mult), f"{nm}.O{s}")

                    for step in range(G + 2):
                        yield STACKED + SEQ16 * step
                        if step < G:
                            maxima(step)
                        if step >= 2:
                            divide(step - 2)
                    yield STACKED + SEQ16 * (G + 2) + 2
                    residual_dve(dve, q, nm + ".y")

                def pool_f(pool, q):
                    pool.wait_ge(ev(f"{u}.hn"), G * norm(nm) + 1)
                    pool.memset(vaug[:, :, :, DH:DH + 1], 1.0).then_inc(ev(f"{u}.ones"), 1)
                    pool.memset(mparts, 0.0).then_inc(ev(f"{u}.ones"), 1)

                def sp_f(sp):
                    yield 5
                    for part in range(3):
                        for k in range(2):
                            sp.wait_ge(ev(f"{u}.part{part + 1}"), 2 * at + k + 1)
                            for par in range(2):
                                dst = stack_d[k][par, SLOTS[part][k]].rearrange("c p t -> p c t")
                                sp.dma_start(dst, spread(parts[k][64 * par:64 * par + 64, part, :], dst.shape[1])
                                             ).then_inc(s_stored, 16)
                    yield 9
                    sp.wait_ge(s_stored, 16 * 12 * (at + 1))
                    for k in range(2):
                        for par in range(2):
                            sp.dma_start(stack[k][64 * par:64 * par + 6 * DH], stack_d[k][par].rearrange(
                                "c (r a) t -> (c r) a t", r=DH)).then_inc(s_stack, 16)

                return pe_f, act_f, dve_f, pool_f, sp_f

            def nothing(*_):
                pass

            def ffn(nm):
                S = Scratch(scratch)
                nch = FFH // 128
                act_out = S.take(nch * N).rearrange("p (c t) -> p c t", c=nch)
                hid = S.take(nch * N).rearrange("p (c t) -> p c t", c=nch)

                def pe_f(pe):
                    yield from norm_pe(pe, nm)
                    yield 5
                    P.wait_given(pe, nm + ".hT")
                    for c in range(nch):
                        for k in ("gate", "up"):
                            t = P.open(pe, f"{nm}.{k}{c}")
                            P.close(pe.matmul(t, fw[k][:, c * 128:(c + 1) * 128], hT[:], start=True, stop=True),
                                    f"{nm}.{k}{c}")
                    yield 10
                    for c in range(nch):
                        P.wait_given(pe, f"{nm}.up{c}")
                    t = P.open(pe, nm + ".y", ACC)
                    for s in range(G):
                        for c in range(nch):
                            last = pe.matmul(t[:, col(s)], hid[:, c, col(s)], fw["down"][:, c, :], start=c == 0,
                                             stop=c == nch - 1, skip_group_check=True)
                    P.close(last, nm + ".y")

                def act_f(act, q):
                    yield from norm_act(act, nm)
                    yield 5
                    for c in range(nch):
                        t = P.take(act, f"{nm}.gate{c}")
                        P.give(act.activation(act_out[:, c, :], t, ACT.Silu), f"{nm}.gate{c}")

                def dve_f(dve, q):
                    norm_dve(dve, q, nm)
                    yield 5
                    for c in range(nch):
                        P.wait_given(dve, f"{nm}.gate{c}")
                        t = P.take(dve, f"{nm}.up{c}")
                        P.give(dve.tensor_tensor(hid[:, c, :], act_out[:, c, :], t, ALU.mult), f"{nm}.up{c}")
                    yield 10
                    residual_dve(dve, q, nm + ".y")

                return pe_f, act_f, dve_f, nothing, nothing

            def mixer(nm):
                S = Scratch(scratch)
                mean_wide = S.take(N)

                def pe_f(pe):
                    yield from norm_pe(pe, nm)
                    yield 5
                    P.wait_given(pe, nm + ".hT")
                    t = P.open(pe, nm + ".y", ACC)
                    bias_row(pe, t, W["m_b"][:])
                    pe.wait_ge(ev(nm + ".mean"), 1)
                    for s in range(G):
                        pe.matmul(t[:, col(s)], hT[:, col(s)], W["m_W1"][:], start=False, stop=False,
                                  skip_group_check=True)
                        last = pe.matmul(t[:, col(s)], mean_wide[:, col(s)], W["m_W2"][:], start=False, stop=True,
                                         skip_group_check=True)
                    P.close(last, nm + ".y")

                def act_f(act, q):
                    yield from norm_act(act, nm)

                def dve_f(dve, q):
                    norm_dve(dve, q, nm)
                    yield 5
                    dve.tensor_scalar(row_tiles(mean_wide), spread(ctx_sum[:], L, 2), 1.0 / L, None,
                                      ALU.mult).then_inc(ev(nm + ".mean"), 1)
                    residual_dve(dve, q, nm + ".y")

                return pe_f, act_f, dve_f, nothing, nothing

            def first_max(dve, q, onehot, values, top, tmp, width):
                q.link(dve.tensor_reduce(top, values, X, ALU.max))
                q.link(dve.tensor_tensor(tmp, values, spread(top, width, 2), ALU.is_ge))
                q.link(dve.tensor_tensor(tmp, tmp, spread(W["rev"][:, 0:width], G), ALU.mult))
                q.link(dve.tensor_reduce(rms[:], tmp, X, ALU.max))
                q.link(dve.tensor_tensor(onehot, tmp, spread(rms[:], width, 2), ALU.is_equal))

            def gates_pe(pe, nm, gate, width, base):
                pe.wait_ge(ev(f"{u}.gate"), base["gate"] + 1)
                t = P.open(pe, nm + ".gT")
                for s in range(G):
                    last = pe.transpose(t[0:width, col(s)], gate[:, s, :], ident[:])
                P.close(last, nm + ".gT")

            def router_pe(pe, nm, w, width):
                t = P.open(pe, nm + ".router")
                for s in range(G):
                    last = pe.matmul(t[:, s * width:(s + 1) * width], hT[:, col(s)], w, start=True, stop=True,
                                     skip_group_check=True)
                P.close(last, nm + ".router")

            def moe1(nm):
                S = Scratch(scratch)
                base = share(diff=1, exp=1, gate=1, down=len(SCH) + C1 - 1)
                RING = 3
                lg, lg2, oh1, oh2, tmp, gate = (S.take(G * E1).rearrange("p (s e) -> p s e", s=G) for _ in range(6))
                top1, top2, p1, p2, ex = (S.take(G) for _ in range(5))
                gT = S.take(N)
                a_out = S.take(RING * N).rearrange("p (r t) -> p r t", r=RING)
                h_mid = S.take(RING * N).rearrange("p (r t) -> p r t", r=RING)
                hid = S.take(RING * N).rearrange("p (r t) -> p r t", r=RING)
                chunks = [(None, c, r0, rows) for c, (r0, rows) in enumerate(SCH)] + \
                         [("e", c, c * 128, 128) for c in range(C1)]

                def pe_f(pe):
                    yield from norm_pe(pe, nm)
                    yield 5
                    P.wait_given(pe, nm + ".hT")
                    router_pe(pe, nm, W["e1_Wg"][:], E1)

                    def up(n):
                        kind, c, r0, rows = chunks[n]
                        for k, (wa, wb) in enumerate((("e1_Ws1", "e1_W1"), ("e1_Ws2", "e1_W2"))):
                            t = P.open(pe, f"{nm}.u{k}{n}")
                            w = W[wb if kind else wa]
                            P.close(pe.matmul(t[0:rows, :], w[:, r0:r0 + rows], hT[:], start=True, stop=True),
                                    f"{nm}.u{k}{n}")
                        if kind:
                            if c == 0:
                                gates_pe(pe, nm, gate, E1, base)
                                P.wait_given(pe, nm + ".gT")
                            t = P.open(pe, f"{nm}.g{n}")
                            P.close(pe.matmul(t, W["sel1"][:, r0:r0 + 128], gT[0:E1, :], start=True, stop=True),
                                    f"{nm}.g{n}")

                    def down(n):
                        kind, c, r0, rows = chunks[n]
                        P.wait_given(pe, f"{nm}.g{n}" if kind else f"{nm}.u1{n}")
                        w = W["e1_W3" if kind else "e1_Ws3"]
                        for s in range(G):
                            last = pe.matmul(acc[:, col(s)], hid[0:rows, n % RING, col(s)], w[0:rows, c, :],
                                             start=n == 0 and s == 0, stop=n == len(chunks) - 1, skip_group_check=True)
                        if n < len(chunks) - 1:
                            last.then_inc(ev(f"{u}.down"), 1)
                        return last

                    acc = P.open(pe, nm + ".y", ACC)
                    for n in range(len(chunks) + 1):
                        yield CH1 * n + 8
                        if n < len(chunks):
                            up(n)
                        if n >= 1:
                            last = down(n - 1)
                    P.close(last, nm + ".y")

                def act_f(act, q):
                    yield from norm_act(act, nm)
                    yield 5
                    act.wait_ge(ev(f"{u}.diff"), base["diff"] + 1)
                    act.activation(ex, p1, ACT.Exp).then_inc(ev(f"{u}.exp"), 1)
                    for n, (kind, c, r0, rows) in enumerate(chunks):
                        yield CH1 * n + 8
                        t = P.take(act, f"{nm}.u0{n}")
                        if n >= RING:
                            P.wait_given(act, f"{nm}.u1{n - RING}")
                        P.give(act.activation(a_out[0:rows, n % RING, :], t[0:rows, :], ACT.Silu), f"{nm}.u0{n}")
                        if kind and c == 0:
                            t = P.take(act, nm + ".gT")
                            P.give(act.copy(gT[0:E1, :], t[0:E1, :]), nm + ".gT")

                def dve_f(dve, q):
                    norm_dve(dve, q, nm)
                    yield 5
                    t = P.take(dve, nm + ".router")
                    P.give(dve.tensor_copy(lg, t[:, 0:G * E1].rearrange("p (s e) -> p s e", s=G)), nm + ".router")
                    P.wait_given(dve, nm + ".router")
                    first_max(dve, q, oh1, lg, top1, tmp, E1)
                    q.link(dve.scalar_tensor_tensor(out=lg2, in0=oh1, scalar=-BIG, in1=lg, op0=ALU.mult, op1=ALU.add))
                    first_max(dve, q, oh2, lg2, top2, tmp, E1)
                    dve.tensor_tensor(p1, top2, top1, ALU.subtract).then_inc(ev(f"{u}.diff"), 1)
                    dve.wait_ge(ev(f"{u}.exp"), base["exp"] + 1)
                    q.link(dve.tensor_scalar(p1, ex, 1.0, None, ALU.add))
                    q.link(dve.reciprocal(p1, p1))
                    q.link(dve.tensor_tensor(p2, p1, ex, ALU.mult))
                    q.link(dve.tensor_tensor(oh1, oh1, spread(p1, E1, 2), ALU.mult))
                    q.link(dve.tensor_tensor(oh2, oh2, spread(p2, E1, 2), ALU.mult))
                    dve.tensor_tensor(gate, oh1, oh2, ALU.add).then_inc(ev(f"{u}.gate"), 1)
                    for n, (kind, c, r0, rows) in enumerate(chunks):
                        yield CH1 * n + 8
                        P.wait_given(dve, f"{nm}.u0{n}")
                        t = P.take(dve, f"{nm}.u1{n}")
                        if n >= RING:
                            dve.wait_ge(ev(f"{u}.down"), base["down"] + n - RING + 1)
                        dst = h_mid if kind else hid
                        P.give(dve.tensor_tensor(dst[0:rows, n % RING, :], a_out[0:rows, n % RING, :], t[0:rows, :],
                                                 ALU.mult), f"{nm}.u1{n}")
                        if kind:
                            P.wait_given(dve, f"{nm}.u1{n}")
                            t = P.take(dve, f"{nm}.g{n}")
                            P.give(dve.tensor_tensor(hid[:, n % RING, :], h_mid[:, n % RING, :], t, ALU.mult),
                                   f"{nm}.g{n}")
                    yield CH1 * len(chunks) + 8
                    residual_dve(dve, q, nm + ".y")

                return pe_f, act_f, dve_f, nothing, nothing

            def moe2(nm):
                S = Scratch(scratch)
                base = share(diff=1, exp=1, gate=1)
                RING = 3
                lg, oh, tmp, gate = (S.take(G * E2).rearrange("p (s e) -> p s e", s=G) for _ in range(4))
                top, den = S.take(G), S.take(G)
                gT = S.take(N)
                hid = S.take(RING * 2 * N).rearrange("p (r c t) -> p r c t", r=RING, c=2)
                w1 = experts[:, 0:E2 * F2]
                w2 = experts[:, E2 * F2:2 * E2 * F2].rearrange("p (c f) -> p c f", f=D)

                def pe_f(pe):
                    yield from norm_pe(pe, nm)
                    yield 5
                    P.wait_given(pe, nm + ".hT")
                    router_pe(pe, nm, W["e2_Wr"][:], E2)
                    pe.wait_ge(s_e2, 48)

                    def up(e):
                        for c in range(2):
                            t = P.open(pe, f"{nm}.u{e}.{c}")
                            f0 = e * F2 + c * 128
                            P.close(pe.matmul(t, w1[:, f0:f0 + 128], hT[:], start=True, stop=True), f"{nm}.u{e}.{c}")

                    def down(e):
                        P.wait_given(pe, f"{nm}.u{e}.0")
                        P.wait_given(pe, f"{nm}.u{e}.1")
                        t = P.open(pe, f"{nm}.d{e}")
                        for s in range(G):
                            for c in range(2):
                                last = pe.matmul(t[:, col(s)], hid[:, e % RING, c, col(s)], w2[:, 2 * e + c, :],
                                                 start=c == 0, stop=c == 1, skip_group_check=True)
                        P.close(last, f"{nm}.d{e}")

                    for e in range(E2 + 1):
                        yield CH2 * e + 8
                        if e < E2:
                            up(e)
                        if e >= 1:
                            down(e - 1)
                    yield CH2 * E2 + 10
                    gates_pe(pe, nm, gate, E2, base)
                    P.wait_given(pe, nm + ".gT")
                    t = P.open(pe, nm + ".y", ACC)
                    for s in range(G):
                        last = pe.matmul(t[:, col(s)], gT[0:E2, col(s)], W["e2_b2"][:], start=True, stop=True,
                                         skip_group_check=True)
                    P.close(last, nm + ".y")

                def act_f(act, q):
                    yield from norm_act(act, nm)
                    yield 5
                    act.wait_ge(ev(f"{u}.diff"), base["diff"] + 1)
                    act.activation(lg, tmp, ACT.Exp).then_inc(ev(f"{u}.exp"), 1)
                    for e in range(E2):
                        yield CH2 * e + 8
                        for c in range(2):
                            t = P.take(act, f"{nm}.u{e}.{c}")
                            if e >= RING and c == 0:
                                P.take(act, f"{nm}.d{e - RING}")
                                P.take(act, f"{nm}.u{e}.{c}")
                            P.give(act.activation(hid[:, e % RING, c, :], t, ACT.Gelu,
                                                  bias=W["e2_b1"][:, 2 * e + c:2 * e + c + 1]), f"{nm}.u{e}.{c}")
                    yield CH2 * E2 + 10
                    t = P.take(act, nm + ".gT")
                    P.give(act.copy(gT[0:E2, :], t[0:E2, :]), nm + ".gT")

                def dve_f(dve, q):
                    norm_dve(dve, q, nm)
                    yield 5
                    t = P.take(dve, nm + ".router")
                    P.give(dve.tensor_copy(lg, t[:, 0:G * E2].rearrange("p (s e) -> p s e", s=G)), nm + ".router")
                    P.wait_given(dve, nm + ".router")
                    first_max(dve, q, oh, lg, top, tmp, E2)
                    dve.tensor_tensor(tmp, lg, spread(top, E2, 2), ALU.subtract).then_inc(ev(f"{u}.diff"), 1)
                    dve.wait_ge(ev(f"{u}.exp"), base["exp"] + 1)
                    q.link(dve.tensor_reduce(den, lg, X, ALU.add))
                    q.link(dve.reciprocal(den, den))
                    dve.tensor_tensor(gate, oh, spread(den, E2, 2), ALU.mult).then_inc(ev(f"{u}.gate"), 1)
                    dve.wait_ge(ev(f"{u}.gate"), base["gate"] + 1)
                    for e in range(E2):
                        yield CH2 * (e + 1) + 8
                        t = P.take(dve, f"{nm}.d{e}")
                        for s in range(G):
                            ins = dve.scalar_tensor_tensor(out=xres[:, s, :], in0=t[:, col(s)],
                                                           scalar=gate[:, s, e:e + 1], in1=xres[:, s, :],
                                                           op0=ALU.mult, op1=ALU.add)
                        P.give(ins, f"{nm}.d{e}")
                        P.wait_given(dve, f"{nm}.d{e}")
                    yield CH2 * E2 + 10
                    residual_dve(dve, q, nm + ".y")

                return pe_f, act_f, dve_f, nothing, nothing

            def moe3(nm):
                S = Scratch(scratch)
                base = share(diff=1, exp=1)
                lg, oh, tmp, rank = (S.take(G * E3).rearrange("p (s e) -> p s e", s=G) for _ in range(4))
                top, den, mine = S.take(G), S.take(G), S.take(G)
                scaled = S.take(N).rearrange("p (s f) -> p s f", s=G)

                def pe_f(pe):
                    yield from norm_pe(pe, nm)
                    yield 5
                    P.wait_given(pe, nm + ".hT")
                    router_pe(pe, nm, W["e3_Wr"][:], E3)
                    pe.wait_ge(ev(f"{u}.diff"), base["diff"] + 1)
                    t = P.open(pe, nm + ".rank")
                    for s in range(G):
                        for k in range(s):
                            pe.matmul(t[:, s * E3:(s + 1) * E3], ones_sq[:], oh[:, k, :], start=k == 0, stop=False,
                                      skip_group_check=True)
                        pe.matmul(t[:, s * E3:(s + 1) * E3], W["before_T"][:], oh[:, s, :], start=s == 0, stop=True,
                                  skip_group_check=True)
                    for k in range(G):
                        last = pe.matmul(t[:, G * E3:(G + 1) * E3], ones_sq[:], oh[:, k, :], start=k == 0,
                                         stop=k == G - 1, skip_group_check=True)
                    P.close(last, nm + ".rank")

                def act_f(act, q):
                    yield from norm_act(act, nm)
                    yield 5
                    act.wait_ge(ev(f"{u}.diff"), base["diff"] + 1)
                    act.activation(lg, tmp, ACT.Exp).then_inc(ev(f"{u}.exp"), 1)

                def dve_f(dve, q):
                    norm_dve(dve, q, nm)
                    yield 5
                    t = P.take(dve, nm + ".router")
                    P.give(dve.tensor_copy(lg, t[:, 0:G * E3].rearrange("p (s e) -> p s e", s=G)), nm + ".router")
                    P.wait_given(dve, nm + ".router")
                    first_max(dve, q, oh, lg, top, tmp, E3)
                    dve.tensor_tensor(tmp, lg, spread(top, E3, 2), ALU.subtract).then_inc(ev(f"{u}.diff"), 1)
                    t = P.take(dve, nm + ".rank")
                    q.link(dve.tensor_tensor(rank, t[:, 0:G * E3].rearrange("p (s e) -> p s e", s=G),
                                             spread(counts[:], G), ALU.add))
                    P.give(dve.tensor_tensor(counts[:], t[:, G * E3:(G + 1) * E3], counts[:], ALU.add), nm + ".rank")
                    q.link(dve.tensor_tensor(rank, rank, oh, ALU.mult))
                    q.link(dve.tensor_reduce(mine, rank, X, ALU.add))
                    q.link(dve.tensor_scalar(mine, mine, float(CAP), float(2 * E3 * CAP), ALU.is_ge, ALU.mult))
                    q.link(dve.tensor_tensor(oh, oh, spread(W["first_place"][:], G), ALU.mult))
                    q.link(dve.tensor_tensor(rank, rank, oh, ALU.add))
                    q.link(dve.tensor_reduce(top, rank, X, ALU.add))
                    q.link(dve.tensor_tensor(top, top, mine, ALU.add))
                    dve.wait_ge(ev(f"{u}.exp"), base["exp"] + 1)
                    q.link(dve.tensor_reduce(den, lg, X, ALU.add))
                    q.link(dve.reciprocal(den, den))
                    dve.tensor_copy(place[:], top).then_inc(ev(nm + ".placed"), 1)
                    for s in range(G):
                        dve.tensor_scalar(scaled[:, s, :], hn[:, s, :], den[:, s:s + 1], None,
                                          ALU.mult).then_inc(ev(nm + ".placed"), 1)

                def pool_f(pool, q):
                    yield 5
                    pool.wait_ge(ev(nm + ".placed"), G + 1)
                    pool.wait_ge(s_zero, 16)
                    for s in range(G):
                        pool.indirect_dma_start(
                            expert_in, bass.IndirectOffsetOnAxis(place[:, s:s + 1], 0), scaled[:, s, :], None,
                            bounds_check=E3 * CAP - 1, oob_is_err=False).then_inc(s_scatter, 16)

                return pe_f, act_f, dve_f, pool_f, nothing

            def cross3(nm):
                H3, DV = 4, 32
                S = Scratch(scratch)
                r = [S.take(N) for _ in range(4)]
                qT, kT = S.take(N), S.take(N)
                vaug = S.take(G * (DV + 1)).rearrange("p (s e) -> p s e", s=G)
                negm = S.take(N).rearrange("p (s h) -> p s h", s=G)
                mT = S.take(N)
                pT = S.take(2 * H3 * L).rearrange("p (b f) -> p b f", b=2)
                rden = S.take(G * H3).rearrange("p (s h) -> p s h", s=G)
                osb, oT = S.take(N), S.take(N)

                def pe_f(pe):
                    yield from norm_pe(pe, nm)
                    yield 5
                    P.wait_given(pe, nm + ".hT")
                    for name, wn, src in (("q", "Wq", hT), ("qs", "Wq_swap", hT), ("k", "Wk", ctxnT),
                                          ("ks", "Wk_swap", ctxnT)):
                        t = P.open(pe, f"{nm}.{name}")
                        P.close(pe.matmul(t, W["x3_" + wn][:], src[:], start=True, stop=True), f"{nm}.{name}")
                    t = P.open(pe, nm + ".v")
                    for s in range(G):
                        last = pe.matmul(t[:, s * DV:(s + 1) * DV], ctxnT[:, col(s)], W["x3_Wv"][:], start=True,
                                         stop=True, skip_group_check=True)
                    P.close(last, nm + ".v")
                    yield 10
                    pe.wait_ge(ev(nm + ".qk"), 1)

                    def scores(s):
                        for h in range(H3):
                            t = P.open(pe, f"{nm}.S{s}{h}")
                            rr = slice(32 * h, 32 * h + 32)
                            pe.matmul(t[:, 0:L], qT[rr, col(s)], kT[rr, col(s)], start=True, stop=False,
                                      skip_group_check=True)
                            P.close(pe.matmul(t[:, 0:L], ones_first[:], pad_wide[:, col(s)], start=False, stop=True,
                                              skip_group_check=True), f"{nm}.S{s}{h}")

                    def turned(s):
                        for h in range(H3):
                            P.wait_given(pe, f"{nm}.S{s}{h}")
                        t = P.open(pe, f"{nm}.mT{s}")
                        P.close(pe.transpose(t[:, 0:L], negm[:, s, :], ident[:]), f"{nm}.mT{s}")
                        P.wait_given(pe, f"{nm}.mT{s}")
                        for h in range(H3):
                            t = P.open(pe, f"{nm}.T{s}{h}")
                            rr = slice(32 * h, 32 * h + 32)
                            pe.matmul(t[:, 0:L], kT[rr, col(s)], qT[rr, col(s)], start=True, stop=False,
                                      skip_group_check=True)
                            P.close(pe.matmul(t[:, 0:L], ident[:, h:h + 1].broadcast_to([128, 128]), mT[:, col(s)],
                                              start=False, stop=True, skip_group_check=True), f"{nm}.T{s}{h}")

                    def values(s):
                        if s == 0:
                            P.wait_given(pe, nm + ".v")
                        t = P.open(pe, f"{nm}.O{s}")
                        for h in range(H3):
                            P.wait_given(pe, f"{nm}.T{s}{h}")
                            last = pe.matmul(t[:, h * (DV + 1):(h + 1) * (DV + 1)], pT[:, s % 2, h * L:(h + 1) * L],
                                             vaug[:, s, :], start=True, stop=True, skip_group_check=True)
                        P.close(last, f"{nm}.O{s}")

                    for step in range(G + 2):
                        yield 12 + SEQ3 * step
                        if step < G:
                            scores(step)
                        if 1 <= step <= G:
                            turned(step - 1)
                        if step >= 2:
                            values(step - 2)
                    yield 12 + SEQ3 * (G + 2)
                    t = P.open(pe, nm + ".oT")
                    for s in range(G):
                        P.wait_given(pe, f"{nm}.O{s}")
                        last = pe.transpose(t[:, col(s)], osb[:, col(s)], ident[:])
                    P.close(last, nm + ".oT")
                    yield 14 + SEQ3 * (G + 2)
                    P.wait_given(pe, nm + ".oT")
                    t = P.open(pe, nm + ".y", ACC)
                    for s in range(G):
                        last = pe.matmul(t[:, col(s)], oT[:, col(s)], W["x3_Wo"][:], start=True, stop=True,
                                         skip_group_check=True)
                    P.close(last, nm + ".y")

                def act_f(act, q):
                    yield from norm_act(act, nm, True)
                    yield 5
                    t = P.take(act, nm + ".v")
                    P.give(act.copy(vaug[:, :, 0:DV], t[:, 0:G * DV].rearrange("p (s e) -> p s e", s=G)), nm + ".v")
                    for s in range(G):
                        yield 12 + SEQ3 * (s + 1)
                        t = P.take(act, f"{nm}.mT{s}")
                        P.give(act.copy(mT[:, col(s)], t[:, 0:L]), f"{nm}.mT{s}")
                        if s >= 2:
                            P.take(act, f"{nm}.O{s - 2}")
                        for h in range(H3):
                            t = P.take(act, f"{nm}.T{s}{h}")
                            P.give(act.activation(pT[:, s % 2, h * L:(h + 1) * L], t[:, 0:L], ACT.Exp,
                                                  bias=pad_col[:, s:s + 1]), f"{nm}.T{s}{h}")
                    yield 12 + SEQ3 * (G + 2)
                    t = P.take(act, nm + ".oT")
                    P.give(act.copy(oT, t), nm + ".oT")

                def dve_f(dve, q):
                    norm_dve(dve, q, nm, True)
                    yield 5
                    for k, name in enumerate(("q", "qs", "k", "ks")):
                        t = P.take(dve, f"{nm}.{name}")
                        P.give(dve.tensor_tensor(row_tiles(r[k]), row_tiles(t), spread(W["rope3"][:, k, :], G),
                                                 ALU.mult), f"{nm}.{name}")
                    dve.wait_ge(ev(nm + ".ones"), 2)
                    for step in range(G + 2):
                        yield 12 + SEQ3 * step
                        if step < G:
                            s = step
                            for h in range(H3):
                                t = P.take(dve, f"{nm}.S{s}{h}")
                                P.give(dve.tensor_reduce(negm[:, s, h:h + 1], t[:, 0:L], X, ALU.max, negate=True),
                                       f"{nm}.S{s}{h}")
                        if step >= 2:
                            s = step - 2
                            t = P.take(dve, f"{nm}.O{s}")[:, 0:H3 * (DV + 1)].rearrange("p (h e) -> p h e", h=H3)
                            q.link(dve.reciprocal(rden[:, s, :], t[:, :, DV]))
                            P.give(dve.tensor_tensor(osb[:, col(s)].rearrange("p (h e) -> p h e", h=H3), t[:, :, 0:DV],
                                                     spread(rden[:, s, :], DV, 2), ALU.mult), f"{nm}.O{s}")
                    yield 14 + SEQ3 * (G + 2)
                    residual_dve(dve, q, nm + ".y")

                def pool_f(pool, q):
                    pool.wait_ge(ev(f"{u}.hn"), G * norm(nm) + 1)
                    pool.memset(vaug[:, :, DV:DV + 1], 1.0).then_inc(ev(nm + ".ones"), 1)
                    pool.memset(negm[:, :, H3:], 0.0).then_inc(ev(nm + ".ones"), 1)
                    yield 5
                    for k, name in ((0, "q"), (1, "qs"), (2, "k"), (3, "ks")):
                        P.wait_given(pool, f"{nm}.{name}")
                    pool.tensor_tensor(qT, r[0], r[1], ALU.add)
                    pool.tensor_tensor(kT, r[2], r[3], ALU.add).then_inc(ev(nm + ".qk"), 1)

                return pe_f, act_f, dve_f, pool_f, nothing

            def mamba(nm):
                S = Scratch(scratch)
                base = share(zero=1, conv=2, sum=DS)
                xpad = S.take(2 * G * (L + 3)).rearrange("p (c s t) -> p c s t", c=2, s=G)
                xc, z, delta, du, pos, neg = (S.take(2 * N).rearrange("p (c t) -> p c t", c=2) for _ in range(6))
                dstart, yacc = neg, pos
                dtr = du
                RING = 2
                rings = S.take(4 * RING * 2 * N)
                decay, inp, state, yc = (rings[:, k * RING * 2 * N:(k + 1) * RING * 2 * N].rearrange(
                    "p (r j t) -> p r j t", r=RING, j=2) for k in range(4))
                ysum = S.take(4 * N).rearrange("p (c j t) -> p c j t", c=2, j=2)
                parts = S.take(4 * N, BF16).rearrange("p (k c t) -> p k c t", k=2, c=2)
                rest = rings[:, 0:4 * N].rearrange("p (k c t) -> p k c t", k=2, c=2)
                pairs = [(k, c) for c in range(2) for k in range(2)]
                steps = [(c, n) for c in range(2) for n in range(0, DS, 2)]

                def pe_f(pe):
                    yield from norm_pe(pe, nm)
                    yield 5
                    P.wait_given(pe, nm + ".hT")
                    for m in range(4):
                        t = P.open(pe, f"{nm}.in{m}")
                        P.close(pe.matmul(t, W["s_in"][:, m * 128:(m + 1) * 128], hT[:], start=True, stop=True),
                                f"{nm}.in{m}")
                    yield 9
                    for c in range(2):
                        pe.wait_ge(ev(nm + ".xc"), c + 1)
                        t = P.open(pe, f"{nm}.dtr{c}")
                        P.close(pe.matmul(t[0:2 * DS, :], W["s_x"][:, c * 32:c * 32 + 32], xc[:, c, :],
                                          start=True, stop=True), f"{nm}.dtr{c}")
                    for k, c in pairs:
                        t = P.open(pe, f"{nm}.rows{k}{c}")
                        P.close(pe.matmul(t[0:96, :], W["s_bc"][:, (k * 2 + c) * 96:(k * 2 + c) * 96 + 96], xc[:, c, :],
                                          start=True, stop=True), f"{nm}.rows{k}{c}")
                    for c in range(2):
                        P.wait_given(pe, f"{nm}.dtr{c}")
                        t = P.open(pe, f"{nm}.dt{c}")
                        P.close(pe.matmul(t, W["s_dt"][:, c * 128:(c + 1) * 128], dtr[0:2 * DS, c, :],
                                          start=True, stop=True), f"{nm}.dt{c}")
                    for c, n in steps:
                        yield 24 + CHS * (16 * c + n)
                        if n == 0:
                            pe.wait_ge(ev(nm + ".parts"), 1)
                        for k in (1, 2):
                            t = P.open(pe, f"{nm}.bc{k}.{c}.{n}", width=2 * N)
                            for j in range(2):
                                last = pe.matmul(t[:, j * N:(j + 1) * N], sel_state[:, n + j, :],
                                                 parts[0:96, k - 1, c, :], start=True, stop=True,
                                                 skip_group_check=True)
                            P.close(last, f"{nm}.bc{k}.{c}.{n}")
                    yield 25 + CHS * 32
                    pe.wait_ge(ev(nm + ".gated"), 1)
                    t = P.open(pe, nm + ".y", ACC)
                    for s in range(G):
                        for c in range(2):
                            last = pe.matmul(t[:, col(s)], yacc[:, c, col(s)], W["s_out"][:, c, :], start=c == 0,
                                             stop=c == 1, skip_group_check=True)
                    P.close(last, nm + ".y")

                def act_f(act, q):
                    yield from norm_act(act, nm)
                    yield 5
                    act.wait_ge(ev(f"{u}.zero"), base["zero"] + 1)
                    for c in range(2):
                        t = P.take(act, f"{nm}.in{c}")
                        P.give(act.copy(xpad[:, c, :, 3:], row_tiles(t)), f"{nm}.in{c}")
                    for c in range(2):
                        t = P.take(act, f"{nm}.in{2 + c}")
                        P.give(act.activation(z[:, c, :], t, ACT.Silu), f"{nm}.in{2 + c}")
                    for c in range(2):
                        act.wait_ge(ev(f"{u}.conv"), base["conv"] + c + 1)
                        act.activation(xc[:, c, :], delta[:, c, :], ACT.Silu,
                                       bias=W["s_conv_b"][:, c:c + 1]).then_inc(ev(nm + ".xc"), 1)
                    yield 9
                    for c in range(2):
                        t = P.take(act, f"{nm}.dtr{c}")
                        P.give(act.copy(dtr[0:2 * DS, c, :], t[0:2 * DS, :]), f"{nm}.dtr{c}")
                    for k, c in pairs:
                        t = P.take(act, f"{nm}.rows{k}{c}")
                        act.copy(parts[0:96, k, c, :], t[0:96, :]).then_inc(ev(nm + ".high"), 1)
                    act.wait_ge(ev(nm + ".high"), 4)
                    for k, c in pairs:
                        P.wait_given(act, f"{nm}.rows{k}{c}")
                    act.copy(parts[32:64], rest[32:64])
                    act.copy(parts[64:96], rest[64:96]).then_inc(ev(nm + ".high"), 1)
                    for c in range(2):
                        t = P.take(act, f"{nm}.dt{c}")
                        b = W["s_dt_b"][:, c:c + 1]
                        q.mark(act.activation(pos[:, c, :], t, ACT.Relu, bias=b))
                        P.give(act.activation(neg[:, c, :], t, ACT.Abs, bias=b), f"{nm}.dt{c}")
                    P.wait_given(act, nm + ".dt1")
                    q.link(act.activation(neg[:], neg[:], ACT.Exp, scale=-1.0))
                    act.activation(neg[:], neg[:], ACT.Ln, bias=ones_col[:]).then_inc(ev(nm + ".soft"), 1)
                    yield 24
                    act.wait_ge(ev(nm + ".start"), 1)
                    for k, (c, n) in enumerate(steps):
                        yield 24 + CHS * (16 * c + n)
                        if k >= RING:
                            act.wait_ge(ev(nm + ".state"), k - RING + 1)
                        for j in range(2):
                            ins = act.activation(decay[:, k % RING, j, :], dstart[:, c, :], ACT.Exp,
                                                 scale=ssm_A[:, c, n + j:n + j + 1])
                        ins.then_inc(ev(nm + ".decay"), 1)

                def dve_f(dve, q):
                    norm_dve(dve, q, nm)
                    yield 5
                    w = W["s_conv_w"]
                    for c in range(2):
                        P.wait_given(dve, f"{nm}.in{c}")
                    for k in range(CONV_K):
                        for c in range(2):
                            dst = row_tiles(delta[:, c, :])
                            src = xpad[:, c, :, k:k + L]
                            if k == 0:
                                ins = dve.tensor_scalar(dst, src, w[:, c, k:k + 1], None, ALU.mult)
                            else:
                                q.wait(m[c])
                                ins = dve.scalar_tensor_tensor(out=dst, in0=src, scalar=w[:, c, k:k + 1], in1=dst,
                                                               op0=ALU.mult, op1=ALU.add)
                            if k == 0 and c == 0:
                                m = [0, 0]
                            if k < CONV_K - 1:
                                m[c] = q.mark(ins)
                            else:
                                ins.then_inc(ev(f"{u}.conv"), 1)
                    yield 9
                    for n, (k, c) in enumerate(pairs):
                        dve.wait_ge(ev(nm + ".high"), n + 1)
                        t = P.take(dve, f"{nm}.rows{k}{c}")
                        P.give(dve.tensor_tensor(rest[0:96, k, c, :], t[0:96, :], parts[0:96, k, c, :], ALU.subtract),
                               f"{nm}.rows{k}{c}")
                    dve.wait_ge(ev(nm + ".high"), 5)
                    dve.tensor_tensor(parts[64:96], rest[64:96], parts[64:96],
                                      ALU.subtract).then_inc(ev(nm + ".parts"), 1)
                    dve.wait_ge(ev(nm + ".parts"), 1)
                    dve.wait_ge(ev(nm + ".soft"), 1)
                    q.link(dve.tensor_tensor(delta[:], pos[:], neg[:], ALU.add))
                    q.mark(dve.tensor_tensor(du[:], delta[:], xc[:], ALU.mult))
                    q.link(dve.tensor_copy(dstart[:], delta[:]))
                    dve.memset(dstart[:].rearrange("p c (s t) -> p c s t", s=G)[:, :, :, 0:1],
                               BIG).then_inc(ev(nm + ".start"), 1)
                    for k, (c, n) in enumerate(steps):
                        yield 24 + CHS * (16 * c + n)
                        t = P.take(dve, f"{nm}.bc1.{c}.{n}").rearrange("p (j t) -> p j t", j=2)
                        P.give(dve.tensor_tensor(inp[:, k % RING], spread(du[:, c, :], 2), t, ALU.mult),
                               f"{nm}.bc1.{c}.{n}")
                        P.wait_given(dve, f"{nm}.bc1.{c}.{n}")
                        dve.wait_ge(ev(nm + ".decay"), k + 1)
                        flat = [r[:, k % RING].rearrange("p j t -> p (j t)") for r in (state, decay, inp)]
                        dve.tensor_tensor_scan(*flat, 0.0, ALU.mult, ALU.add).then_inc(ev(nm + ".state"), 1)
                        dve.wait_ge(ev(nm + ".state"), k + 1)
                        if k >= RING:
                            dve.wait_ge(ev(f"{u}.sum"), base["sum"] + k - RING + 1)
                        t = P.take(dve, f"{nm}.bc2.{c}.{n}").rearrange("p (j t) -> p j t", j=2)
                        P.give(dve.tensor_tensor(yc[:, k % RING], state[:, k % RING], t, ALU.mult),
                               f"{nm}.bc2.{c}.{n}")
                    yield 25 + CHS * 32
                    dve.wait_ge(ev(f"{u}.sum"), base["sum"] + DS)
                    q.link(dve.tensor_tensor(yacc, ysum[:, :, 0, :], ysum[:, :, 1, :], ALU.add))
                    dve.tensor_tensor(yacc, yacc, z, ALU.mult).then_inc(ev(nm + ".gated"), 1)
                    residual_dve(dve, q, nm + ".y")

                def pool_f(pool, q):
                    pool.wait_ge(ev(f"{u}.hn"), G * norm(nm) + 1)
                    pool.memset(xpad[:, :, :, 0:3], 0.0).then_inc(ev(f"{u}.zero"), 1)
                    yield 9
                    pool.wait_ge(ev(nm + ".xc"), 2)
                    for c in range(2):
                        q.link(pool.tensor_scalar(ysum[:, c, 0, :], xc[:, c, :], W["s_D"][:, c:c + 1], None, ALU.mult))
                    q.link(pool.memset(ysum[:, :, 1, :], 0.0))
                    for k, (c, n) in enumerate(steps):
                        yield 24 + CHS * (16 * c + n)
                        P.wait_given(pool, f"{nm}.bc2.{c}.{n}")
                        pool.tensor_tensor(ysum[:, c], ysum[:, c], yc[:, k % RING], ALU.add).then_inc(ev(f"{u}.sum"), 1)
                        pool.wait_ge(ev(f"{u}.sum"), base["sum"] + k + 1)

                return pe_f, act_f, dve_f, pool_f, nothing

            def delta(nm):
                S = Scratch(scratch)
                base = share(diff=1, exp=1, zero=1, conv=3, sum=G)
                qk = S.take(2 * N).rearrange("p (k t) -> p k t", k=2)
                kb = S.take(N)
                outs = S.take(G * 4 * D).rearrange("p (s o f) -> p s o f", s=G, o=4)
                mats = S.take(G * DELTA_H * 3 * L).rearrange("p (s h m t) -> p s h m t", s=G, h=DELTA_H, m=3)
                TT_flat, Pm_flat, Nb_flat = (S.take(G * DELTA_H * L) for _ in range(3))
                TT, Pm, Nb = (a.rearrange("p (s h t) -> p s h t", s=G, h=DELTA_H) for a in (TT_flat, Pm_flat, Nb_flat))
                Zf, Rf, Uf = (S.take(G * D) for _ in range(3))
                Z, R, U = (a.rearrange("p (s f) -> p s f", s=G) for a in (Zf, Rf, Uf))
                local, mid, mid_odd = (a.rearrange("p (s t) -> p s t", s=G) for a in (Zf, Rf, Uf))
                vb = Pm_flat[:, 0:N]
                vpad = S.take(G * (L + PAD)).rearrange("p (s t) -> p s t", s=G)
                late = S.at
                S = Scratch(scratch)
                S.at = 3 * N + G * 4 * D
                pads = S.take(3 * G * (L + 3)).rearrange("p (k s t) -> p k s t", k=3, s=G)
                conv = S.take(3 * N).rearrange("p (k s t) -> p k s t", k=3, s=G)
                smooth = S.take(2 * N).rearrange("p (k t) -> p k t", k=2)
                squares = S.take(2 * N).rearrange("p (k t) -> p k t", k=2)
                length = S.take(2 * N).rearrange("p (k t) -> p k t", k=2)
                beta = S.take(N)
                S = Scratch(scratch)
                S.at = 3 * N + G * 4 * D
                cross = S.take(G * 4 * D).rearrange("p (s k h e) -> p s k h e", s=G, k=4, h=DELTA_H)
                cross_sums = S.take(G * 16).rearrange("p (s k h) -> p s k h", s=G, k=4)
                feat = S.take(G * NFEAT).rearrange("p (s k h) -> p s k h", s=G, k=14)
                tmp = S.take(G * 16).rearrange("p (s o h) -> p s o h", s=G, o=4)
                fT = S.take(N)
                h1T = S.take(3 * N).rearrange("p (c t) -> p c t", c=3)
                lg, pr = (S.take(G * 16).rearrange("p (a i) -> p a i", i=4) for _ in range(2))
                t16, ss, rr = (S.take(G * DELTA_H) for _ in range(3))
                pm = S.take(2 * 4 * D).rearrange("p (r i h e) -> p r i h e", r=2, i=4, h=DELTA_H)
                mixed, msq, oT = S.take(N), S.take(N), S.take(N)

                early = [Scratch(scratch) for _ in range(G)]
                for s in range(G):
                    early[s].at = 0 if s == 0 else late + (s - 1) * 6 * D
                prod = [e.take(6 * D).rearrange("p (k h e) -> p k h e", k=6, h=DELTA_H) for e in early]
                last_place = early[-1]
                sums = last_place.take(G * 16).rearrange("p (s o h) -> p s o h", s=G, o=4)
                psums = last_place.take(G * 40).rearrange("p (s k h) -> p s k h", s=G, k=10)

                NT, T, AT = (lambda s, h, m=m: mats[:, s, h, m, :] for m in range(3))
                heads = range(DELTA_H)

                def hs(h):
                    return slice(DELTA_D * h, DELTA_D * h + DELTA_D)

                def pe_f(pe):
                    yield from norm_pe(pe, nm)
                    yield 5
                    P.wait_given(pe, nm + ".hT")
                    for name, w in (("p0", "d_Wq"), ("p1", "d_Wk"), ("p2", "d_Wv"), ("beta", "d_Wb_wide")):
                        t = P.open(pe, f"{nm}.{name}")
                        P.close(pe.matmul(t, W[w][:], hT[:], start=True, stop=True), f"{nm}.{name}")
                    yield 12
                    pe.wait_ge(ev(nm + ".sq"), 2)
                    for k in range(2):
                        t = P.open(pe, f"{nm}.len{k}")
                        P.close(pe.matmul(t, W["same_head"][:], squares[:, k, :], start=True, stop=True), f"{nm}.len{k}")
                    for s in range(G):
                        for h in heads:
                            yield 18 + 1.5 * (s * DELTA_H + h)
                            if s == 0 and h == 0:
                                pe.wait_ge(ev(nm + ".kb"), 2)
                                pe.wait_ge(ev(nm + ".unit"), 2)
                            t = P.open(pe, f"{nm}.M{s}{h}", width=3 * L)
                            kh, qh, kbh = qk[hs(h), 1, col(s)], qk[hs(h), 0, col(s)], kb[hs(h), col(s)]
                            pe.matmul(t[:, 0:L], kh, kbh, start=True, stop=True, skip_group_check=True)
                            pe.matmul(t[:, L:2 * L], kbh, kh, start=True, stop=True, skip_group_check=True)
                            P.close(pe.matmul(t[:, 2 * L:3 * L], kh, qh, start=True, stop=True,
                                              skip_group_check=True), f"{nm}.M{s}{h}")
                    yield 31
                    pe.wait_ge(ev(nm + ".mid"), 1)
                    for s in range(G):
                        t = P.open(pe, f"{nm}.tok{s}", width=4 * L)
                        for o, src in enumerate((local[:, s, :], mid[:, s, :], vb[:, col(s)], vpad[:, s, PAD:])):
                            last = pe.transpose(t[:, o * L:(o + 1) * L], src, ident[:])
                        P.close(last, f"{nm}.tok{s}")

                    def product(name, s, lhs, rhs, width=L):
                        t = P.open(pe, f"{nm}.{name}{s}", width=DELTA_H * width)
                        for h in heads:
                            last = pe.matmul(t[:, h * width:(h + 1) * width], lhs(h), rhs(h), start=True, stop=True,
                                             skip_group_check=True)
                        P.close(last, f"{nm}.{name}{s}")

                    for lv in range(1, 6):
                        yield 34 + LEVEL * (lv - 1)
                        for s in range(G):
                            pe.wait_ge(ev(f"{nm}.Nb"), G * (lv - 1) + s + 1)
                            if lv == 1:
                                pe.wait_ge(ev(nm + ".T"), s + 1)
                                pe.wait_ge(ev(nm + ".TT"), s + 1)
                            else:
                                P.wait_given(pe, f"{nm}.L{lv - 1}t{s}")
                            product(f"L{lv}P", s, lambda h: Nb[:, s, h, :], lambda h: T(s, h))
                        for s in range(G):
                            P.wait_given(pe, f"{nm}.L{lv}P{s}")
                            if lv < 5:
                                product(f"L{lv}T", s, lambda h: TT[:, s, h, :], lambda h: Pm[:, s, h, :])
                            product(f"L{lv}t", s, lambda h: Pm[:, s, h, :], lambda h: TT[:, s, h, :])
                    yield 34 + LEVEL * 5 + 0
                    for s in range(G):
                        P.wait_given(pe, f"{nm}.L5t{s}")
                        product("Z", s, lambda h: TT[:, s, h, :], lambda h: outs[:, s, 2, hs(h)], DELTA_D)
                    for s in range(G):
                        P.wait_given(pe, f"{nm}.Z{s}")
                        pe.wait_ge(ev(f"{nm}.Nb"), G * 5 + s + 1)
                        product("R", s, lambda h: Nb[:, s, h, :], lambda h: Z[:, s, hs(h)], DELTA_D)
                    for s in range(G):
                        P.wait_given(pe, f"{nm}.R{s}")
                        product("U", s, lambda h: TT[:, s, h, :], lambda h: R[:, s, hs(h)], DELTA_D)
                    for s in range(G):
                        P.wait_given(pe, f"{nm}.U{s}")
                        product("D", s, lambda h: AT(s, h), lambda h: U[:, s, hs(h)], DELTA_D)
                    yield 34 + LEVEL * 5 + 8
                    banks_h = [P.open(pe, f"{nm}.h{c}") for c in range(3)]
                    for c, (r0, rows) in enumerate(RCH):
                        pe.matmul(banks_h[c][0:rows, :], W["d_r_w1a"][:, r0:r0 + rows], hT[:], start=True, stop=False)
                    pe.wait_ge(ev(nm + ".feat"), 1)
                    t = P.open(pe, nm + ".fT")
                    for s in range(G):
                        last = pe.transpose(t[0:NFEAT, col(s)], feat[:, s, :, :].rearrange("p k h -> p (k h)"), ident[:])
                    P.close(last, nm + ".fT")
                    P.wait_given(pe, nm + ".fT")
                    for c, (r0, rows) in enumerate(RCH):
                        P.close(pe.matmul(banks_h[c][0:rows, :], W["d_r_w1b"][0:NFEAT, r0:r0 + rows], fT[0:NFEAT, :],
                                          start=False, stop=True), f"{nm}.h{c}")
                    for c in range(3):
                        P.wait_given(pe, f"{nm}.h{c}")
                    yield 34 + LEVEL * 5 + 18
                    t = P.open(pe, nm + ".lg")
                    bias_row(pe, t, W["d_r_b2"][:])
                    for s in range(G):
                        for c, (r0, rows) in enumerate(RCH):
                            last = pe.matmul(t[:, s * 16:(s + 1) * 16], h1T[0:rows, c, col(s)], W["d_r_w2"][0:rows, c, :],
                                             start=False, stop=c == 2, skip_group_check=True)
                    P.close(last, nm + ".lg")
                    yield 34 + LEVEL * 5 + 26
                    pe.wait_ge(ev(nm + ".mixed"), 1)
                    t = P.open(pe, nm + ".oT")
                    for s in range(G):
                        last = pe.transpose(t[:, col(s)], mixed[:, col(s)], ident[:])
                    P.close(last, nm + ".oT")
                    P.wait_given(pe, nm + ".oT")
                    t = P.open(pe, nm + ".y", ACC)
                    for s in range(G):
                        last = pe.matmul(t[:, col(s)], oT[:, col(s)], W["d_Wo"][:], start=True, stop=True,
                                         skip_group_check=True)
                    P.close(last, nm + ".y")

                def act_f(act, q):
                    yield from norm_act(act, nm)
                    yield 5
                    act.wait_ge(ev(f"{u}.zero"), base["zero"] + 1)
                    for k in range(3):
                        t = P.take(act, f"{nm}.p{k}")
                        P.give(act.copy(pads[:, k, :, 3:], row_tiles(t)), f"{nm}.p{k}")
                    t = P.take(act, nm + ".beta")
                    P.give(act.activation(beta, t, ACT.Sigmoid), nm + ".beta")
                    for k in (2, 0, 1):
                        act.wait_ge(ev(f"{u}.conv"), base["conv"] + {2: 1, 0: 2, 1: 3}[k])
                        dst = vpad[:, :, PAD:] if k == 2 else row_tiles(smooth[:, k, :])
                        act.activation(dst, conv[:, k, :, :], ACT.Silu).then_inc(ev(nm + ".silu"), 1)
                    act.wait_ge(ev(nm + ".silu"), 3)
                    for k in range(2):
                        act.activation(squares[:, k, :], smooth[:, k, :], ACT.Square).then_inc(ev(nm + ".sq"), 1)
                    yield 12
                    for k in range(2):
                        t = P.take(act, f"{nm}.len{k}")
                        P.give(act.activation(length[:, k, :], t, ACT.Sqrt, bias=eps12[:]), f"{nm}.len{k}")
                    yield 31
                    for s in range(G):
                        t = P.take(act, f"{nm}.tok{s}")
                        P.give(act.copy(outs[:, s, :, :].rearrange("p o f -> p (o f)"), t), f"{nm}.tok{s}")
                    for lv in range(1, 6):
                        yield 34 + LEVEL * (lv - 1)
                        for s in range(G):
                            t = P.take(act, f"{nm}.L{lv}P{s}")
                            P.give(act.copy(Pm[:, s, :, :].rearrange("p h t -> p (h t)"), t), f"{nm}.L{lv}P{s}")
                    yield 34 + LEVEL * 5 + 0
                    for name, dst in (("Z", Z), ("R", R)):
                        for s in range(G):
                            t = P.take(act, f"{nm}.{name}{s}")
                            P.give(act.copy(dst[:, s, :], t[:, 0:D]), f"{nm}.{name}{s}")
                    for s in range(G):
                        t = P.take(act, f"{nm}.D{s}")
                        P.give(act.copy(outs[:, s, 2, :], t[:, 0:D]), f"{nm}.D{s}")
                    yield 34 + LEVEL * 5 + 8
                    t = P.take(act, nm + ".fT")
                    P.give(act.copy(fT[0:NFEAT, :], t[0:NFEAT, :]), nm + ".fT")
                    for c, (r0, rows) in enumerate(RCH):
                        t = P.take(act, f"{nm}.h{c}")
                        P.give(act.activation(h1T[0:rows, c, :], t[0:rows, :], ACT.Silu, bias=W["d_r_b1"][0:rows, c, :]),
                               f"{nm}.h{c}")
                    yield 34 + LEVEL * 5 + 18
                    act.wait_ge(ev(f"{u}.diff"), base["diff"] + 1)
                    act.activation(pr, lg, ACT.Exp).then_inc(ev(f"{u}.exp"), 1)
                    yield 34 + LEVEL * 5 + 23
                    for k in range(2):
                        act.wait_ge(ev(nm + ".ss"), k + 1)
                        act.activation(rr, ss, ACT.Sqrt, scale=1.0 / DELTA_D, bias=eps5[:]).then_inc(ev(nm + ".rr"), 1)
                    yield 34 + LEVEL * 5 + 26
                    t = P.take(act, nm + ".oT")
                    P.give(act.copy(oT, t), nm + ".oT")

                def dve_f(dve, q):
                    norm_dve(dve, q, nm)
                    yield 5
                    marks = {}

                    def tap(key, dst, src, w, k, done=None):
                        if key in marks:
                            q.wait(marks[key])
                            ins = dve.scalar_tensor_tensor(out=dst, in0=src, scalar=w[:, k:k + 1], in1=dst,
                                                           op0=ALU.mult, op1=ALU.add)
                        else:
                            ins = dve.tensor_scalar(dst, src, w[:, k:k + 1], None, ALU.mult)
                        if done:
                            ins.then_inc(ev(done), 1)
                        else:
                            marks[key] = q.mark(ins)

                    names = ("d_conv_q_w", "d_conv_k_w", "d_conv_v_w")
                    for k in range(3):
                        P.wait_given(dve, f"{nm}.p{k}")
                    for tp in range(CONV_K):
                        for k in (2, 0, 1):
                            tap(k, conv[:, k, :, :], pads[:, k, :, tp:tp + L], W[names[k]], tp,
                                f"{u}.conv" if tp == CONV_K - 1 else None)
                    yield 12
                    dve.wait_ge(ev(nm + ".silu"), 1)
                    def mid_taps(first, last):
                        for n in range(first, last):
                            tap("odd" if n % 2 else "even", mid_odd if n % 2 else mid, vpad[:, :, n:n + L],
                                W["d_mid_w"], n)

                    for n in range(LOCAL_K):
                        o = PAD - LOCAL_K + 1 + n
                        tap("local", local, vpad[:, :, o:o + L], W["d_local_w"], n)
                        mid_taps(n, n + 1)
                    yield 15
                    for k in (1, 0):
                        P.wait_given(dve, f"{nm}.len{k}")
                        q.link(dve.reciprocal(length[:, k, :], length[:, k, :]))
                        dve.tensor_tensor(qk[:, k, :], smooth[:, k, :], length[:, k, :],
                                          ALU.mult).then_inc(ev(nm + ".unit"), 1)
                    done, units = LOCAL_K, G * DELTA_H
                    for s in range(G):
                        for h in heads:
                            n = s * DELTA_H + h
                            yield 18 + 1.5 * n
                            upto = LOCAL_K + (MID_K - LOCAL_K) * (n + 1) // units
                            mid_taps(done, upto)
                            done = upto
                            t = P.take(dve, f"{nm}.M{s}{h}")
                            P.give(dve.tensor_tensor(mats[:, s, h, :, :], t[:, 0:3 * L].rearrange(
                                "p (m t) -> p m t", m=3), W["delta_masks"][:], ALU.mult), f"{nm}.M{s}{h}")
                        P.wait_given(dve, f"{nm}.M{s}{DELTA_H - 1}")
                        dve.tensor_tensor(mats[:, s, :, 1, :], mats[:, s, :, 1, :], spread(ident[:], DELTA_H),
                                          ALU.add).then_inc(ev(nm + ".T"), 1)
                    yield 31
                    q.wait(max(marks.values()))
                    dve.tensor_tensor(mid, mid, mid_odd, ALU.add).then_inc(ev(nm + ".mid"), 1)
                    for lv in range(1, 6):
                        yield 34 + LEVEL * (lv - 1)
                        if lv == 2:
                            for s in range(G):
                                dve.wait_ge(ev(nm + ".prod"), s + 1)
                                q.mark(dve.tensor_reduce(sums[:, s, :, :], outs[:, s, :, :].rearrange(
                                    "p o (h e) -> p o h e", e=DELTA_D), X, ALU.add))
                                for k, slots in ((0, slice(0, 2)), (2, slice(3, 5)), (4, slice(6, 9, 2))):
                                    dve.tensor_reduce(psums[:, s, slots, :], prod[s][:, k:k + 2], X, ALU.add)
                        for s in range(G):
                            if lv < 5:
                                t = P.take(dve, f"{nm}.L{lv}T{s}")
                                P.give(dve.tensor_tensor(mats[:, s, :, 1, :], mats[:, s, :, 1, :], row_tiles(t), ALU.add),
                                       f"{nm}.L{lv}T{s}")
                            t = P.take(dve, f"{nm}.L{lv}t{s}")
                            P.give(dve.tensor_tensor(TT[:, s, :, :], TT[:, s, :, :], row_tiles(t), ALU.add),
                                   f"{nm}.L{lv}t{s}")
                    yield 34 + LEVEL * 5 + 0
                    for s in range(G):
                        P.wait_given(dve, f"{nm}.Z{s}")
                        t = P.take(dve, f"{nm}.U{s}")
                        P.give(dve.tensor_tensor(U[:, s, :], Z[:, s, :], t[:, 0:D], ALU.add), f"{nm}.U{s}")
                    yield 34 + LEVEL * 5 + 8
                    for s in range(G):
                        P.wait_given(dve, f"{nm}.D{s}")
                        o = outs[:, s].rearrange("p o (h e) -> p o h e", h=DELTA_H)
                        ins = dve.tensor_tensor(cross[:, s], o, spread(outs[:, s, 2, :], 4).rearrange(
                            "p k (h e) -> p k h e", h=DELTA_H), ALU.mult)
                    q.mark(ins)
                    dve.tensor_reduce(sums[:, :, 2, :], outs[:, :, 2, :].rearrange("p s (h e) -> p s h e", e=DELTA_D),
                                      X, ALU.add)
                    q.wait(q.count)
                    for s in range(G):
                        ins = dve.tensor_reduce(cross_sums[:, s], cross[:, s], X, ALU.add)
                    q.link(ins)
                    dve.tensor_copy(psums[:, :, 2, :], cross_sums[:, :, 2, :])
                    dve.tensor_copy(psums[:, :, 5:8:2, :], cross_sums[:, :, 0:2, :])
                    q.link(dve.tensor_copy(psums[:, :, 9, :], cross_sums[:, :, 3, :]))
                    mean = feat[:, :, 0:8:2, :]
                    q.link(dve.tensor_scalar(mean, sums, 1.0 / DELTA_D, None, ALU.mult))
                    q.link(dve.tensor_tensor(tmp, mean, sums, ALU.mult))
                    q.link(dve.tensor_tensor(tmp, psums[:, :, 0:4, :], tmp, ALU.subtract))
                    dve.tensor_scalar(feat[:, :, 1:8:2, :], tmp, 1.0 / (DELTA_D - 1), None, ALU.mult)
                    dve.tensor_scalar(feat[:, :, 8:14, :], psums[:, :, 4:10, :], 1.0 / DELTA_D, None,
                                      ALU.mult).then_inc(ev(nm + ".feat"), 1)
                    yield 34 + LEVEL * 5 + 18
                    t = P.take(dve, nm + ".lg")[:, 0:G * 16].rearrange("p (a i) -> p a i", i=4)
                    q.link(dve.tensor_reduce(t16, t, X, ALU.max))
                    P.give(dve.tensor_tensor(lg, t, spread(t16, 4, 2), ALU.subtract), nm + ".lg")
                    P.wait_given(dve, nm + ".lg")
                    dve.tensor_copy(t16, t16).then_inc(ev(f"{u}.diff"), 1)
                    dve.wait_ge(ev(f"{u}.exp"), base["exp"] + 1)
                    q.link(dve.tensor_reduce(t16, pr, X, ALU.add))
                    q.link(dve.reciprocal(t16, t16))
                    q.link(dve.tensor_tensor(pr, pr, spread(t16, 4, 2), ALU.mult))
                    dve.tensor_scalar(pr, pr, 1.0 - 4.0 * 0.01, 0.01, ALU.mult, ALU.add).then_inc(ev(nm + ".probs"), 1)
                    for s in range(G):
                        dve.wait_ge(ev(nm + ".pm"), s + 1)
                        dve.tensor_reduce(mixed[:, col(s)].rearrange("p (h e) -> p h e", h=DELTA_H),
                                          pm[:, s % 2].rearrange("p i h e -> p h e i"), X,
                                          ALU.add).then_inc(ev(f"{u}.sum"), 1)
                    yield 34 + LEVEL * 5 + 23
                    dve.wait_ge(ev(f"{u}.sum"), base["sum"] + G)
                    hv = [a.rearrange("p (a e) -> p a e", e=DELTA_D) for a in (mixed, msq)]
                    for k, w in enumerate(("d_mix_w", "d_onorm_w")):
                        q.link(dve.tensor_tensor(msq, mixed, mixed, ALU.mult))
                        dve.tensor_reduce(ss, hv[1], X, ALU.add).then_inc(ev(nm + ".ss"), 1)
                        dve.wait_ge(ev(nm + ".rr"), k + 1)
                        q.link(dve.reciprocal(t16, rr))
                        q.link(dve.tensor_tensor(hv[0], hv[0], spread(t16, DELTA_D, 2), ALU.mult))
                        ins = dve.tensor_tensor(row_tiles(mixed), row_tiles(mixed), spread(W[w][:], G), ALU.mult)
                        if k == 0:
                            q.link(ins)
                        else:
                            ins.then_inc(ev(nm + ".mixed"), 1)
                    yield 34 + LEVEL * 5 + 26
                    residual_dve(dve, q, nm + ".y")

                def pool_f(pool, q):
                    pool.wait_ge(ev(f"{u}.hn"), G * norm(nm) + 1)
                    pool.memset(pads[:, :, :, 0:3], 0.0)
                    pool.memset(vpad[:, :, 0:PAD], 0.0).then_inc(ev(f"{u}.zero"), 1)
                    yield 5
                    P.wait_given(pool, nm + ".beta")
                    pool.wait_ge(ev(nm + ".silu"), 1)
                    pool.tensor_tensor(row_tiles(vb), vpad[:, :, PAD:], row_tiles(beta), ALU.mult).then_inc(ev(nm + ".kb"), 1)
                    yield 15
                    pool.wait_ge(ev(nm + ".unit"), 1)
                    pool.tensor_tensor(kb, qk[:, 1, :], beta, ALU.mult).then_inc(ev(nm + ".kb"), 1)

                    def level(lv, s):
                        pool.tensor_tensor(Nb[:, s, :, :], mats[:, s, :, 0, :], spread(W["level_T"][:, lv, :], DELTA_H),
                                           ALU.mult).then_inc(ev(f"{nm}.Nb"), 1)

                    for s in range(G):
                        yield 18 + 1.5 * (s * DELTA_H + DELTA_H - 1)
                        for h in heads:
                            P.wait_given(pool, f"{nm}.M{s}{h}")
                        q.link(pool.tensor_tensor(TT[:, s, :, :], mats[:, s, :, 0, :],
                                                  spread(W["level_T"][:, 0, :], DELTA_H), ALU.mult))
                        pool.tensor_tensor(TT[:, s, :, :], TT[:, s, :, :], spread(ident[:], DELTA_H),
                                           ALU.add).then_inc(ev(nm + ".TT"), 1)
                        level(1, s)
                    o4 = outs.rearrange("p s o (h e) -> p s o h e", h=DELTA_H)
                    for lv in range(2, 7):
                        yield 34 + LEVEL * (lv - 2)
                        for s in range(G):
                            P.take(pool, f"{nm}.L{lv - 1}P{s}")
                            level(lv, s)
                        if lv == 2:
                            for s in range(G):
                                P.wait_given(pool, f"{nm}.tok{s}")
                                o, w = o4[:, s], prod[s]
                                pool.tensor_tensor(w[:, 0:2], o[:, 0:2], o[:, 0:2], ALU.mult)
                                pool.tensor_tensor(w[:, 2], o[:, 3], o[:, 3], ALU.mult)
                                pool.tensor_tensor(w[:, 3], o[:, 0], o[:, 1], ALU.mult)
                                for k in range(2):
                                    ins = pool.tensor_tensor(w[:, 4 + k], o[:, k], o[:, 3], ALU.mult)
                                ins.then_inc(ev(nm + ".prod"), 1)
                    yield 34 + LEVEL * 5 + 18
                    pool.wait_ge(ev(nm + ".probs"), 1)
                    pv = pr.rearrange("p (s h) i -> p s h i", s=G)
                    for s in range(G):
                        if s >= 2:
                            pool.wait_ge(ev(f"{u}.sum"), base["sum"] + s - 1)
                        pool.tensor_tensor(pm[:, s % 2], o4[:, s],
                                           spread(pv[:, s].rearrange("p h i -> p i h"), DELTA_D, 3),
                                           ALU.mult).then_inc(ev(nm + ".pm"), 1)

                return pe_f, act_f, dve_f, pool_f, nothing
            sections = {
                "L0_delta": delta(f"{u}d0"),
                "L0_cross": attention16(f"{u}x0", "x0_", src="ctx"),
                "L0_ffn": ffn(f"{u}f0"),
                "L1_attn": attention16(f"{u}a1", "a1_", bias=True, bias_out=True, mask="causal"),
                "L1_mix": mixer(f"{u}m1"),
                "L1_moe": moe1(f"{u}e1"),
                "L2_attn": attention16(f"{u}a2", "a2_", rope=True, mask="causal"),
                "L2_cross": attention16(f"{u}x2", "x2_", src="ctx", bias=True, bias_out=True, mask="given"),
                "L2_moe": moe2(f"{u}e2"),
                "L3_mamba": mamba(f"{u}s3"),
                "L3_cross": cross3(f"{u}x3"),
                "L3_moe": moe3(f"{u}e3"),
            }
            last_sum = {"L0_delta": "d0", "L0_cross": "x0", "L0_ffn": "f0", "L1_attn": "a1", "L1_mix": "m1",
                        "L1_moe": "e1", "L2_attn": "a2", "L2_cross": "x2", "L2_moe": "e2", "L3_mamba": "s3",
                        "L3_cross": "x3", "L3_moe": "e3"}[SECTIONS[-1]]
            x_d, c_d, m_d, o_d, r_d = (a.rearrange("(g u s) t f -> u g t s f", u=STREAMS, s=G)[u]
                                  for a in (dram["x"], dram["ctx"], dram["mask"], out, res_d))
            p_d = dram["key_pad"].rearrange("(g u a s) t -> u g a (s t)", u=STREAMS, a=1, s=G)[u]

            def load(sp, g):
                sp.dma_start(xres[:], x_d[g]).then_inc(s_in, 16)
                sp.dma_start(ctx_tok[:], c_d[g]).then_inc(s_ctx, 16)
                sp.dma_start(mask_i[:], m_d[g]).then_inc(s_ctx, 16)
                sp.dma_start(pad_row_u8[:], p_d[g]).then_inc(s_ctx, 16)

            def store(sp, g):
                if "L3_moe" in SECTIONS:
                    P.wait_given(sp, f"{u}x3.y") if "L3_cross" in SECTIONS else sp.wait_ge(s_in, 16)
                    sp.dma_start(r_d[g], xres[:]).then_inc(s_out, 16)
                    sp.wait_ge(ev(f"{u}e3.placed"), 1)
                    sp.dma_start(place_d.rearrange("(g u) p s -> u g p s", u=STREAMS)[u][g], place[:]
                                 ).then_inc(s_out, 16)
                    sp.wait_ge(s_out, 32)
                    sp.wait_ge(s_scatter, g * (16 * G) + 16 * G)
                else:
                    P.wait_given(sp, f"{u}{last_sum}.y")
                    sp.dma_start(o_d[g], xres[:]).then_inc(s_out, 16)
                    sp.wait_ge(s_out, 16)

            def steps(engine, *args):
                yield 0.0
                if engine == 2:
                    args[0].wait_ge(s_in, 16)
                prepared = False
                for name in SECTIONS:
                    start = PLACE[name]
                    if name != "L0_delta" and not prepared:
                        yield start - 2
                        if engine < 4:
                            args[0].wait_ge(s_late, 16 * len(late_loads))
                        context[engine](*args)
                        prepared = True
                    yield start
                    labels = sections[name][engine](*args)
                    if labels is not None:
                        for part in labels:
                            yield start + part

            context = {0: ctx_pe, 1: ctx_act, 2: ctx_dve, 3: nothing, 4: nothing}
            sems = [s_in, s_out, s_ctx, s_stack, s_stored]
            return load, store, steps, sems

        def clear(sems):
            numbers = sorted(s.num for s in sems)
            first = numbers[0]
            for a, b in zip(numbers, numbers[1:] + [None]):
                if b != a + 1:
                    nc.sync.sem_clear(range(first, a + 1))
                    first = b

        groups = [stream(u) for u in range(STREAMS)]

        def in_turns(engine, *args):
            runs = [g[2](engine, *args) for g in groups]
            place = [next(r) + LAG * u for u, r in enumerate(runs)]
            while any(p is not None for p in place):
                p, u = min((p, u) for u, p in enumerate(place) if p is not None)
                p = next(runs[u], None)
                place[u] = None if p is None else p + LAG * u

        with nc.Fori(0, NGROUPS) as g:
            with nc.Block() as block:
                @block.tensor
                def _(pe):
                    in_turns(0, pe)

                @block.scalar
                def _(act):
                    in_turns(1, act, Order(act, s_act))

                @block.vector
                def _(dve):
                    in_turns(2, dve, Order(dve, s_dve))

                @block.gpsimd
                def _(pool):
                    in_turns(3, pool, Order(pool, s_pool))

                @block.sync
                def _(sp):
                    for load, _, _, _ in groups:
                        load(sp, g)
                    in_turns(4, sp)
                    for _, store, _, _ in groups:
                        store(sp, g)

            clear([s_dve, s_act, s_pool] + [s for g4 in groups for s in g4[3]] + filled + emptied +
                  list(events.values()))
            nc.all_engine_barrier()

        if "L3_moe" not in SECTIONS:
            return

        S = Scratch(scratches[0])
        nch, lots = F3 // 128, range(LOT3)
        rows_in = S.take(LOT3 * CAP).rearrange("p (i c f) -> p i c f", i=LOT3, f=D)
        rows_out = S.take(LOT3 * CAP).rearrange("p (i c f) -> p i c f", i=LOT3, f=D)
        xT = S.take(2 * CAP).rearrange("p (r t) -> p r t", r=2)
        hid = S.take(2 * nch * CAP).rearrange("p (r c t) -> p r c t", r=2, c=nch)
        w1 = experts[:, 0:LOT3 * F3].rearrange("p (i f) -> p i f", i=LOT3)
        w2 = experts[:, LOT3 * F3:2 * LOT3 * F3].rearrange("p (i c f) -> p i c f", i=LOT3, f=D)
        s_lot, s_stored3 = [sem(f"expert{i}_loaded") for i in lots], sem("experts3_stored")
        P = Psum(banks, filled, emptied)
        w1_d = dram["e3_W1"].rearrange("p (r i f) -> r p i f", i=LOT3, f=F3)
        w2_d = dram["e3_W2"].rearrange("(r i c p) f -> r p i c f", i=LOT3, c=nch, p=128)
        in_d, out_d = (a.rearrange("(r i c p) f -> r p i c f", i=LOT3, c=CAP // 128, p=128)
                       for a in (expert_in, expert_out))
        with nc.Fori(0, E3 // LOT3) as r:
            with nc.Block(no_gpsimd_drain=True) as block:
                @block.tensor
                def _(pe):
                    def up(i):
                        pe.wait_ge(s_lot[i], 48)
                        t = P.open(pe, f"xT{i}", width=CAP)
                        for c in range(CAP // 128):
                            last = pe.transpose(t[:, c * 128:(c + 1) * 128], rows_in[:, i, c, :], ident[:])
                        P.close(last, f"xT{i}")
                        P.wait_given(pe, f"xT{i}")
                        for c in range(nch):
                            t = P.open(pe, f"up{i}.{c}", width=CAP)
                            P.close(pe.matmul(t, w1[:, i, c * 128:(c + 1) * 128], xT[:, i % 2, :], start=True,
                                              stop=True), f"up{i}.{c}")

                    def down(i):
                        for c in range(nch):
                            P.wait_given(pe, f"up{i}.{c}")
                        t = P.open(pe, f"down{i}", width=CAP)
                        for k in range(CAP // 128):
                            for c in range(nch):
                                last = pe.matmul(t[:, k * D:(k + 1) * D], hid[:, i % 2, c, k * 128:(k + 1) * 128],
                                                 w2[:, i, c, :], start=c == 0, stop=c == nch - 1,
                                                 skip_group_check=True)
                        P.close(last, f"down{i}")

                    for i in range(LOT3 + 1):
                        if i < LOT3:
                            up(i)
                        if i >= 1:
                            down(i - 1)

                def relu(eng, i, c):
                    if i >= 2 and c < 2:
                        P.take(eng, f"down{i - 2}")
                    t = P.take(eng, f"up{i}.{c}")
                    if c % 2 == 0:
                        ins = eng.activation(hid[:, i % 2, c, :], t, ACT.Relu)
                    else:
                        ins = eng.tensor_scalar(hid[:, i % 2, c, :], t, 0.0, None, ALU.max)
                    P.give(ins, f"up{i}.{c}")

                @block.scalar
                def _(act):
                    for i in lots:
                        t = P.take(act, f"xT{i}")
                        P.give(act.copy(xT[:, i % 2, :], t), f"xT{i}")
                        for c in range(0, nch, 2):
                            relu(act, i, c)

                @block.vector
                def _(dve):
                    for i in range(LOT3 + 1):
                        if i < LOT3:
                            for c in range(1, nch, 2):
                                relu(dve, i, c)
                        if i >= 1:
                            t = P.take(dve, f"down{i - 1}")
                            P.give(dve.tensor_copy(rows_out[:, i - 1].rearrange("p c f -> p (c f)"), t),
                                   f"down{i - 1}")

                @block.sync
                def _(sp):
                    for i in lots:
                        sp.dma_start(rows_in[:, i], in_d[r][:, i]).then_inc(s_lot[i], 16)
                        sp.dma_start(w1[:, i], w1_d[r][:, i]).then_inc(s_lot[i], 16)
                        sp.dma_start(w2[:, i], w2_d[r][:, i]).then_inc(s_lot[i], 16)
                    for i in lots:
                        P.wait_given(sp, f"down{i}")
                        sp.dma_start(out_d[r][:, i], rows_out[:, i]).then_inc(s_stored3, 16)
                    sp.wait_ge(s_stored3, 16 * LOT3)

            clear(s_lot + [s_stored3] + filled + emptied)
            nc.all_engine_barrier()

        S = Scratch(scratches[1])
        pieces = 4
        stream_in, taken = (S.take(LOTC * D).rearrange("p (b f) -> p b f", f=D) for _ in range(2))
        places = sb("places_all", [128, LOTC // G, G], U32)
        s_places, s_stream, s_clear, s_added, s_final = (sem(n) for n in (
            "places_loaded", "residual_loaded", "rows_zeroed", "rows_added", "result_stored"))
        s_taken = [sem(f"rows_taken{k}") for k in range(pieces)]
        per = LOTC // pieces
        with nc.Fori(0, NGROUPS * STREAMS * G // LOTC) as r:
            with nc.Block() as block:
                @block.sync
                def _(sp):
                    sp.dma_start(places[:], place_d.rearrange("(r a) p s -> r p a s", a=LOTC // G)[r]
                                 ).then_inc(s_places, 16)
                    for k in range(pieces):
                        b = slice(k * per, (k + 1) * per)
                        sp.dma_start(stream_in[:, b], res_d.rearrange("(r b) t f -> r t b f", b=LOTC)[r][:, b]
                                     ).then_inc(s_stream, 16)
                    for k in range(pieces):
                        sp.wait_ge(s_added, k + 1)
                        b = slice(k * per, (k + 1) * per)
                        sp.dma_start(out.rearrange("(r b) t f -> r t b f", b=LOTC)[r][:, b], stream_in[:, b]
                                     ).then_inc(s_final, 16)
                    sp.wait_ge(s_final, 16 * pieces)

                @block.gpsimd
                def _(pool):
                    pool.wait_ge(s_clear, 1)
                    pool.wait_ge(s_places, 16)
                    for b in range(LOTC):
                        pool.indirect_dma_start(
                            taken[:, b, :], None, expert_out,
                            bass.IndirectOffsetOnAxis(places[:, b // G, b % G:b % G + 1], 0),
                            bounds_check=E3 * CAP - 1, oob_is_err=False).then_inc(s_taken[b // per], 16)

                @block.vector
                def _(dve):
                    dve.memset(taken, 0.0).then_inc(s_clear, 1)
                    dve.wait_ge(s_stream, 16 * pieces)
                    for k in range(pieces):
                        dve.wait_ge(s_taken[k], r * (16 * per) + 16 * per)
                        b = slice(k * per, (k + 1) * per)
                        dve.tensor_tensor(stream_in[:, b], stream_in[:, b], taken[:, b], ALU.add).then_inc(s_added, 1)

            clear([s_places, s_stream, s_clear, s_added, s_final])
            nc.all_engine_barrier()


def kernel(**inputs):
    import concourse.bacc as bacc
    from concourse.bass_utils import run_bass_kernel_spmd

    arrays = host_layout({k: np.asarray(v) for k, v in inputs.items()})
    arrays.update(host_constants())
    nc = bacc.Bacc("TRN2", target_bir_lowering=False, num_devices=1)
    dram = {n: nc.dram_tensor("in_" + n, a.shape, mybir.dt.from_np(a.dtype), kind="ExternalInput").ap()
            for n, a in arrays.items()}
    out = nc.dram_tensor("out", (B, L, D), F32, kind="ExternalOutput").ap()
    build(nc, dram, out)
    r = run_bass_kernel_spmd(nc, [{"in_" + n: a for n, a in arrays.items()}], core_ids=[0])
    return r.results[0]["out"]
```
